# Optimizing a Trainium2 kernel written in Bass

```python
import numpy as np
import jax
import jax.numpy as jnp

def _softmax(x, axis=-1):
    return jax.nn.softmax(x, axis=axis)

def _gelu(x):
    return jax.nn.gelu(x, approximate=True)

def _silu(x):
    return jax.nn.silu(x)

def _sigmoid(x):
    return jax.nn.sigmoid(x)

def _layernorm(x, axis=-1, eps=1e-05):
    m = jnp.mean(x, axis=axis, keepdims=True)
    v = jnp.var(x, axis=axis, keepdims=True)
    return (x - m) / jnp.sqrt(v + eps)

def _scatter_add(tgt, idx, src, axis=0):
    return tgt.at[idx].add(src)

def _segment_sum(src, seg, n):
    return jax.ops.segment_sum(src, seg, n)
kernel_name = 'mk_decoder_preln_d4_seqx_r8_669df8'

def setup_inputs(seed: int=0):
    np.random.seed(seed)
    _w = jnp.asarray

    def _rec_inputs():
        import jax
        import jax.numpy as jnp
        _rk = jax.random.key(seed)
        x = 7.22e-05 + 1 * jax.random.normal(jax.random.fold_in(_rk, 1), (8, 128, 256), jnp.float32)
        _lenS = 128 - jax.random.randint(jax.random.fold_in(_rk, 7), (8,), 0, max(1, 128 // 4) + 1, jnp.int32)
        _lenS2 = 128 - jax.random.randint(jax.random.fold_in(_rk, 8), (8,), 0, max(1, 128 // 4) + 1, jnp.int32)
        _ctx_1024P = jax.random.normal(jax.random.fold_in(_rk, 11), (8, 16, 128), jnp.float32)
        _ctx_1024c = jax.random.dirichlet(jax.random.fold_in(_rk, 511), 0.3 * jnp.ones((16,), jnp.float32), (8, 128))
        _ctx_1024t = jnp.einsum('bsk,bkd->bsd', _ctx_1024c, _ctx_1024P)
        _ctx_1024t = _ctx_1024t * jax.lax.rsqrt(jnp.mean(jnp.square(_ctx_1024t)) + 1e-12) * 0.953939
        ctx_1024 = -1.39393e-06 + 0.999914 * (_ctx_1024t + 0.3 * jax.random.normal(jax.random.fold_in(_rk, 611), (8, 128, 128), jnp.float32))
        fside_BxSx2_0 = jax.random.uniform(jax.random.fold_in(_rk, 12), (8, 128, 2), jnp.float32, 0.0, 0.999707)
        _validS = jnp.arange(128)[None, :] < _lenS[:, None]
        _validS2 = jnp.arange(128)[None, :] < _lenS2[:, None]
        _causal = jnp.tril(jnp.ones((128, 128), dtype=bool))
        mask_BxS2_bf1 = jnp.ones((8, 128), dtype=bool)
        return (x, ctx_1024, fside_BxSx2_0, mask_BxS2_bf1)
    x, ctx_1024, fside_BxSx2_0, mask_BxS2_bf1 = _rec_inputs()

    def _L0_attn_setup():
        import jax, jax.numpy as jnp
        import numpy as np
        B, T, C = (2, 256, 256)
        N_HEAD = 16
        HEAD_DIM = C // N_HEAD
        key = jax.random.key(seed)
        ks = jax.random.split(key, 5)
        s = 1.0 / np.sqrt(C)
        return {'x': jax.random.normal(ks[0], (B, T, C), dtype=jnp.float32), 'Wq': jax.random.normal(ks[1], (C, C), dtype=jnp.float32) * s, 'bq': jnp.zeros((C,), dtype=jnp.float32), 'Wk': jax.random.normal(ks[2], (C, C), dtype=jnp.float32) * s, 'bk': jnp.zeros((C,), dtype=jnp.float32), 'Wv': jax.random.normal(ks[3], (C, C), dtype=jnp.float32) * s, 'bv': jnp.zeros((C,), dtype=jnp.float32), 'Wp': jax.random.normal(ks[4], (C, C), dtype=jnp.float32) * s, 'bp': jnp.zeros((C,), dtype=jnp.float32)}
    _L0_attn_all = _L0_attn_setup()
    _L0_attn_in = {k: v for k, v in _L0_attn_all.items() if k in ('Wq', 'bq', 'Wk', 'bk', 'Wv', 'bv', 'Wp', 'bp')}
    del _L0_attn_all

    def _L0_xattn_setup():
        import jax, jax.numpy as jnp
        import numpy as np
        DIM = 256
        CTX_DIM = 128
        N_HEADS = 32
        HEAD_DIM = DIM // N_HEADS
        POS_DIM = 2
        B, N, CTXN = (2, 256, 256)
        ROPE_BASE = 10000.0

        def apply_axial_rope(x, pos):
            b, n, h, d = x.shape
            p = pos.shape[-1]
            dpa = d // p
            half = dpa // 2
            freqs = ROPE_BASE ** (-jnp.arange(half, dtype=x.dtype) / half)
            ang = pos[..., :, None] * freqs
            cos = jnp.cos(ang)[:, :, None, :, :]
            sin = jnp.sin(ang)[:, :, None, :, :]
            xr = x.reshape(b, n, h, p, half, 2)
            x1, x2 = (xr[..., 0], xr[..., 1])
            out = jnp.stack([x1 * cos - x2 * sin, x1 * sin + x2 * cos], axis=-1)
            return out.reshape(b, n, h, d)
        key = jax.random.key(seed)
        ks = jax.random.split(key, 8)
        x = jax.random.normal(ks[0], (B, N, DIM), jnp.float32)
        ctx = jax.random.normal(ks[1], (B, CTXN, CTX_DIM), jnp.float32)
        pos_map = jax.random.uniform(ks[2], (B, N, POS_DIM), jnp.float32)
        ctx_pos_map = jax.random.uniform(ks[3], (B, CTXN, POS_DIM), jnp.float32)
        Wq = jax.random.normal(ks[4], (DIM, DIM), jnp.float32) / np.sqrt(DIM)
        Wkv = jax.random.normal(ks[5], (CTX_DIM, 2 * DIM), jnp.float32) / np.sqrt(CTX_DIM)
        Wout = jax.random.normal(ks[6], (DIM, DIM), jnp.float32) / np.sqrt(DIM)
        bout = jnp.zeros((DIM,), jnp.float32)
        return {'x': x, 'ctx': ctx, 'pos_map': pos_map, 'ctx_pos_map': ctx_pos_map, 'Wq': Wq, 'Wkv': Wkv, 'Wout': Wout, 'bout': bout}
    _L0_xattn_all = _L0_xattn_setup()
    _L0_xattn_in = {k: v for k, v in _L0_xattn_all.items() if k in ('Wq', 'Wkv', 'Wout', 'bout')}
    del _L0_xattn_all

    def _L0_ffn_setup():
        import jax, jax.numpy as jnp
        import numpy as np
        D_MODEL = 256
        HIDDEN = 4 * D_MODEL
        B, S = (2, 512)

        def bit_linear(x, w, b):
            gamma_x = jnp.clip(jnp.max(jnp.abs(x), axis=-1, keepdims=True), 1e-05, None)
            scale_x = 127.0 / gamma_x
            x_dq = jnp.clip(jnp.round(x * scale_x), -128.0, 127.0) / scale_x
            x_ste = x + jax.lax.stop_gradient(x_dq - x)
            gamma_w = jnp.clip(jnp.mean(jnp.abs(w)), 1e-05, None)
            w_dq = jnp.clip(jnp.round(w / gamma_w), -1.0, 1.0) * gamma_w
            w_ste = w + jax.lax.stop_gradient(w_dq - w)
            return jnp.einsum('bsd,hd->bsh', x_ste, w_ste) + b
        key = jax.random.key(seed)
        ks = jax.random.split(key, 7)
        std = 0.02
        return {'x': jax.random.normal(ks[0], (B, S, D_MODEL), dtype=jnp.float32), 'gate_w': jax.random.normal(ks[1], (HIDDEN, D_MODEL), dtype=jnp.float32) * std, 'gate_b': jnp.zeros((HIDDEN,), dtype=jnp.float32), 'val_w': jax.random.normal(ks[2], (HIDDEN, D_MODEL), dtype=jnp.float32) * std, 'val_b': jnp.zeros((HIDDEN,), dtype=jnp.float32), 'out_w': jax.random.normal(ks[3], (D_MODEL, HIDDEN), dtype=jnp.float32) * std, 'out_b': jnp.zeros((D_MODEL,), dtype=jnp.float32)}
    _L0_ffn_all = _L0_ffn_setup()
    _L0_ffn_in = {k: v for k, v in _L0_ffn_all.items() if k in ('gate_w', 'gate_b', 'val_w', 'val_b', 'out_w', 'out_b')}
    del _L0_ffn_all

    def _L1_attn_setup():
        import jax, jax.numpy as jnp
        import numpy as np
        NUM_HEADS = 16

        def _l2_normalize_complex(z):
            n = jnp.sqrt(jnp.sum(jnp.abs(z) ** 2, axis=-1, keepdims=True))
            return z / n
        key = jax.random.key(seed)
        k1, k2, k3, k4 = jax.random.split(key, 4)
        B, S, D = (4, 512, 256)
        scale = 1.0 / np.sqrt(D)
        return {'x': jax.random.normal(k1, (B, S, D), dtype=jnp.float32), 'W_q': jax.random.normal(k2, (D, D), dtype=jnp.float32) * scale, 'W_kv': jax.random.normal(k3, (D, D), dtype=jnp.float32) * scale, 'W_o': jax.random.normal(k4, (D, D), dtype=jnp.float32) * scale}
    _L1_attn_all = _L1_attn_setup()
    _L1_attn_in = {k: v for k, v in _L1_attn_all.items() if k in ('W_q', 'W_kv', 'W_o')}
    del _L1_attn_all

    def _L1_xattn_setup():
        import jax, jax.numpy as jnp
        import numpy as np
        EPS = 1e-05

        def rmsnorm(x, g, eps=EPS):
            var = jnp.mean(jnp.square(x), axis=-1, keepdims=True)
            return x * jax.lax.rsqrt(var + eps) * g
        key = jax.random.key(seed)
        ks = jax.random.split(key, 8)
        B, Sq, Skv = (2, 512, 64)
        dim, cdim, H, D = (256, 128, 16, 128)
        inner = H * D
        s = lambda f: 1.0 / np.sqrt(f)
        return {'hidden_states': jax.random.normal(ks[0], (B, Sq, dim), jnp.float32), 'encoder_hidden_states': jax.random.normal(ks[1], (B, Skv, cdim), jnp.float32), 'Wq': jax.random.normal(ks[2], (dim, inner), jnp.float32) * s(dim), 'Wk': jax.random.normal(ks[3], (cdim, inner), jnp.float32) * s(cdim), 'Wv': jax.random.normal(ks[4], (cdim, inner), jnp.float32) * s(cdim), 'Wo': jax.random.normal(ks[5], (inner, dim), jnp.float32) * s(inner), 'gq': jnp.ones((D,), jnp.float32), 'gk': jnp.ones((D,), jnp.float32)}
    _L1_xattn_all = _L1_xattn_setup()
    _L1_xattn_in = {k: v for k, v in _L1_xattn_all.items() if k in ('Wq', 'Wk', 'Wv', 'Wo', 'gq', 'gk')}
    del _L1_xattn_all

    def _L1_ffn_setup():
        import jax, jax.numpy as jnp
        import numpy as np
        E, TOPK, H, I = (8, 2, 256, 512)
        SOFTCAP = 30.0
        key = jax.random.key(seed)
        ks = jax.random.split(key, 5)
        s = 1.0 / np.sqrt(H)
        si = 1.0 / np.sqrt(I)
        return {'hidden_states': jax.random.normal(ks[0], (4, 256, H), jnp.float32), 'w_gate': jax.random.normal(ks[1], (H, E), jnp.float32) * s, 'w1': jax.random.normal(ks[2], (E, H, I), jnp.float32) * s, 'w3': jax.random.normal(ks[3], (E, H, I), jnp.float32) * s, 'w2': jax.random.normal(ks[4], (E, I, H), jnp.float32) * si}
    _L1_ffn_all = _L1_ffn_setup()
    _L1_ffn_in = {k: v for k, v in _L1_ffn_all.items() if k in ('w_gate', 'w1', 'w3', 'w2')}
    del _L1_ffn_all

    def _L2_attn_setup():
        import jax, jax.numpy as jnp
        import numpy as np
        H = 16
        EPS_DEN = 1e-06

        def _decay_scan(x, decay, init):
            xT = jnp.moveaxis(x, 2, 0)

            def step(s, xt):
                s = decay * s + xt
                return (s, s)
            _, ys = jax.lax.scan(step, init, xT)
            return jnp.moveaxis(ys, 0, 2)

        def _phi(z):
            return jax.nn.elu(z) + 1.0

        def _reference_tuple_inner(x, w_qkv, w_out, decay_param):
            B, T, Hid = x.shape
            D = Hid // H
            qkv = x @ w_qkv
            q, k, v = jnp.split(qkv, 3, axis=-1)

            def to_bhtd(t):
                return t.reshape(B, T, H, D).transpose(0, 2, 1, 3)
            q = _phi(to_bhtd(q))
            k = _phi(to_bhtd(k))
            v = to_bhtd(v)
            decay = jax.nn.sigmoid(decay_param).reshape(1, H, 1)
            init = jnp.zeros((B, H, D), dtype=x.dtype)
            running_kv = _decay_scan(k * v, decay, init)
            running_ksum = _decay_scan(k, decay, init)
            den = jnp.clip(jnp.sum(q * running_ksum, axis=-1, keepdims=True), EPS_DEN, None)
            out = q * running_kv / den
            out = out.transpose(0, 2, 1, 3).reshape(B, T, Hid) @ w_out
            new_kv = running_kv[:, :, -1, :]
            new_ksum = running_ksum[:, :, -1, :]
            return (out, new_kv, new_ksum)
        key = jax.random.key(seed)
        k1, k2, k3 = jax.random.split(key, 3)
        x = jax.random.normal(k1, (2, 512, 256), dtype=jnp.float32)
        w_qkv = jax.random.normal(k2, (256, 768), dtype=jnp.float32) * 0.02
        w_out = jax.random.normal(k3, (256, 256), dtype=jnp.float32) * 0.02
        decay_param = jnp.full((H,), 0.95, dtype=jnp.float32)
        return {'x': x, 'w_qkv': w_qkv, 'w_out': w_out, 'decay_param': decay_param}
    _L2_attn_all = _L2_attn_setup()
    _L2_attn_in = {k: v for k, v in _L2_attn_all.items() if k in ('w_qkv', 'w_out', 'decay_param')}
    del _L2_attn_all

    def _L2_xattn_setup():
        import jax, jax.numpy as jnp
        import numpy as np
        B, S1, S2, DCA = (2, 256, 128, 16)
        QDIM, KDIM, H = (256, 128, 16)
        HD = QDIM // H
        SCALE = HD ** (-0.5)
        EPS = 1e-06
        DCA_WEIGHT = 1.0

        def _ln(t, w, b):
            m = jnp.mean(t, axis=-1, keepdims=True)
            v = jnp.var(t, axis=-1, keepdims=True)
            return (t - m) * jax.lax.rsqrt(v + EPS) * w + b

        def _attn(q, k, v):
            s = jnp.einsum('bhqd,bhkd->bhqk', q, k) * SCALE
            p = jax.nn.softmax(s, axis=-1)
            return jnp.einsum('bhqk,bhkd->bhqd', p, v)
        key = jax.random.key(seed)
        ks = jax.random.split(key, 8)
        w = lambda k, shape: jax.random.normal(k, shape, jnp.float32) * 0.02
        return {'x': jax.random.normal(ks[0], (B, S1, QDIM), jnp.float32), 'y': jax.random.normal(ks[1], (B, S2 + DCA, KDIM), jnp.float32), 'Wq': w(ks[2], (QDIM, QDIM)), 'bq': jnp.zeros((QDIM,), jnp.float32), 'Wk': w(ks[3], (KDIM, QDIM)), 'bk': jnp.zeros((QDIM,), jnp.float32), 'Wv': w(ks[4], (KDIM, QDIM)), 'bv': jnp.zeros((QDIM,), jnp.float32), 'Wkv_dca': w(ks[5], (KDIM, 2 * QDIM)), 'bkv_dca': jnp.zeros((2 * QDIM,), jnp.float32), 'qn_w': jnp.ones((HD,), jnp.float32), 'qn_b': jnp.zeros((HD,), jnp.float32), 'kn_w': jnp.ones((HD,), jnp.float32), 'kn_b': jnp.zeros((HD,), jnp.float32), 'kn_dca_w': jnp.ones((HD,), jnp.float32), 'kn_dca_b': jnp.zeros((HD,), jnp.float32), 'Wo': w(ks[6], (QDIM, QDIM)), 'bo': jnp.zeros((QDIM,), jnp.float32)}
    _L2_xattn_all = _L2_xattn_setup()
    _L2_xattn_in = {k: v for k, v in _L2_xattn_all.items() if k in ('Wq', 'bq', 'Wk', 'bk', 'Wv', 'bv', 'Wkv_dca', 'bkv_dca', 'qn_w', 'qn_b', 'kn_w', 'kn_b', 'kn_dca_w', 'kn_dca_b', 'Wo', 'bo')}
    del _L2_xattn_all

    def _L2_ffn_setup():
        import jax, jax.numpy as jnp
        import numpy as np
        B, S, D, E, R, TOP_K = (4, 512, 256, 6, 16, 2)
        key = jax.random.key(seed)
        ks = jax.random.split(key, 9)
        scale = 0.02
        return {'x': jax.random.normal(ks[0], (B, S, D), dtype=jnp.float32), 'W_base': jax.random.normal(ks[1], (D, D), dtype=jnp.float32) * scale, 'b_base': jax.random.normal(ks[2], (D,), dtype=jnp.float32) * scale, 'A_s': jax.random.normal(ks[3], (D, R), dtype=jnp.float32) * scale, 'B_s': jax.random.normal(ks[4], (R, D), dtype=jnp.float32) * scale, 'A_r': jax.random.normal(ks[5], (E, D, R), dtype=jnp.float32) * scale, 'B_r': jax.random.normal(ks[6], (E, R, D), dtype=jnp.float32) * scale, 'W_router': jax.random.normal(ks[7], (D, E), dtype=jnp.float32) * scale, 'b_router': jax.random.normal(ks[8], (E,), dtype=jnp.float32) * scale}
    _L2_ffn_all = _L2_ffn_setup()
    _L2_ffn_in = {k: v for k, v in _L2_ffn_all.items() if k in ('W_base', 'b_base', 'A_s', 'B_s', 'A_r', 'B_r', 'W_router', 'b_router')}
    del _L2_ffn_all

    def _L3_attn_setup():
        import jax, jax.numpy as jnp
        import numpy as np
        D_MODEL = 256
        D_STATE = 128
        D_CONV = 4
        NHEADS = 64
        NGROUPS = 1
        HEAD_DIM = 64
        CHUNK = 128
        EPS = 1e-05
        D_INNER = NHEADS * HEAD_DIM
        CONV_DIM = D_INNER + 2 * NGROUPS * D_STATE
        D_IN_PROJ = 2 * D_INNER + 2 * NGROUPS * D_STATE + NHEADS

        def _silu(x):
            return x * jax.nn.sigmoid(x)

        def _causal_conv1d(x, w, b):
            K = w.shape[1]
            S = x.shape[1]
            xp = jnp.pad(x, ((0, 0), (K - 1, 0), (0, 0)))
            y = sum((xp[:, k:k + S, :] * w[None, None, :, k].swapaxes(-1, -1) for k in range(0)))
            y = jnp.zeros_like(x)
            for k in range(K):
                y = y + xp[:, k:k + S, :] * w[:, k][None, None, :]
            return _silu(y + b)

        def _ssd(x, dt, A, Bm, Cm, chunk):
            b, s, h, p = x.shape
            g, n = (Bm.shape[2], Bm.shape[3])
            hh = h // g
            c = s // chunk
            x = x.reshape(b, c, chunk, g, hh, p)
            dt = dt.reshape(b, c, chunk, g, hh)
            Bm = Bm.reshape(b, c, chunk, g, n)
            Cm = Cm.reshape(b, c, chunk, g, n)
            dA = dt * A.reshape(g, hh)
            dA_cs = jnp.cumsum(dA, axis=2)
            dtx = dt[..., None] * x
            diff = dA_cs[:, :, :, None] - dA_cs[:, :, None, :]
            mask = jnp.tril(jnp.ones((chunk, chunk), bool))
            L = jnp.exp(jnp.where(mask[None, None, :, :, None, None], diff, -jnp.inf))
            Y = jnp.einsum('bcign,bcjgn,bcijgh,bcjghp->bcighp', Cm, Bm, L, dtx)
            decay = jnp.exp(dA_cs[:, :, -1:] - dA_cs)
            states = jnp.einsum('bcjgn,bcjgh,bcjghp->bcghpn', Bm, decay, dtx)
            chunk_decay = jnp.exp(dA_cs[:, :, -1])

            def step(prev, inp):
                cd, st = inp
                return (cd[..., None, None] * prev + st, prev)
            init = jnp.zeros_like(states[:, 0])
            _, prevs = jax.lax.scan(step, init, (jnp.moveaxis(chunk_decay, 1, 0), jnp.moveaxis(states, 1, 0)))
            prevs = jnp.moveaxis(prevs, 0, 1)
            Y = Y + jnp.einsum('bcign,bcghpn,bcigh->bcighp', Cm, prevs, jnp.exp(dA_cs))
            return Y.reshape(b, s, h, p)
        key = jax.random.key(seed)
        ks = jax.random.split(key, 9)
        B, S = (2, 512)
        return dict(hidden_states=jax.random.normal(ks[0], (B, S, D_MODEL), jnp.float32), W_in=jax.random.normal(ks[1], (D_MODEL, D_IN_PROJ), jnp.float32) * 0.02, conv_w=jax.random.normal(ks[2], (CONV_DIM, D_CONV), jnp.float32) * 0.2, conv_b=jax.random.normal(ks[3], (CONV_DIM,), jnp.float32) * 0.1, A=-jnp.exp(jax.random.uniform(ks[4], (NHEADS,), jnp.float32, 0.0, 2.0)), D=jax.random.normal(ks[5], (NHEADS,), jnp.float32), dt_bias=jax.random.normal(ks[6], (NHEADS,), jnp.float32), norm_w=jnp.ones((D_INNER,), jnp.float32), W_out=jax.random.normal(ks[7], (D_INNER, D_MODEL), jnp.float32) * 0.02)
    _L3_attn_all = _L3_attn_setup()
    _L3_attn_in = {k: v for k, v in _L3_attn_all.items() if k in ('W_in', 'conv_w', 'conv_b', 'A', 'D', 'dt_bias', 'norm_w', 'W_out')}
    del _L3_attn_all

    def _L3_xattn_setup():
        import jax, jax.numpy as jnp
        import numpy as np
        N_HEADS = 16
        N_KV_HEADS = 8
        HEAD_DIM = 128
        D_TEXT = 256
        D_VISION = 128
        GROUPS = N_HEADS // N_KV_HEADS
        key = jax.random.key(seed)
        ks = jax.random.split(key, 6)
        B, T_text, T_vis = (4, 256, 72)
        text_hidden = jax.random.normal(ks[0], (B, T_text, D_TEXT), dtype=jnp.float32)
        vision_tokens = jax.random.normal(ks[1], (B, T_vis, D_VISION), dtype=jnp.float32)
        vision_mask = jnp.ones((B, T_vis), dtype=bool)
        s = 0.02
        Wq = jax.random.normal(ks[2], (D_TEXT, N_HEADS * HEAD_DIM), dtype=jnp.float32) * s
        Wk = jax.random.normal(ks[3], (D_VISION, N_KV_HEADS * HEAD_DIM), dtype=jnp.float32) * s
        Wv = jax.random.normal(ks[4], (D_VISION, N_KV_HEADS * HEAD_DIM), dtype=jnp.float32) * s
        Wo = jax.random.normal(ks[5], (N_HEADS * HEAD_DIM, D_TEXT), dtype=jnp.float32) * s
        return {'text_hidden': text_hidden, 'vision_tokens': vision_tokens, 'vision_mask': vision_mask, 'Wq': Wq, 'Wk': Wk, 'Wv': Wv, 'Wo': Wo}
    _L3_xattn_all = _L3_xattn_setup()
    _L3_xattn_in = {k: v for k, v in _L3_xattn_all.items() if k in ('Wq', 'Wk', 'Wv', 'Wo')}
    del _L3_xattn_all

    def _L3_ffn_setup():
        import jax, jax.numpy as jnp
        import numpy as np
        COST_LAMBDA = 1e-07
        HID = [128, 256, 384, 512, 128, 256, 384, 512]
        TOP_K = 2

        def _gelu(v):
            return jax.nn.gelu(v, approximate=False)

        def _forward(x, down_w, down_b, up_w, up_b, router_w, router_b, shared_w1, shared_b1, shared_w2, shared_b2, core_w, core_b, expert_params):
            E = len(expert_params)
            h = x @ down_w + down_b
            cost = jnp.array([w1.shape[0] * w1.shape[1] + w2.shape[0] * w2.shape[1] for w1, _, w2, _ in expert_params], jnp.float32)
            logits = x @ router_w + router_b - COST_LAMBDA * cost
            probs = jax.nn.softmax(logits, axis=-1)
            topv, topi = jax.lax.top_k(probs, TOP_K)
            gate = jax.nn.softmax(topv, axis=-1)
            out = jnp.zeros_like(h)
            for k in range(TOP_K):
                mask = jax.nn.one_hot(topi[..., k], E, dtype=h.dtype)
                acc = jnp.zeros_like(h)
                for e, (w1, b1, w2, b2) in enumerate(expert_params):
                    hm = h * mask[..., e:e + 1]
                    acc = acc + (_gelu(_gelu(hm) @ w1 + b1) @ w2 + b2)
                out = out + acc * gate[..., k:k + 1]
            out = out + 0.1 * (_gelu(_gelu(h) @ shared_w1 + shared_b1) @ shared_w2 + shared_b2)
            out = out @ up_w + up_b
            out = out + (_gelu(x) @ core_w + core_b)
            return out
        key = jax.random.key(seed)
        ks = iter(jax.random.split(key, 80))

        def W(shape):
            return jax.random.normal(next(ks), shape, jnp.float32) * 0.02
        B, T, D, L = (4, 256, 256, 128)
        inp = {'x': jax.random.normal(next(ks), (B, T, D), jnp.float32)}
        inp['down_w'] = W((D, L))
        inp['down_b'] = jnp.zeros((L,), jnp.float32)
        inp['up_w'] = W((L, D))
        inp['up_b'] = jnp.zeros((D,), jnp.float32)
        inp['router_w'] = W((D, len(HID)))
        inp['router_b'] = jnp.zeros((len(HID),), jnp.float32)
        inp['shared_w1'] = W((L, L))
        inp['shared_b1'] = jnp.zeros((L,), jnp.float32)
        inp['shared_w2'] = W((L, L))
        inp['shared_b2'] = jnp.zeros((L,), jnp.float32)
        inp['core_w'] = W((D, D))
        inp['core_b'] = jnp.zeros((D,), jnp.float32)
        for e, h in enumerate(HID):
            inp[f'e{e}_w1'] = W((L, h))
            inp[f'e{e}_b1'] = jnp.zeros((h,), jnp.float32)
            inp[f'e{e}_w2'] = W((h, L))
            inp[f'e{e}_b2'] = jnp.zeros((L,), jnp.float32)
        return inp
    _L3_ffn_all = _L3_ffn_setup()
    _L3_ffn_in = {k: v for k, v in _L3_ffn_all.items() if k in ('down_w', 'down_b', 'up_w', 'up_b', 'router_w', 'router_b', 'shared_w1', 'shared_b1', 'shared_w2', 'shared_b2', 'core_w', 'core_b', 'e0_w1', 'e0_b1', 'e0_w2', 'e0_b2', 'e1_w1', 'e1_b1', 'e1_w2', 'e1_b2', 'e2_w1', 'e2_b1', 'e2_w2', 'e2_b2', 'e3_w1', 'e3_b1', 'e3_w2', 'e3_b2', 'e4_w1', 'e4_b1', 'e4_w2', 'e4_b2', 'e5_w1', 'e5_b1', 'e5_w2', 'e5_b2', 'e6_w1', 'e6_b1', 'e6_w2', 'e6_b2', 'e7_w1', 'e7_b1', 'e7_w2', 'e7_b2')}
    del _L3_ffn_all
    return {'x': x, 'ctx_1024': ctx_1024, 'fside_BxSx2_0': fside_BxSx2_0, 'mask_BxS2_bf1': mask_BxS2_bf1, 'L0_attn_Wq': _L0_attn_in['Wq'], 'L0_attn_bq': _L0_attn_in['bq'], 'L0_attn_Wk': _L0_attn_in['Wk'], 'L0_attn_bk': _L0_attn_in['bk'], 'L0_attn_Wv': _L0_attn_in['Wv'], 'L0_attn_bv': _L0_attn_in['bv'], 'L0_attn_Wp': _L0_attn_in['Wp'], 'L0_attn_bp': _L0_attn_in['bp'], 'L0_xattn_Wq': _L0_xattn_in['Wq'], 'L0_xattn_Wkv': _L0_xattn_in['Wkv'], 'L0_xattn_Wout': _L0_xattn_in['Wout'], 'L0_xattn_bout': _L0_xattn_in['bout'], 'L0_ffn_gate_w': _L0_ffn_in['gate_w'], 'L0_ffn_gate_b': _L0_ffn_in['gate_b'], 'L0_ffn_val_w': _L0_ffn_in['val_w'], 'L0_ffn_val_b': _L0_ffn_in['val_b'], 'L0_ffn_out_w': _L0_ffn_in['out_w'], 'L0_ffn_out_b': _L0_ffn_in['out_b'], 'L1_attn_W_q': _L1_attn_in['W_q'], 'L1_attn_W_kv': _L1_attn_in['W_kv'], 'L1_attn_W_o': _L1_attn_in['W_o'], 'L1_xattn_Wq': _L1_xattn_in['Wq'], 'L1_xattn_Wk': _L1_xattn_in['Wk'], 'L1_xattn_Wv': _L1_xattn_in['Wv'], 'L1_xattn_Wo': _L1_xattn_in['Wo'], 'L1_xattn_gq': _L1_xattn_in['gq'], 'L1_xattn_gk': _L1_xattn_in['gk'], 'L1_ffn_w_gate': _L1_ffn_in['w_gate'], 'L1_ffn_w1': _L1_ffn_in['w1'], 'L1_ffn_w3': _L1_ffn_in['w3'], 'L1_ffn_w2': _L1_ffn_in['w2'], 'L2_attn_w_qkv': _L2_attn_in['w_qkv'], 'L2_attn_w_out': _L2_attn_in['w_out'], 'L2_attn_decay_param': _L2_attn_in['decay_param'], 'L2_xattn_Wq': _L2_xattn_in['Wq'], 'L2_xattn_bq': _L2_xattn_in['bq'], 'L2_xattn_Wk': _L2_xattn_in['Wk'], 'L2_xattn_bk': _L2_xattn_in['bk'], 'L2_xattn_Wv': _L2_xattn_in['Wv'], 'L2_xattn_bv': _L2_xattn_in['bv'], 'L2_xattn_Wkv_dca': _L2_xattn_in['Wkv_dca'], 'L2_xattn_bkv_dca': _L2_xattn_in['bkv_dca'], 'L2_xattn_qn_w': _L2_xattn_in['qn_w'], 'L2_xattn_qn_b': _L2_xattn_in['qn_b'], 'L2_xattn_kn_w': _L2_xattn_in['kn_w'], 'L2_xattn_kn_b': _L2_xattn_in['kn_b'], 'L2_xattn_kn_dca_w': _L2_xattn_in['kn_dca_w'], 'L2_xattn_kn_dca_b': _L2_xattn_in['kn_dca_b'], 'L2_xattn_Wo': _L2_xattn_in['Wo'], 'L2_xattn_bo': _L2_xattn_in['bo'], 'L2_ffn_W_base': _L2_ffn_in['W_base'], 'L2_ffn_b_base': _L2_ffn_in['b_base'], 'L2_ffn_A_s': _L2_ffn_in['A_s'], 'L2_ffn_B_s': _L2_ffn_in['B_s'], 'L2_ffn_A_r': _L2_ffn_in['A_r'], 'L2_ffn_B_r': _L2_ffn_in['B_r'], 'L2_ffn_W_router': _L2_ffn_in['W_router'], 'L2_ffn_b_router': _L2_ffn_in['b_router'], 'L3_attn_W_in': _L3_attn_in['W_in'], 'L3_attn_conv_w': _L3_attn_in['conv_w'], 'L3_attn_conv_b': _L3_attn_in['conv_b'], 'L3_attn_A': _L3_attn_in['A'], 'L3_attn_D': _L3_attn_in['D'], 'L3_attn_dt_bias': _L3_attn_in['dt_bias'], 'L3_attn_norm_w': _L3_attn_in['norm_w'], 'L3_attn_W_out': _L3_attn_in['W_out'], 'L3_xattn_Wq': _L3_xattn_in['Wq'], 'L3_xattn_Wk': _L3_xattn_in['Wk'], 'L3_xattn_Wv': _L3_xattn_in['Wv'], 'L3_xattn_Wo': _L3_xattn_in['Wo'], 'L3_ffn_down_w': _L3_ffn_in['down_w'], 'L3_ffn_down_b': _L3_ffn_in['down_b'], 'L3_ffn_up_w': _L3_ffn_in['up_w'], 'L3_ffn_up_b': _L3_ffn_in['up_b'], 'L3_ffn_router_w': _L3_ffn_in['router_w'], 'L3_ffn_router_b': _L3_ffn_in['router_b'], 'L3_ffn_shared_w1': _L3_ffn_in['shared_w1'], 'L3_ffn_shared_b1': _L3_ffn_in['shared_b1'], 'L3_ffn_shared_w2': _L3_ffn_in['shared_w2'], 'L3_ffn_shared_b2': _L3_ffn_in['shared_b2'], 'L3_ffn_core_w': _L3_ffn_in['core_w'], 'L3_ffn_core_b': _L3_ffn_in['core_b'], 'L3_ffn_e0_w1': _L3_ffn_in['e0_w1'], 'L3_ffn_e0_b1': _L3_ffn_in['e0_b1'], 'L3_ffn_e0_w2': _L3_ffn_in['e0_w2'], 'L3_ffn_e0_b2': _L3_ffn_in['e0_b2'], 'L3_ffn_e1_w1': _L3_ffn_in['e1_w1'], 'L3_ffn_e1_b1': _L3_ffn_in['e1_b1'], 'L3_ffn_e1_w2': _L3_ffn_in['e1_w2'], 'L3_ffn_e1_b2': _L3_ffn_in['e1_b2'], 'L3_ffn_e2_w1': _L3_ffn_in['e2_w1'], 'L3_ffn_e2_b1': _L3_ffn_in['e2_b1'], 'L3_ffn_e2_w2': _L3_ffn_in['e2_w2'], 'L3_ffn_e2_b2': _L3_ffn_in['e2_b2'], 'L3_ffn_e3_w1': _L3_ffn_in['e3_w1'], 'L3_ffn_e3_b1': _L3_ffn_in['e3_b1'], 'L3_ffn_e3_w2': _L3_ffn_in['e3_w2'], 'L3_ffn_e3_b2': _L3_ffn_in['e3_b2'], 'L3_ffn_e4_w1': _L3_ffn_in['e4_w1'], 'L3_ffn_e4_b1': _L3_ffn_in['e4_b1'], 'L3_ffn_e4_w2': _L3_ffn_in['e4_w2'], 'L3_ffn_e4_b2': _L3_ffn_in['e4_b2'], 'L3_ffn_e5_w1': _L3_ffn_in['e5_w1'], 'L3_ffn_e5_b1': _L3_ffn_in['e5_b1'], 'L3_ffn_e5_w2': _L3_ffn_in['e5_w2'], 'L3_ffn_e5_b2': _L3_ffn_in['e5_b2'], 'L3_ffn_e6_w1': _L3_ffn_in['e6_w1'], 'L3_ffn_e6_b1': _L3_ffn_in['e6_b1'], 'L3_ffn_e6_w2': _L3_ffn_in['e6_w2'], 'L3_ffn_e6_b2': _L3_ffn_in['e6_b2'], 'L3_ffn_e7_w1': _L3_ffn_in['e7_w1'], 'L3_ffn_e7_b1': _L3_ffn_in['e7_b1'], 'L3_ffn_e7_w2': _L3_ffn_in['e7_w2'], 'L3_ffn_e7_b2': _L3_ffn_in['e7_b2']}

def reference(x, ctx_1024, fside_BxSx2_0, mask_BxS2_bf1, L0_attn_Wq, L0_attn_bq, L0_attn_Wk, L0_attn_bk, L0_attn_Wv, L0_attn_bv, L0_attn_Wp, L0_attn_bp, L0_xattn_Wq, L0_xattn_Wkv, L0_xattn_Wout, L0_xattn_bout, L0_ffn_gate_w, L0_ffn_gate_b, L0_ffn_val_w, L0_ffn_val_b, L0_ffn_out_w, L0_ffn_out_b, L1_attn_W_q, L1_attn_W_kv, L1_attn_W_o, L1_xattn_Wq, L1_xattn_Wk, L1_xattn_Wv, L1_xattn_Wo, L1_xattn_gq, L1_xattn_gk, L1_ffn_w_gate, L1_ffn_w1, L1_ffn_w3, L1_ffn_w2, L2_attn_w_qkv, L2_attn_w_out, L2_attn_decay_param, L2_xattn_Wq, L2_xattn_bq, L2_xattn_Wk, L2_xattn_bk, L2_xattn_Wv, L2_xattn_bv, L2_xattn_Wkv_dca, L2_xattn_bkv_dca, L2_xattn_qn_w, L2_xattn_qn_b, L2_xattn_kn_w, L2_xattn_kn_b, L2_xattn_kn_dca_w, L2_xattn_kn_dca_b, L2_xattn_Wo, L2_xattn_bo, L2_ffn_W_base, L2_ffn_b_base, L2_ffn_A_s, L2_ffn_B_s, L2_ffn_A_r, L2_ffn_B_r, L2_ffn_W_router, L2_ffn_b_router, L3_attn_W_in, L3_attn_conv_w, L3_attn_conv_b, L3_attn_A, L3_attn_D, L3_attn_dt_bias, L3_attn_norm_w, L3_attn_W_out, L3_xattn_Wq, L3_xattn_Wk, L3_xattn_Wv, L3_xattn_Wo, L3_ffn_down_w, L3_ffn_down_b, L3_ffn_up_w, L3_ffn_up_b, L3_ffn_router_w, L3_ffn_router_b, L3_ffn_shared_w1, L3_ffn_shared_b1, L3_ffn_shared_w2, L3_ffn_shared_b2, L3_ffn_core_w, L3_ffn_core_b, L3_ffn_e0_w1, L3_ffn_e0_b1, L3_ffn_e0_w2, L3_ffn_e0_b2, L3_ffn_e1_w1, L3_ffn_e1_b1, L3_ffn_e1_w2, L3_ffn_e1_b2, L3_ffn_e2_w1, L3_ffn_e2_b1, L3_ffn_e2_w2, L3_ffn_e2_b2, L3_ffn_e3_w1, L3_ffn_e3_b1, L3_ffn_e3_w2, L3_ffn_e3_b2, L3_ffn_e4_w1, L3_ffn_e4_b1, L3_ffn_e4_w2, L3_ffn_e4_b2, L3_ffn_e5_w1, L3_ffn_e5_b1, L3_ffn_e5_w2, L3_ffn_e5_b2, L3_ffn_e6_w1, L3_ffn_e6_b1, L3_ffn_e6_w2, L3_ffn_e6_b2, L3_ffn_e7_w1, L3_ffn_e7_b1, L3_ffn_e7_w2, L3_ffn_e7_b2):
    import jax
    import jax.numpy as jnp

    def _L0_attn_ref(x, Wq, bq, Wk, bk, Wv, bv, Wp, bp):
        import jax, jax.numpy as jnp
        import numpy as np
        B, T, C = (2, 256, 256)
        N_HEAD = 16
        HEAD_DIM = C // N_HEAD
        Bx, Tx, Cx = x.shape

        def lin(x, W, b):
            return jnp.einsum('btc,dc->btd', x, W) + b

        def split_heads(y):
            return y.reshape(Bx, Tx, N_HEAD, HEAD_DIM).transpose(0, 2, 1, 3)
        q = split_heads(lin(x, Wq, bq))
        k = split_heads(lin(x, Wk, bk))
        v = split_heads(lin(x, Wv, bv))
        scale = 1.0 / np.sqrt(HEAD_DIM).astype(np.float32)
        attn = jnp.einsum('bhqd,bhkd->bhqk', q, k) * scale
        causal = jnp.tril(jnp.ones((Tx, Tx), dtype=bool))
        attn = jnp.where(causal[None, None], attn, -jnp.inf)
        attn = jax.nn.softmax(attn, axis=-1)
        out = jnp.einsum('bhqk,bhkd->bhqd', attn, v)
        out = out.transpose(0, 1, 3, 2).reshape(Bx, Tx, Cx)
        return lin(out, Wp, bp)

    def _L0_xattn_ref(x, ctx, pos_map, ctx_pos_map, Wq, Wkv, Wout, bout):
        import jax, jax.numpy as jnp
        import numpy as np
        DIM = 256
        CTX_DIM = 128
        N_HEADS = 32
        HEAD_DIM = DIM // N_HEADS
        POS_DIM = 2
        B, N, CTXN = (2, 256, 256)
        ROPE_BASE = 10000.0

        def apply_axial_rope(x, pos):
            b, n, h, d = x.shape
            p = pos.shape[-1]
            dpa = d // p
            half = dpa // 2
            freqs = ROPE_BASE ** (-jnp.arange(half, dtype=x.dtype) / half)
            ang = pos[..., :, None] * freqs
            cos = jnp.cos(ang)[:, :, None, :, :]
            sin = jnp.sin(ang)[:, :, None, :, :]
            xr = x.reshape(b, n, h, p, half, 2)
            x1, x2 = (xr[..., 0], xr[..., 1])
            out = jnp.stack([x1 * cos - x2 * sin, x1 * sin + x2 * cos], axis=-1)
            return out.reshape(b, n, h, d)
        b, n, _ = x.shape
        ctx_n = ctx.shape[1]
        q = (x @ Wq).reshape(b, n, N_HEADS, HEAD_DIM)
        k, v = jnp.split(ctx @ Wkv, 2, axis=-1)
        k = k.reshape(b, ctx_n, N_HEADS, HEAD_DIM)
        v = v.reshape(b, ctx_n, N_HEADS, HEAD_DIM)
        q = apply_axial_rope(q, pos_map)
        k = apply_axial_rope(k, ctx_pos_map)
        scale = 1.0 / np.sqrt(HEAD_DIM).astype(np.float32)
        logits = jnp.einsum('bqhd,bkhd->bhqk', q, k) * scale
        w = jax.nn.softmax(logits, axis=-1)
        attn = jnp.einsum('bhqk,bkhd->bqhd', w, v)
        attn = attn.reshape(b, n, N_HEADS * HEAD_DIM)
        return attn @ Wout + bout

    def _L0_ffn_ref(x, gate_w, gate_b, val_w, val_b, out_w, out_b):
        import jax, jax.numpy as jnp
        import numpy as np
        D_MODEL = 256
        HIDDEN = 4 * D_MODEL
        B, S = (2, 512)

        def bit_linear(x, w, b):
            gamma_x = jnp.clip(jnp.max(jnp.abs(x), axis=-1, keepdims=True), 1e-05, None)
            scale_x = 127.0 / gamma_x
            x_dq = jnp.clip(jnp.round(x * scale_x), -128.0, 127.0) / scale_x
            x_ste = x + jax.lax.stop_gradient(x_dq - x)
            gamma_w = jnp.clip(jnp.mean(jnp.abs(w)), 1e-05, None)
            w_dq = jnp.clip(jnp.round(w / gamma_w), -1.0, 1.0) * gamma_w
            w_ste = w + jax.lax.stop_gradient(w_dq - w)
            return jnp.einsum('bsd,hd->bsh', x_ste, w_ste) + b
        gate = jax.nn.silu(bit_linear(x, gate_w, gate_b))
        val = bit_linear(x, val_w, val_b)
        return bit_linear(gate * val, out_w, out_b)

    def _L1_attn_ref(x, W_q, W_kv, W_o):
        import jax, jax.numpy as jnp
        import numpy as np
        NUM_HEADS = 16

        def _l2_normalize_complex(z):
            n = jnp.sqrt(jnp.sum(jnp.abs(z) ** 2, axis=-1, keepdims=True))
            return z / n
        B, S, D = x.shape
        H = NUM_HEADS
        hd = D // H
        q = (x @ W_q.T).reshape(B, S, H, hd)
        kv = (x @ W_kv.T).reshape(B, S, H, hd)
        qf = jnp.fft.fft(q, axis=-1)
        kvf = jnp.fft.fft(kv, axis=-1)
        qf = _l2_normalize_complex(qf)
        kvf = _l2_normalize_complex(kvf)
        kvf = jnp.cumsum(kvf, axis=1)
        qv = qf * kvf
        values_hat = jnp.fft.ifft(qv, axis=-1).real.astype(x.dtype)
        values_hat = values_hat.reshape(B, S, D)
        return values_hat @ W_o.T

    def _L1_xattn_ref(hidden_states, encoder_hidden_states, Wq, Wk, Wv, Wo, gq, gk):
        import jax, jax.numpy as jnp
        import numpy as np
        EPS = 1e-05

        def rmsnorm(x, g, eps=EPS):
            var = jnp.mean(jnp.square(x), axis=-1, keepdims=True)
            return x * jax.lax.rsqrt(var + eps) * g
        B, Sq, _ = hidden_states.shape
        Skv = encoder_hidden_states.shape[1]
        D = gq.shape[0]
        H = Wq.shape[1] // D
        scale = 1.0 / np.sqrt(D)
        q = (hidden_states @ Wq).reshape(B, Sq, H, D)
        k = (encoder_hidden_states @ Wk).reshape(B, Skv, H, D)
        v = (encoder_hidden_states @ Wv).reshape(B, Skv, H, D)
        q = rmsnorm(q, gq)
        k = rmsnorm(k, gk)
        scores = jnp.einsum('bqhd,bkhd->bhqk', q, k) * scale
        attn = jax.nn.softmax(scores, axis=-1)
        out = jnp.einsum('bhqk,bkhd->bqhd', attn, v)
        out = out.reshape(B, Sq, H * D)
        return out @ Wo

    def _L1_ffn_ref(hidden_states, w_gate, w1, w3, w2):
        import jax, jax.numpy as jnp
        import numpy as np
        E, TOPK, H, I = (8, 2, 256, 512)
        SOFTCAP = 30.0
        orig_shape = hidden_states.shape
        x = hidden_states.reshape(-1, H)
        logits = x @ w_gate
        logits = SOFTCAP * jnp.tanh(logits / SOFTCAP)
        probs = jax.nn.softmax(logits, axis=-1)
        _, idx = jax.lax.top_k(probs, TOPK)
        mask = jax.nn.one_hot(idx, E, dtype=probs.dtype).sum(-2)
        weights = probs * mask
        out = jnp.zeros_like(x)
        for e in range(E):
            h = jax.nn.silu(x @ w1[e]) * (x @ w3[e])
            out = out + h @ w2[e] * weights[:, e:e + 1]
        return out.reshape(orig_shape)

    def _L2_attn_ref(x, w_qkv, w_out, decay_param):
        import jax, jax.numpy as jnp
        import numpy as np
        H = 16
        EPS_DEN = 1e-06

        def _decay_scan(x, decay, init):
            xT = jnp.moveaxis(x, 2, 0)

            def step(s, xt):
                s = decay * s + xt
                return (s, s)
            _, ys = jax.lax.scan(step, init, xT)
            return jnp.moveaxis(ys, 0, 2)

        def _phi(z):
            return jax.nn.elu(z) + 1.0

        def _reference_tuple_inner(x, w_qkv, w_out, decay_param):
            B, T, Hid = x.shape
            D = Hid // H
            qkv = x @ w_qkv
            q, k, v = jnp.split(qkv, 3, axis=-1)

            def to_bhtd(t):
                return t.reshape(B, T, H, D).transpose(0, 2, 1, 3)
            q = _phi(to_bhtd(q))
            k = _phi(to_bhtd(k))
            v = to_bhtd(v)
            decay = jax.nn.sigmoid(decay_param).reshape(1, H, 1)
            init = jnp.zeros((B, H, D), dtype=x.dtype)
            running_kv = _decay_scan(k * v, decay, init)
            running_ksum = _decay_scan(k, decay, init)
            den = jnp.clip(jnp.sum(q * running_ksum, axis=-1, keepdims=True), EPS_DEN, None)
            out = q * running_kv / den
            out = out.transpose(0, 2, 1, 3).reshape(B, T, Hid) @ w_out
            new_kv = running_kv[:, :, -1, :]
            new_ksum = running_ksum[:, :, -1, :]
            return (out, new_kv, new_ksum)
        return _reference_tuple_inner(x, w_qkv, w_out, decay_param)[0]

    def _L2_xattn_ref(x, y, Wq, bq, Wk, bk, Wv, bv, Wkv_dca, bkv_dca, qn_w, qn_b, kn_w, kn_b, kn_dca_w, kn_dca_b, Wo, bo):
        import jax, jax.numpy as jnp
        import numpy as np
        B, S1, S2, DCA = (2, 256, 128, 16)
        QDIM, KDIM, H = (256, 128, 16)
        HD = QDIM // H
        SCALE = HD ** (-0.5)
        EPS = 1e-06
        DCA_WEIGHT = 1.0

        def _ln(t, w, b):
            m = jnp.mean(t, axis=-1, keepdims=True)
            v = jnp.var(t, axis=-1, keepdims=True)
            return (t - m) * jax.lax.rsqrt(v + EPS) * w + b

        def _attn(q, k, v):
            s = jnp.einsum('bhqd,bhkd->bhqk', q, k) * SCALE
            p = jax.nn.softmax(s, axis=-1)
            return jnp.einsum('bhqk,bhkd->bhqd', p, v)
        b, s1, _ = x.shape
        y_dca = y[:, -DCA:, :]
        y_main = y[:, :-DCA, :]
        kv_dca = (y_dca @ Wkv_dca + bkv_dca).reshape(b, DCA, 2, H, HD)
        k_dca = _ln(kv_dca[:, :, 0], kn_dca_w, kn_dca_b)
        v_dca = kv_dca[:, :, 1]
        s2 = y_main.shape[1]
        q = _ln((x @ Wq + bq).reshape(b, s1, H, HD), qn_w, qn_b)
        kv = jnp.concatenate([y_main @ Wk + bk, y_main @ Wv + bv], axis=-1)
        kv = kv.reshape(b, s2, H, 2 * HD)
        k = _ln(kv[..., :HD], kn_w, kn_b)
        v = kv[..., HD:]
        qT = q.transpose(0, 2, 1, 3)
        ctx = _attn(qT, k.transpose(0, 2, 1, 3), v.transpose(0, 2, 1, 3))
        ctx = ctx.transpose(0, 2, 1, 3).reshape(b, s1, QDIM)
        ctx_dca = _attn(qT, k_dca.transpose(0, 2, 1, 3), v_dca.transpose(0, 2, 1, 3))
        ctx_dca = ctx_dca.transpose(0, 2, 1, 3).reshape(b, s1, QDIM)
        ctx = ctx + DCA_WEIGHT * ctx_dca
        return ctx @ Wo + bo

    def _L2_ffn_ref(x, W_base, b_base, A_s, B_s, A_r, B_r, W_router, b_router):
        import jax, jax.numpy as jnp
        import numpy as np
        B, S, D, E, R, TOP_K = (4, 512, 256, 6, 16, 2)
        base_out = jax.lax.stop_gradient(jnp.einsum('bsd,df->bsf', x, W_base) + b_base)
        shared_out = jnp.einsum('bsr,rf->bsf', jnp.einsum('bsd,dr->bsr', x, A_s), B_s)
        gates = jax.nn.softmax(jnp.einsum('bsd,de->bse', x, W_router) + b_router, axis=-1)
        topk_w, topk_i = jax.lax.top_k(gates, TOP_K)
        w_per_e = jnp.sum(topk_w[..., None] * jax.nn.one_hot(topk_i, E, dtype=x.dtype), axis=2)
        h = jnp.einsum('bsd,edr->bser', x, A_r)
        hw = h * w_per_e[..., None]
        routed_out = jnp.einsum('bser,erf->bsf', hw, B_r)
        return base_out + shared_out + routed_out

    def _L3_attn_ref(hidden_states, W_in, conv_w, conv_b, A, D, dt_bias, norm_w, W_out):
        import jax, jax.numpy as jnp
        import numpy as np
        D_MODEL = 256
        D_STATE = 128
        D_CONV = 4
        NHEADS = 64
        NGROUPS = 1
        HEAD_DIM = 64
        CHUNK = 128
        EPS = 1e-05
        D_INNER = NHEADS * HEAD_DIM
        CONV_DIM = D_INNER + 2 * NGROUPS * D_STATE
        D_IN_PROJ = 2 * D_INNER + 2 * NGROUPS * D_STATE + NHEADS

        def _silu(x):
            return x * jax.nn.sigmoid(x)

        def _causal_conv1d(x, w, b):
            K = w.shape[1]
            S = x.shape[1]
            xp = jnp.pad(x, ((0, 0), (K - 1, 0), (0, 0)))
            y = sum((xp[:, k:k + S, :] * w[None, None, :, k].swapaxes(-1, -1) for k in range(0)))
            y = jnp.zeros_like(x)
            for k in range(K):
                y = y + xp[:, k:k + S, :] * w[:, k][None, None, :]
            return _silu(y + b)

        def _ssd(x, dt, A, Bm, Cm, chunk):
            b, s, h, p = x.shape
            g, n = (Bm.shape[2], Bm.shape[3])
            hh = h // g
            c = s // chunk
            x = x.reshape(b, c, chunk, g, hh, p)
            dt = dt.reshape(b, c, chunk, g, hh)
            Bm = Bm.reshape(b, c, chunk, g, n)
            Cm = Cm.reshape(b, c, chunk, g, n)
            dA = dt * A.reshape(g, hh)
            dA_cs = jnp.cumsum(dA, axis=2)
            dtx = dt[..., None] * x
            diff = dA_cs[:, :, :, None] - dA_cs[:, :, None, :]
            mask = jnp.tril(jnp.ones((chunk, chunk), bool))
            L = jnp.exp(jnp.where(mask[None, None, :, :, None, None], diff, -jnp.inf))
            Y = jnp.einsum('bcign,bcjgn,bcijgh,bcjghp->bcighp', Cm, Bm, L, dtx)
            decay = jnp.exp(dA_cs[:, :, -1:] - dA_cs)
            states = jnp.einsum('bcjgn,bcjgh,bcjghp->bcghpn', Bm, decay, dtx)
            chunk_decay = jnp.exp(dA_cs[:, :, -1])

            def step(prev, inp):
                cd, st = inp
                return (cd[..., None, None] * prev + st, prev)
            init = jnp.zeros_like(states[:, 0])
            _, prevs = jax.lax.scan(step, init, (jnp.moveaxis(chunk_decay, 1, 0), jnp.moveaxis(states, 1, 0)))
            prevs = jnp.moveaxis(prevs, 0, 1)
            Y = Y + jnp.einsum('bcign,bcghpn,bcigh->bcighp', Cm, prevs, jnp.exp(dA_cs))
            return Y.reshape(b, s, h, p)
        Bsz, S, _ = hidden_states.shape
        zxbcdt = hidden_states @ W_in
        z = zxbcdt[..., :D_INNER]
        xbc = zxbcdt[..., D_INNER:D_INNER + CONV_DIM]
        dt = zxbcdt[..., D_INNER + CONV_DIM:]
        xbc = _causal_conv1d(xbc, conv_w, conv_b)
        x = xbc[..., :D_INNER].reshape(Bsz, S, NHEADS, HEAD_DIM)
        Bm = xbc[..., D_INNER:D_INNER + NGROUPS * D_STATE].reshape(Bsz, S, NGROUPS, D_STATE)
        Cm = xbc[..., D_INNER + NGROUPS * D_STATE:].reshape(Bsz, S, NGROUPS, D_STATE)
        dt = jax.nn.softplus(dt + dt_bias)
        y = _ssd(x, dt, A, Bm, Cm, CHUNK)
        y = y + D[None, None, :, None] * x
        y = y.reshape(Bsz, S, D_INNER)
        yg = y * _silu(z)
        gsz = D_INNER // NGROUPS
        ygr = yg.reshape(Bsz, S, NGROUPS, gsz)
        rms = jax.lax.rsqrt(jnp.mean(ygr * ygr, axis=-1, keepdims=True) + EPS)
        yn = (ygr * rms).reshape(Bsz, S, D_INNER) * norm_w
        return yn @ W_out

    def _L3_xattn_ref(text_hidden, vision_tokens, vision_mask, Wq, Wk, Wv, Wo):
        import jax, jax.numpy as jnp
        import numpy as np
        N_HEADS = 16
        N_KV_HEADS = 8
        HEAD_DIM = 128
        D_TEXT = 256
        D_VISION = 128
        GROUPS = N_HEADS // N_KV_HEADS
        B, T_text, _ = text_hidden.shape
        T_vis = vision_tokens.shape[1]
        scale = jnp.float32(np.sqrt(HEAD_DIM))
        q = (text_hidden @ Wq).reshape(B, T_text, N_HEADS, HEAD_DIM).transpose(0, 2, 1, 3)
        k = (vision_tokens @ Wk).reshape(B, T_vis, N_KV_HEADS, HEAD_DIM).transpose(0, 2, 1, 3)
        v = (vision_tokens @ Wv).reshape(B, T_vis, N_KV_HEADS, HEAD_DIM).transpose(0, 2, 1, 3)
        k = jnp.repeat(k, GROUPS, axis=1)
        v = jnp.repeat(v, GROUPS, axis=1)
        scores = jnp.einsum('bhtd,bhsd->bhts', q, k) / scale
        mask = vision_mask[:, None, None, :]
        scores = jnp.where(mask, scores, -jnp.inf)
        attn = jax.nn.softmax(scores, axis=-1)
        attn = jnp.nan_to_num(attn, nan=0.0)
        out = jnp.einsum('bhts,bhsd->bhtd', attn, v)
        out = out.transpose(0, 2, 1, 3).reshape(B, T_text, N_HEADS * HEAD_DIM)
        return out @ Wo

    def _L3_ffn_ref(x, down_w, down_b, up_w, up_b, router_w, router_b, shared_w1, shared_b1, shared_w2, shared_b2, core_w, core_b, e0_w1, e0_b1, e0_w2, e0_b2, e1_w1, e1_b1, e1_w2, e1_b2, e2_w1, e2_b1, e2_w2, e2_b2, e3_w1, e3_b1, e3_w2, e3_b2, e4_w1, e4_b1, e4_w2, e4_b2, e5_w1, e5_b1, e5_w2, e5_b2, e6_w1, e6_b1, e6_w2, e6_b2, e7_w1, e7_b1, e7_w2, e7_b2):
        import jax, jax.numpy as jnp
        import numpy as np
        COST_LAMBDA = 1e-07
        HID = [128, 256, 384, 512, 128, 256, 384, 512]
        TOP_K = 2

        def _gelu(v):
            return jax.nn.gelu(v, approximate=False)

        def _forward(x, down_w, down_b, up_w, up_b, router_w, router_b, shared_w1, shared_b1, shared_w2, shared_b2, core_w, core_b, expert_params):
            E = len(expert_params)
            h = x @ down_w + down_b
            cost = jnp.array([w1.shape[0] * w1.shape[1] + w2.shape[0] * w2.shape[1] for w1, _, w2, _ in expert_params], jnp.float32)
            logits = x @ router_w + router_b - COST_LAMBDA * cost
            probs = jax.nn.softmax(logits, axis=-1)
            topv, topi = jax.lax.top_k(probs, TOP_K)
            gate = jax.nn.softmax(topv, axis=-1)
            out = jnp.zeros_like(h)
            for k in range(TOP_K):
                mask = jax.nn.one_hot(topi[..., k], E, dtype=h.dtype)
                acc = jnp.zeros_like(h)
                for e, (w1, b1, w2, b2) in enumerate(expert_params):
                    hm = h * mask[..., e:e + 1]
                    acc = acc + (_gelu(_gelu(hm) @ w1 + b1) @ w2 + b2)
                out = out + acc * gate[..., k:k + 1]
            out = out + 0.1 * (_gelu(_gelu(h) @ shared_w1 + shared_b1) @ shared_w2 + shared_b2)
            out = out @ up_w + up_b
            out = out + (_gelu(x) @ core_w + core_b)
            return out
        ep = [(e0_w1, e0_b1, e0_w2, e0_b2), (e1_w1, e1_b1, e1_w2, e1_b2), (e2_w1, e2_b1, e2_w2, e2_b2), (e3_w1, e3_b1, e3_w2, e3_b2), (e4_w1, e4_b1, e4_w2, e4_b2), (e5_w1, e5_b1, e5_w2, e5_b2), (e6_w1, e6_b1, e6_w2, e6_b2), (e7_w1, e7_b1, e7_w2, e7_b2)]
        return _forward(x, down_w, down_b, up_w, up_b, router_w, router_b, shared_w1, shared_b1, shared_w2, shared_b2, core_w, core_b, ep)
    x = x + _L0_attn_ref(_layernorm(x, axis=-1), L0_attn_Wq, L0_attn_bq, L0_attn_Wk, L0_attn_bk, L0_attn_Wv, L0_attn_bv, L0_attn_Wp, L0_attn_bp)
    x = x + _L0_xattn_ref(_layernorm(x, axis=-1), ctx_1024, fside_BxSx2_0, fside_BxSx2_0, L0_xattn_Wq, L0_xattn_Wkv, L0_xattn_Wout, L0_xattn_bout)
    x = x + _L0_ffn_ref(_layernorm(x, axis=-1), L0_ffn_gate_w, L0_ffn_gate_b, L0_ffn_val_w, L0_ffn_val_b, L0_ffn_out_w, L0_ffn_out_b)
    x = x + _L1_attn_ref(_layernorm(x, axis=-1), L1_attn_W_q, L1_attn_W_kv, L1_attn_W_o)
    x = x + _L1_xattn_ref(_layernorm(x, axis=-1), ctx_1024, L1_xattn_Wq, L1_xattn_Wk, L1_xattn_Wv, L1_xattn_Wo, L1_xattn_gq, L1_xattn_gk)
    x = x + _L1_ffn_ref(_layernorm(x, axis=-1), L1_ffn_w_gate, L1_ffn_w1, L1_ffn_w3, L1_ffn_w2)
    x = x + _L2_attn_ref(_layernorm(x, axis=-1), L2_attn_w_qkv, L2_attn_w_out, L2_attn_decay_param)
    x = x + _L2_xattn_ref(_layernorm(x, axis=-1), ctx_1024, L2_xattn_Wq, L2_xattn_bq, L2_xattn_Wk, L2_xattn_bk, L2_xattn_Wv, L2_xattn_bv, L2_xattn_Wkv_dca, L2_xattn_bkv_dca, L2_xattn_qn_w, L2_xattn_qn_b, L2_xattn_kn_w, L2_xattn_kn_b, L2_xattn_kn_dca_w, L2_xattn_kn_dca_b, L2_xattn_Wo, L2_xattn_bo)
    x = x + _L2_ffn_ref(_layernorm(x, axis=-1), L2_ffn_W_base, L2_ffn_b_base, L2_ffn_A_s, L2_ffn_B_s, L2_ffn_A_r, L2_ffn_B_r, L2_ffn_W_router, L2_ffn_b_router)
    x = x + _L3_attn_ref(_layernorm(x, axis=-1), L3_attn_W_in, L3_attn_conv_w, L3_attn_conv_b, L3_attn_A, L3_attn_D, L3_attn_dt_bias, L3_attn_norm_w, L3_attn_W_out)
    x = x + _L3_xattn_ref(_layernorm(x, axis=-1), ctx_1024, mask_BxS2_bf1, L3_xattn_Wq, L3_xattn_Wk, L3_xattn_Wv, L3_xattn_Wo)
    x = x + _L3_ffn_ref(_layernorm(x, axis=-1), L3_ffn_down_w, L3_ffn_down_b, L3_ffn_up_w, L3_ffn_up_b, L3_ffn_router_w, L3_ffn_router_b, L3_ffn_shared_w1, L3_ffn_shared_b1, L3_ffn_shared_w2, L3_ffn_shared_b2, L3_ffn_core_w, L3_ffn_core_b, L3_ffn_e0_w1, L3_ffn_e0_b1, L3_ffn_e0_w2, L3_ffn_e0_b2, L3_ffn_e1_w1, L3_ffn_e1_b1, L3_ffn_e1_w2, L3_ffn_e1_b2, L3_ffn_e2_w1, L3_ffn_e2_b1, L3_ffn_e2_w2, L3_ffn_e2_b2, L3_ffn_e3_w1, L3_ffn_e3_b1, L3_ffn_e3_w2, L3_ffn_e3_b2, L3_ffn_e4_w1, L3_ffn_e4_b1, L3_ffn_e4_w2, L3_ffn_e4_b2, L3_ffn_e5_w1, L3_ffn_e5_b1, L3_ffn_e5_w2, L3_ffn_e5_b2, L3_ffn_e6_w1, L3_ffn_e6_b1, L3_ffn_e6_w2, L3_ffn_e6_b2, L3_ffn_e7_w1, L3_ffn_e7_b1, L3_ffn_e7_w2, L3_ffn_e7_b2)
    return x

_drawn_inputs = setup_inputs


def setup_inputs(seed=0):
    import zlib

    import numpy as np

    out = dict(_drawn_inputs(seed))
    spreads = {'L0_attn_bq': (0.0, 0.273),
     'L0_attn_bk': (0.0, 0.8),
     'L0_attn_bv': (0.0, 0.1),
     'L0_attn_bp': (0.0, 0.1),
     'L0_xattn_bout': (0.0, 0.1),
     'L0_ffn_gate_b': (0.0, 0.8),
     'L0_ffn_val_b': (0.0, 0.658),
     'L0_ffn_out_b': (0.0, 0.1),
     'L1_xattn_gq': (1.0, 0.2),
     'L1_xattn_gk': (1.0, 0.2),
     'L2_attn_decay_param': (0.949999988079071, 0.6),
     'L2_xattn_bq': (0.0, 0.8),
     'L2_xattn_bk': (0.0, 0.48),
     'L2_xattn_bv': (0.0, 0.447),
     'L2_xattn_bkv_dca': (0.0, 0.316),
     'L2_xattn_qn_w': (1.0, 0.6),
     'L2_xattn_qn_b': (0.0, 0.8),
     'L2_xattn_kn_w': (1.0, 0.6),
     'L2_xattn_kn_b': (0.0, 0.8),
     'L2_xattn_kn_dca_w': (1.0, 0.6),
     'L2_xattn_kn_dca_b': (0.0, 0.8),
     'L2_xattn_bo': (0.0, 0.1),
     'L3_attn_norm_w': (1.0, 0.2),
     'L3_ffn_down_b': (0.0, 0.8),
     'L3_ffn_up_b': (0.0, 0.1),
     'L3_ffn_router_b': (0.0, 0.8),
     'L3_ffn_shared_b1': (0.0, 0.8),
     'L3_ffn_shared_b2': (0.0, 0.8),
     'L3_ffn_core_b': (0.0, 0.1),
     'L3_ffn_e0_b1': (0.0, 0.8),
     'L3_ffn_e0_b2': (0.0, 0.562),
     'L3_ffn_e1_b1': (0.0, 0.8),
     'L3_ffn_e1_b2': (0.0, 0.722),
     'L3_ffn_e2_b1': (0.0, 0.8),
     'L3_ffn_e2_b2': (0.0, 0.715),
     'L3_ffn_e3_b1': (0.0, 0.8),
     'L3_ffn_e3_b2': (0.0, 0.8),
     'L3_ffn_e4_b1': (0.0, 0.8),
     'L3_ffn_e4_b2': (0.0, 0.778),
     'L3_ffn_e5_b1': (0.0, 0.8),
     'L3_ffn_e5_b2': (0.0, 0.635),
     'L3_ffn_e6_b1': (0.0, 0.8),
     'L3_ffn_e6_b2': (0.0, 0.708),
     'L3_ffn_e7_b1': (0.0, 0.8),
     'L3_ffn_e7_b2': (0.0, 0.78)}
    factors = {'L0_ffn_gate_w': 3.468,
     'L0_ffn_val_w': 3.315,
     'L0_ffn_out_w': 3.185,
     'L2_attn_w_qkv': 8.0,
     'L2_attn_w_out': 8.0,
     'L2_xattn_Wq': 3.287,
     'L2_xattn_Wk': 2.683,
     'L2_xattn_Wv': 2.787,
     'L2_ffn_b_base': 3.693,
     'L2_ffn_A_s': 3.009,
     'L2_ffn_B_s': 3.055,
     'L2_ffn_A_r': 8.0,
     'L2_ffn_B_r': 8.0,
     'L2_ffn_W_router': 8.0,
     'L2_ffn_b_router': 8.0,
     'L3_attn_A': 8.0,
     'L3_xattn_Wq': 8.0,
     'L3_xattn_Wk': 8.0,
     'L3_ffn_down_w': 8.0,
     'L3_ffn_router_w': 8.0,
     'L3_ffn_shared_w1': 8.0,
     'L3_ffn_shared_w2': 8.0,
     'L3_ffn_e0_w1': 8.0,
     'L3_ffn_e0_w2': 8.0,
     'L3_ffn_e1_w1': 8.0,
     'L3_ffn_e1_w2': 8.0,
     'L3_ffn_e2_w1': 8.0,
     'L3_ffn_e2_w2': 8.0,
     'L3_ffn_e3_w1': 8.0,
     'L3_ffn_e3_w2': 8.0,
     'L3_ffn_e4_w1': 8.0,
     'L3_ffn_e4_w2': 8.0,
     'L3_ffn_e5_w1': 8.0,
     'L3_ffn_e5_w2': 8.0,
     'L3_ffn_e6_w1': 8.0,
     'L3_ffn_e6_w2': 8.0,
     'L3_ffn_e7_w1': 8.0,
     'L3_ffn_e7_w2': 8.0}
    for name, (base, spread) in spreads.items():
        noise = np.random.default_rng([zlib.crc32(name.encode()), seed]).standard_normal(out[name].shape)
        drawn = base * np.exp(spread * noise) if base else spread * noise
        out[name] = jnp.asarray(drawn.astype(out[name].dtype))
    for name, factor in factors.items():
        out[name] = (out[name] * factor).astype(out[name].dtype)
    return out
```

```python
from contextlib import ExitStack

import numpy as np

import concourse.bass as bass
from concourse import mybir

FIRST, LAST = 0, 11

P = 128
NB = 8
C = 256
KC = C // P
TOK = NB * P
HALF = TOK // 2
F32 = mybir.dt.float32
BF16 = mybir.dt.bfloat16
U8 = mybir.dt.uint8
ALU = mybir.AluOpType
ACT = mybir.ActivationFunctionType
AX = mybir.AxisListType
BIG = 1.0e30
ROUND = 12582912.0
TWO_PI = 6.283185307179586


class Chain:

    def __init__(self, eng, sem):
        self.eng, self.sem, self.n = eng, sem, 0

    def __call__(self, ins):
        self.n += 1
        ins.then_inc(self.sem, 1)
        self.eng.wait_ge(self.sem, self.n)

    def restart(self):
        self.eng.sem_clear(self.sem)
        self.n = 0


class Stage:

    def __init__(self, k, name):
        self.k, self.nc, self.name, self.sems = k, k.nc, name, []

    def __enter__(self):
        self.ctx = ExitStack()
        return self

    def sb(self, name, shape, dt=F32):
        return self.ctx.enter_context(self.nc.sbuf_tensor(f"{self.name}_{name}", shape, dt))

    def sem(self, name):
        s = self.nc.alloc_semaphore(f"{self.name}_{name}")
        self.sems.append(s)
        return s

    def __exit__(self, *e):
        if e[0] is None:
            for s in self.sems:
                self.nc.gpsimd.sem_clear(s)
            self.nc.all_engine_barrier()
            for s in self.sems:
                self.nc.release_semaphore(s)
            self.ctx.close()
        return False


class K:
    pass


def sbuf_views(tile, names, widths):
    out, at = {}, 0
    for n in names:
        out[n] = tile[:, at:at + widths[n]]
        at += widths[n]
    return out


def layernorm(k, tag, eps=1e-5):
    nc, x, xn, xnT, ps = k.nc, k.x, k.xn, k.xnT, k.ps
    with Stage(k, f"ln{tag}") as st:
        stats = st.sb("stats", [P, NB, 6])
        mv = st.sb("mv", [P, NB, 2])
        inv = st.sb("inv", [P, NB])
        rstd = st.sb("rstd", [P, NB])
        s_stats, s_mv, s_rstd = st.sem("stats_done"), st.sem("mean_var_done"), st.sem("rstd_done")
        s_inv = st.sem("inverse_variance")
        s_xn, s_xnT, s_copied = st.sem("xn_done"), st.sem("xnT_in_psum"), st.sem("xnT_copied")
        with nc.Block() as block:

            @block.vector
            def _(dve):
                for b in range(NB):
                    nc.vector.bn_stats(stats[:, b, :], x[:, b, :]).then_inc(s_stats, 1)
                for b in range(NB):
                    dve.wait_ge(s_stats, b + 1)
                    nc.vector.bn_aggr(mv[:, b, :], stats[:, b, :]).then_inc(s_mv, 1)
                dve.wait_ge(s_mv, NB)
                nc.vector.tensor_scalar(inv[:, :], mv[:, :, 1], eps, None, ALU.add).then_inc(s_inv, 1)
                dve.wait_ge(s_inv, 1)
                nc.vector.reciprocal(inv[:, :], inv[:, :]).then_inc(s_inv, 1)
                dve.wait_ge(s_rstd, 1)
                for b in range(NB):
                    nc.vector.tensor_scalar(xn[:, b, :], x[:, b, :], mv[:, b, 0:1], rstd[:, b:b + 1],
                                            ALU.subtract, ALU.mult).then_inc(s_xn, 1)
                for u in range(2, 4):
                    dve.wait_ge(s_xnT, 4 * (u + 1))
                    nc.vector.tensor_copy(xnT[:, u % 2, (u // 2) * HALF:(u // 2 + 1) * HALF],
                                          ps[u][:, :]).then_inc(s_copied, 1)

            @block.scalar
            def _(act):
                act.wait_ge(s_inv, 2)
                nc.scalar.activation(rstd[:, :], inv[:, :], ACT.Sqrt).then_inc(s_rstd, 1)
                for u in range(0, 2):
                    act.wait_ge(s_xnT, 4 * (u + 1))
                    nc.scalar.activation(xnT[:, u % 2, (u // 2) * HALF:(u // 2 + 1) * HALF],
                                         ps[u][:, :], ACT.Copy).then_inc(s_copied, 1)

            @block.tensor
            def _(pe):
                for u in range(4):
                    for j in range(4):
                        b = 4 * (u // 2) + j
                        pe.wait_ge(s_xn, b + 1)
                        nc.tensor.transpose(ps[u][:, j * P:(j + 1) * P],
                                            xn[:, b, (u % 2) * P:(u % 2 + 1) * P],
                                            k.ident).then_inc(s_xnT, 1)


def along(ap, n):
    return ap.unsqueeze(len(ap.shape)).to_broadcast([*ap.shape, n])


def over(ap, n):
    return ap.unsqueeze(1).to_broadcast([ap.shape[0], n, *ap.shape[1:]])


class Router:

    def __init__(self, k, st, E, bank):
        self.k, self.E = k, E
        t = lambda name, *shape: st.sb(name, [P, NB, *shape])
        self.logits = bank[:, 0:NB * E].rearrange("p (b e) -> p b e", b=NB)
        self.z, self.e, self.probs = t("z", E), t("e", E), t("probs", E)
        self.m, self.s, self.r = t("zmax"), t("zsum"), t("zrec")
        self.eq, self.cand, self.left = t("eq", E), t("cand", E), t("left", E)
        self.first, self.second = t("first", E), t("second", E)
        self.at, self.top1, self.top2 = t("at"), t("top1"), t("top2")
        self.s_logits, self.s_z, self.s_e = st.sem("logits_ready"), st.sem("z_ready"), st.sem("z_exp_ready")

    def matmuls(self, w):
        nc = self.k.nc
        for b in range(NB):
            for kc in range(KC):
                mm = nc.tensor.matmul(self.logits[:, b, :], self.k.xnT[:, kc, b * P:(b + 1) * P],
                                      w[:, kc, :], start=(kc == 0), stop=(kc == KC - 1))
        mm.then_inc(self.s_logits, 1)

    def exponent(self, act, scale=1.0):
        act.wait_ge(self.s_z, 1)
        self.k.nc.scalar.activation(self.e[:, :, :], self.z[:, :, :], ACT.Exp, scale=scale).then_inc(self.s_e, 1)

    def softmax(self, dve, step):
        nc, E = self.k.nc, self.E
        step(nc.vector.tensor_reduce(self.m[:, :], self.z[:, :, :], AX.X, ALU.max))
        nc.vector.tensor_tensor(self.z[:, :, :], self.z[:, :, :], along(self.m[:, :], E),
                                ALU.subtract).then_inc(self.s_z, 1)
        dve.wait_ge(self.s_e, 1)
        step(nc.vector.tensor_reduce(self.s[:, :], self.e[:, :, :], AX.X, ALU.add))
        step(nc.vector.reciprocal(self.r[:, :], self.s[:, :]))
        step(nc.vector.tensor_tensor(self.probs[:, :, :], self.e[:, :, :], along(self.r[:, :], E), ALU.mult))

    def pick(self, step, probs, top, onehot):
        nc, E, c = self.k.nc, self.E, self.k.c
        step(nc.vector.tensor_reduce(top[:, :], probs[:, :, :], AX.X, ALU.max))
        step(nc.vector.tensor_tensor(self.eq[:, :, :], probs[:, :, :], along(top[:, :], E), ALU.is_equal))
        step(nc.vector.scalar_tensor_tensor(self.cand[:, :, :], self.eq[:, :, :], -100.0,
                                            over(c["iota_far"][:, 0:E], NB), ALU.mult, ALU.add))
        step(nc.vector.tensor_reduce(self.at[:, :], self.cand[:, :, :], AX.X, ALU.min))
        step(nc.vector.tensor_tensor(onehot[:, :, :], over(c["iota"][:, 0:E], NB), along(self.at[:, :], E),
                                     ALU.is_equal))

    def top_two(self, step):
        nc = self.k.nc
        self.pick(step, self.probs, self.top1, self.first)
        step(nc.vector.scalar_tensor_tensor(self.left[:, :, :], self.first[:, :, :], -2.0, self.probs[:, :, :],
                                            ALU.mult, ALU.add))
        self.pick(step, self.left, self.top2, self.second)

    def masked(self, step, weights):
        nc = self.k.nc
        step(nc.vector.tensor_tensor(self.eq[:, :, :], self.first[:, :, :], self.second[:, :, :], ALU.add))
        step(nc.vector.tensor_tensor(weights, self.probs[:, :, :], self.eq[:, :, :], ALU.mult))


class SmallHeads:

    def __init__(self, k, st, H, hd, parts, scale, mask=None, turn=True):
        self.k, self.nc, self.H, self.hd, self.scale, self.mask, self.turn = k, k.nc, H, hd, scale, mask, turn
        self.parts = parts
        self.VW = len(parts) * (hd + 1)
        self.G = H // 4
        self.HC = H // KC
        self.qT, self.kT = st.sb("qT", [P, KC, TOK]), st.sb("kT", [P, KC, TOK])
        self.v = st.sb("v", [P, NB, H, self.VW])
        self.qb = st.sb("qb", [P, KC, P])
        self.km = st.sb("km", [P, H, P])
        self.sm = st.sb("sm", [P, 2, 4, P])
        self.mx = st.sb("mx", [P, 2, 4, len(parts)])
        self.p = st.sb("p", [P, 2, 4 * P])
        self.pT = st.sb("pT", [P, 2, 4 * P])
        self.rec = st.sb("rec", [P, H, len(parts)])
        self.on = st.sb("on", [P, H, hd])
        self.on2 = st.sb("on2", [P, H, hd])
        self.onT = st.sb("onT", [P, KC, P])
        n = ("qb_ready", "km_ready", "scores_psum", "scores_read", "shifted", "exp_ready", "pT_psum", "pT_ready",
             "pv_done", "o_read", "o_norm", "oT_psum", "oT_ready", "y_psum", "y_added", "attn_step", "max_ready",
             "masked")
        (self.s_qb, self.s_km, self.s_s, self.s_sread, self.s_sm, self.s_p, self.s_pTp, self.s_pT, self.s_pv,
         self.s_oread, self.s_on, self.s_oTp, self.s_oT, self.s_y, self.s_x, self.s_step, self.s_mx,
         self.s_masked) = (st.sem(m) for m in n)

    def run(self, eng, body, tail):
        body(eng, 0, False)
        with eng.Fori(1, NB) as j:
            body(eng, j, True)
        tail(eng)


    def scores(self, pe, j, g):
        c = g // (self.G // KC)
        if g % (self.G // KC) == 0:
            pe.wait_ge(self.s_km, j * KC + c + 1)
            if c == 0:
                pe.wait_ge(self.s_qb, j + 1)
        done = j * self.G + g
        if g < 2:
            pe.wait_ge(self.s_sread, max(done - 1, 0) if isinstance(done, int) else done - 1)
        else:
            pe.wait_ge(self.s_sread, done - 1)
        rhs = self.km[:, 4 * g:4 * g + 4, :].rearrange("p h t -> p (h t)")
        self.nc.tensor.matmul(self.k.ps[g % 2][:, :], self.qb[:, c, :], rhs, start=True, stop=True).then_inc(self.s_s, 1)

    def turn_probs(self, pe, j, g):
        done = j * self.G + g
        pe.wait_ge(self.s_p, done + 1)
        pe.wait_ge(self.s_pT, max(done - 1, 0) if isinstance(done, int) else done - 1)
        for h in range(4):
            mm = self.nc.tensor.transpose(self.k.ps[2 + g % 2][:, h * P:(h + 1) * P],
                                          self.p[:, g % 2, h * P:(h + 1) * P], self.k.ident)
        mm.then_inc(self.s_pTp, 1)

    def o_bank(self, h):
        per = self.H if self.H * self.VW <= HALF else self.H // 2
        return self.k.ps[4 + h // per], (h % per) * self.VW

    def values(self, pe, j, g):
        pe.wait_ge(self.s_pT, j * self.G + g + 1)
        if g == 0:
            pe.wait_ge(self.s_oread, j)
        for h in range(4 * g, 4 * g + 4):
            bank, at = self.o_bank(h)
            mm = self.nc.tensor.matmul(bank[:, at:at + self.VW], self.pT[:, g % 2, (h % 4) * P:(h % 4 + 1) * P],
                                       self.v[:, bass.ds(j, 1), h, :].rearrange("p a n -> p (a n)"),
                                       start=True, stop=True)
        mm.then_inc(self.s_pv, 1)

    def turn_out(self, pe, j):
        pe.wait_ge(self.s_on, j)
        for c in range(KC):
            mm = self.nc.tensor.transpose(self.k.ps[6][:, c * P:(c + 1) * P],
                                          self.on[:, c * self.HC:(c + 1) * self.HC, :].rearrange("p h d -> p (h d)"),
                                          self.k.ident)
        mm.then_inc(self.s_oTp, 1)

    def project(self, pe, j):
        pe.wait_ge(self.s_x, j - 1)
        if self.turn:
            pe.wait_ge(self.s_oT, j)
        else:
            pe.wait_ge(self.s_on, j)
        for c in range(KC):
            if self.turn:
                lhsT = self.onT[:, c, :]
            else:
                lhsT = self.on[:, :, :].rearrange("p h d -> p (h d)")[:, c:C:KC]
            mm = self.nc.tensor.matmul(self.k.ps[6][:, C:2 * C], lhsT, self.w_out[:, c, :],
                                       start=(c == 0), stop=(c == KC - 1))
        mm.then_inc(self.s_y, 1)

    def pe(self, pe, j, prev):
        G = self.G
        self.scores(pe, j, 0)
        self.scores(pe, j, 1)
        if prev and self.turn:
            self.turn_out(pe, j)
        for g in range(G):
            self.turn_probs(pe, j, g)
            if g + 2 < G:
                self.scores(pe, j, g + 2)
            if g == 0 and prev:
                self.project(pe, j)
            if g:
                self.values(pe, j, g - 1)
        self.values(pe, j, G - 1)

    def pe_tail(self, pe):
        if self.turn:
            self.turn_out(pe, NB)
        self.project(pe, NB)


    def act(self, act, j, prev):
        nc, G, ps = self.nc, self.G, self.k.ps
        for g in range(G + 1):
            if g < G:
                done = j * G + g
                act.wait_ge(self.s_sm, done + 1)
                act.wait_ge(self.s_pTp, max(done - 1, 0) if isinstance(done, int) else done - 1)
                nc.scalar.activation(self.p[:, g % 2, :], self.sm[:, g % 2, :, :].rearrange("p h t -> p (h t)"),
                                     ACT.Exp, scale=self.scale).then_inc(self.s_p, 1)
            if g == 0 and prev and self.turn:
                self.copy_out(act, j)
            if g:
                done = j * G + g - 1
                act.wait_ge(self.s_pTp, done + 1)
                act.wait_ge(self.s_pv, max(done - 1, 0) if isinstance(done, int) else done - 1)
                nc.scalar.activation(self.pT[:, (g - 1) % 2, :], ps[2 + (g - 1) % 2][:, :],
                                     ACT.Copy).then_inc(self.s_pT, 1)

    def copy_out(self, act, j):
        act.wait_ge(self.s_oTp, j)
        act.wait_ge(self.s_y, j - 1)
        self.nc.scalar.activation(self.onT[:, :, :], self.k.ps[6][:, 0:C].rearrange("p (c t) -> p c t", c=KC),
                                  ACT.Copy).then_inc(self.s_oT, 1)

    def act_tail(self, act):
        if self.turn:
            self.copy_out(act, NB)


    def softmax(self, dve, j, g):
        nc, k = self.nc, self.k
        done = j * self.G + g
        s = self.k.ps[g % 2][:, :].rearrange("p (h t) -> p h t", h=4)
        sm, mx = self.sm[:, g % 2, :, :], self.mx[:, g % 2, :, :]
        dve.wait_ge(self.s_s, done + 1)
        dve.wait_ge(self.s_p, max(done - 1, 0) if isinstance(done, int) else done - 1)
        if self.mask is not None:
            nc.vector.tensor_tensor(sm, s, over(self.mask, 4), ALU.add).then_inc(self.s_sread, 1)
            dve.wait_ge(self.s_sread, done + 1)
            s = sm
        n = len(self.parts)
        for i, (a, b) in enumerate(self.parts):
            nc.vector.tensor_reduce(mx[:, :, i], s[:, :, a:b], AX.X, ALU.max).then_inc(self.s_mx, 1)
        for i, (a, b) in enumerate(self.parts):
            dve.wait_ge(self.s_mx, done * n + i + 1)
            ins = nc.vector.tensor_tensor(sm[:, :, a:b], s[:, :, a:b], along(mx[:, :, i], b - a), ALU.subtract)
        if self.mask is None:
            ins.then_inc(self.s_sread, 1)
            dve.wait_ge(self.s_sread, done + 1)
            dve.sem_inc(self.s_sm, 1)
        else:
            ins.then_inc(self.s_sm, 1)

    def normalise(self, dve, j):
        nc, n = self.nc, len(self.parts)
        dve.wait_ge(self.s_pv, j * self.G)
        if self.turn:
            dve.wait_ge(self.s_oTp, j - 1)
        else:
            dve.wait_ge(self.s_y, j - 1)
        banks = 1 if self.H * self.VW <= HALF else 2
        hb = self.H // banks
        D = self.hd + 1
        step = self.step
        for b in range(banks):
            o = self.k.ps[4 + b][:, 0:hb * self.VW].rearrange("p (h a d) -> p h a d", h=hb, a=n)
            hs = slice(b * hb, (b + 1) * hb)
            step(nc.vector.reciprocal(self.rec[:, hs, :], o[:, :, :, self.hd]))
            step(nc.vector.tensor_tensor(self.on[:, hs, :], o[:, :, 0, 0:self.hd],
                                         along(self.rec[:, hs, 0], self.hd), ALU.mult))
            if n == 2:
                step(nc.vector.tensor_tensor(self.on2[:, hs, :], o[:, :, 1, 0:self.hd],
                                             along(self.rec[:, hs, 1], self.hd), ALU.mult))
                step(nc.vector.tensor_tensor(self.on[:, hs, :], self.on[:, hs, :], self.on2[:, hs, :], ALU.add))
        dve.sem_inc(self.s_on, 1)
        dve.sem_inc(self.s_oread, 1)

    def add(self, dve, j):
        self.nc_add(dve, j)

    def nc_add(self, dve, j):
        xb = self.k.x[:, bass.ds(j - 1, 1), :].rearrange("p a n -> p (a n)")
        dve.wait_ge(self.s_y, j)
        self.nc.vector.tensor_tensor(xb, xb, self.k.ps[6][:, C:2 * C], ALU.add).then_inc(self.s_x, 1)

    def dve(self, dve, j, prev):
        self.step.restart()
        if prev:
            self.normalise(dve, j)
        for g in range(self.G):
            self.softmax(dve, j, g)
            if g == 1 and prev:
                self.nc_add(dve, j)

    def dve_tail(self, dve):
        self.step.restart()
        self.normalise(dve, NB)
        self.nc_add(dve, NB)


    def pool(self, pool, j, prev):
        nc, G = self.nc, self.G
        for c in range(KC):
            if prev:
                pool.wait_ge(self.s_s, j * G - (KC - 1 - c) * (G // KC))
            if c == 0:
                if prev:
                    pool.wait_ge(self.s_s, j * G)
                nc.gpsimd.tensor_copy(self.qb[:, :, :], self.qT[:, :, bass.ds(j * P, P)]).then_inc(self.s_qb, 1)
            hs = slice(c * self.HC, (c + 1) * self.HC)
            nc.gpsimd.tensor_tensor(self.km[:, hs, :],
                                    over(self.kT[:, c, bass.ds(j * P, P)], self.HC),
                                    along(self.in_head, P), ALU.mult).then_inc(self.s_km, 1)


class Turns:

    def __init__(self, k, uses, sems):
        assert len(uses) % 4 == 0
        self.k, self.uses, self.sems = k, uses, sems
        self.count = {n: sum(u[0] == n for u in uses) for n in {u[0] for u in uses}}

    def bank(self, use):
        return self.k.ps[4 + self.uses.index(use) % 4]

    def free(self, pe, j, use):
        at = self.uses.index(use)
        name, n = self.uses[at - 4]
        if name is None:
            return
        if at >= 4:
            pe.wait_ge(self.sems[name], j * self.count[name] + n + 1)
        elif not (isinstance(j, int) and j == 0):
            pe.wait_ge(self.sems[name], (j - 1) * self.count[name] + n + 1)


class WideHeads:

    def __init__(self, k, st, turns):
        self.k, self.nc, self.turns = k, k.nc, turns
        self.qT, self.kT = st.sb("qT", [P, TOK]), st.sb("kT", [P, TOK])
        self.v = st.sb("v", [P, TOK])
        self.mx = st.sb("mx", [P, 2, 4])
        self.nb = st.sb("minus_max", [P, 2, 4])
        self.p = st.sb("p", [P, 2, HALF])
        self.sum = st.sb("sum", [P, 2, 4])
        self.pT = st.sb("pT", [P, 2, HALF])
        self.oT = st.sb("oT", [P, 2, HALF])
        self.zero = st.sb("zero", [P, P])
        n = ("s_psum", "bias_ready", "exp_done", "probs_ready", "pT_psum", "pT_ready", "oT_psum", "oT_ready", "y_added",
             "zero_set", "back_step")
        (self.s_s, self.s_nb, self.s_exp, self.s_p, self.s_pTp, self.s_pT, self.s_oTp, self.s_oT, self.s_y,
         self.s_zero, self.s_step) = (st.sem(m) for m in n)

    def clear_sums(self, pe):
        pe.wait_ge(self.s_zero, 1)
        for n in range(4):
            self.nc.tensor.matmul(self.k.ps[n][:, :], self.zero[:, :], self.k.xnT[:, 0, 0:HALF], start=True,
                                  stop=False, skip_group_check=True)

    def pe(self, pe, j, u, tag, wo):
        nc, tr = self.nc, self.turns
        for h in range(2):
            tr.free(pe, j, ("s" + tag, h))
            for b in range(4):
                t = slice((4 * h + b) * P, (4 * h + b + 1) * P)
                mm = nc.tensor.matmul(tr.bank(("s" + tag, h))[:, b * P:(b + 1) * P], self.qT[:, t], self.kT[:, t],
                                      start=True, stop=True)
            mm.then_inc(self.s_s, 1)
        for h in range(2):
            tr.free(pe, j, ("t" + tag, h))
            pe.wait_ge(self.s_p, u * 2 + h + 1)
            for b in range(4):
                mm = nc.tensor.transpose(tr.bank(("t" + tag, h))[:, b * P:(b + 1) * P],
                                         self.p[:, h, b * P:(b + 1) * P], self.k.ident)
            mm.then_inc(self.s_pTp, 1)
        for h in range(2):
            tr.free(pe, j, ("o" + tag, h))
            pe.wait_ge(self.s_pT, u * 2 + h + 1)
            for b in range(4):
                t = slice((4 * h + b) * P, (4 * h + b + 1) * P)
                mm = nc.tensor.matmul(tr.bank(("o" + tag, h))[:, b * P:(b + 1) * P], self.v[:, t],
                                      self.pT[:, h, b * P:(b + 1) * P], start=True, stop=True)
            mm.then_inc(self.s_oTp, 1)
        for h in range(2):
            pe.wait_ge(self.s_oT, u * 2 + h + 1)
            for b in range(4):
                g = 4 * h + b
                mm = nc.tensor.matmul(self.k.ps[g // 2][:, (g % 2) * C:(g % 2 + 1) * C],
                                      self.oT[:, h, b * P:(b + 1) * P], wo, start=False, stop=False,
                                      skip_group_check=True)
            mm.then_inc(self.s_y, 1)

    def act(self, act, j, u, tag, scale):
        nc, tr = self.nc, self.turns
        for h in range(2):
            act.wait_ge(self.s_nb, u * 2 + h + 1)
            for b in range(4):
                src = self.scored(tr, tag, h)
                ins = nc.scalar.activation(self.p[:, h, b * P:(b + 1) * P], src[:, b * P:(b + 1) * P], ACT.Exp,
                                           bias=self.nb[:, h, b:b + 1], scale=scale(4 * h + b),
                                           accum_out=self.sum[:, h, b:b + 1])
            ins.then_inc(self.s_exp, 1)
        for h in range(2):
            act.wait_ge(self.s_oTp, u * 2 + h + 1)
            act.wait_ge(self.s_y, self.before(u) + h)
            nc.scalar.activation(self.oT[:, h, :], tr.bank(("o" + tag, h))[:, :], ACT.Copy).then_inc(self.s_oT, 1)

    @staticmethod
    def before(u):
        return max(2 * u - 1, 0) if isinstance(u, int) else 2 * u - 1

    def scored(self, tr, tag, h):
        return tr.bank(("s" + tag, h))

    def dve_probs(self, dve, step, u, h):
        nc = self.nc
        dve.wait_ge(self.s_exp, u * 2 + h + 1)
        step(nc.vector.reciprocal(self.sum[:, h, :], self.sum[:, h, :]))
        p3 = self.p[:, h, :].rearrange("p (b t) -> p b t", b=4)
        nc.vector.tensor_tensor(p3, p3, along(self.sum[:, h, :], P), ALU.mult).then_inc(self.s_p, 1)

    def dve_turned(self, dve, u, tag, h):
        dve.wait_ge(self.s_pTp, u * 2 + h + 1)
        self.nc.vector.tensor_copy(self.pT[:, h, :], self.turns.bank(("t" + tag, h))[:, :]).then_inc(self.s_pT, 1)

    def add(self, dve):
        x = self.k.x
        for n in range(4):
            self.nc.vector.tensor_tensor(x[:, 2 * n:2 * n + 2, :], x[:, 2 * n:2 * n + 2, :],
                                         self.k.ps[n][:, :].rearrange("p (b n) -> p b n", b=2), ALU.add)


def rsqrt(nc, step, v, y, t):
    I32 = mybir.dt.int32
    step(nc.vector.tensor_scalar(t.bitcast(I32), v.bitcast(I32), 1, None, ALU.logical_shift_right))
    step(nc.vector.tensor_scalar(y.bitcast(I32), t.bitcast(I32), -1.0, 1597463007.0, ALU.mult, ALU.add))
    for _ in range(4):
        step(nc.vector.tensor_tensor(t, y, y, ALU.mult))
        step(nc.vector.scalar_tensor_tensor(t, t, -0.5, v, ALU.mult, ALU.mult))
        step(nc.vector.scalar_tensor_tensor(y, t, 1.5, y, ALU.add, ALU.mult))


def l0_attn(k):
    nc, x, xnT, ps = k.nc, k.x, k.xnT, k.ps
    H, hd = 16, 16
    with Stage(k, "L0a") as st:
        img = st.sb("weights", [P, k.width["L0a"]])
        w = sbuf_views(img, *k.parts["L0a"])
        wq, wk, wv, wp = (w[n].rearrange("p (k n) -> p k n", k=KC) for n in ("wq", "wk", "wv", "wp"))
        a = SmallHeads(k, st, H, hd, [(0, P)], 1.0 / hd ** 0.5, mask=k.c["causal"], turn=False)
        a.w_out, a.in_head = wp, k.c["in_head16"]
        s_w, s_qk, s_v = st.sem("w_loaded"), st.sem("qk_psum"), st.sem("v_psum")
        s_in, s_bias, s_ones, s_vin = st.sem("qk_ready"), st.sem("bias_added"), st.sem("ones_set"), st.sem("v_ready")
        with nc.Block() as block:

            @block.sync
            def _(sp):
                sp.dma_start(img[:, :], k.dram["L0a"]).then_inc(s_w, 16)

            @block.tensor
            def _(pe):
                pe.wait_ge(s_w, 16)
                for n, wm in enumerate((wq, wk)):
                    for c in range(KC):
                        for h in range(2):
                            bank = 4 * n + 2 * c + h
                            for kc in range(KC):
                                mm = nc.tensor.matmul(ps[bank][:, :], wm[:, kc, c * P:(c + 1) * P],
                                                      xnT[:, kc, h * HALF:(h + 1) * HALF],
                                                      start=(kc == 0), stop=(kc == KC - 1))
                            mm.then_inc(s_qk, 1)
                for n in range(4):
                    pe.wait_ge(s_in, n + 1)
                    for b in (2 * n, 2 * n + 1):
                        for kc in range(KC):
                            mm = nc.tensor.matmul(ps[n][:, (b % 2) * C:(b % 2 + 1) * C],
                                                  xnT[:, kc, b * P:(b + 1) * P], wv[:, kc, :],
                                                  start=(kc == 0), stop=(kc == KC - 1))
                    mm.then_inc(s_v, 1)
                pe.wait_ge(s_in, 8)
                pe.wait_ge(s_vin, 4)
                a.run(pe, a.pe, a.pe_tail)

            @block.scalar
            def _(act):
                for n, (dst, b) in enumerate(((a.qT, w["bq"]), (a.kT, w["bk"]))):
                    for c in range(KC):
                        for h in range(2):
                            act.wait_ge(s_qk, 4 * n + 2 * c + h + 1)
                            nc.scalar.activation(dst[:, c, h * HALF:(h + 1) * HALF], ps[4 * n + 2 * c + h][:, :],
                                                 ACT.Identity, bias=b[:, c:c + 1]).then_inc(s_in, 1)
                a.run(act, a.act, a.act_tail)

            @block.vector
            def _(dve):
                a.step = Chain(dve, a.s_step)
                dve.wait_ge(s_w, 16)
                for n in range(4):
                    dve.wait_ge(s_v, n + 1)
                    for j in range(2):
                        ins = nc.vector.tensor_tensor(
                            a.v[:, 2 * n + j, :, 0:hd],
                            ps[n][:, j * C:(j + 1) * C].rearrange("p (h d) -> p h d", h=H),
                            w["bv"].rearrange("p (h d) -> p h d", h=H), ALU.add)
                    ins.then_inc(s_vin, 1)
                dve.wait_ge(s_bias, 1)
                a.run(dve, a.dve, a.dve_tail)

            @block.gpsimd
            def _(pool):
                nc.gpsimd.memset(a.v[:, :, :, hd:hd + 1], 1.0).then_inc(s_ones, 1)
                pool.wait_ge(s_w, 16)
                nc.gpsimd.tensor_tensor(x[:, :, :], x[:, :, :], over(w["bp"], NB), ALU.add).then_inc(s_bias, 1)
                pool.wait_ge(s_in, 8)
                a.run(pool, a.pool, lambda eng: None)


def l0_xattn(k):
    nc, x, xnT, ctxT, ps = k.nc, k.x, k.xnT, k.ctxT, k.ps
    H, hd = 32, 8
    PAIRS = hd // 2
    with Stage(k, "L0x") as st:
        img = st.sb("weights", [P, k.width["L0x"]])
        w = sbuf_views(img, *k.parts["L0x"])
        wq, wout = (w[n].rearrange("p (k n) -> p k n", k=KC) for n in ("wq", "wout"))
        wk, wv = w["wkv"][:, 0:C], w["wkv"][:, C:2 * C]
        a = SmallHeads(k, st, H, hd, [(0, P)], 1.0 / hd ** 0.5)
        a.w_out, a.in_head = wout, k.c["in_head8"]
        ang = st.sb("ang", [P, 2, NB, PAIRS])
        turns = st.sb("turns", [P, 2, NB, PAIRS])
        trig = st.sb("trig", [P, 2, NB, PAIRS])
        cosd = st.sb("cosd", [P, NB, PAIRS, 2])
        sind = st.sb("sind", [P, NB, PAIRS, 2])
        rot = st.sb("rot", [P, 2, 2 * C])
        crossed = st.sb("crossed", [P, 2, 2 * C])
        s_w, s_qk, s_v = st.sem("w_loaded"), st.sem("qk_psum"), st.sem("v_psum")
        s_ang, s_trig, s_read, s_rot = st.sem("angles"), st.sem("trig_ready"), st.sem("qk_read"), st.sem("rotated")
        s_t, s_in, s_vin = st.sem("qkT_psum"), st.sem("qkT_ready"), st.sem("v_ready")
        s_ones, s_bias = st.sem("ones_set"), st.sem("bias_added")
        with nc.Block() as block:

            @block.sync
            def _(sp):
                sp.dma_start(img[:, :], k.dram["L0x"]).then_inc(s_w, 16)

            @block.tensor
            def _(pe):
                pe.wait_ge(s_w, 16)

                def turn(b):
                    pe.wait_ge(s_rot, b + 1)
                    if b >= 2:
                        pe.wait_ge(s_in, b - 1)
                    for n in range(4):
                        mm = nc.tensor.transpose(ps[4 + b % 2][:, n * P:(n + 1) * P],
                                                 rot[:, b % 2, n * P:(n + 1) * P], k.ident)
                    mm.then_inc(s_t, 1)

                for b in range(NB):
                    t = slice(b * P, (b + 1) * P)
                    if b >= 2:
                        pe.wait_ge(s_read, b - 1)
                        pe.wait_ge(s_vin, b - 1)
                    for kc in range(KC):
                        nc.tensor.matmul(ps[b % 2][:, 0:C], xnT[:, kc, t], wq[:, kc, :], start=(kc == 0),
                                         stop=(kc == KC - 1))
                    nc.tensor.matmul(ps[b % 2][:, C:2 * C], ctxT[:, t], wk, start=True, stop=True).then_inc(s_qk, 1)
                    nc.tensor.matmul(ps[2 + b % 2][:, 0:C], ctxT[:, t], wv, start=True, stop=True).then_inc(s_v, 1)
                    if b:
                        turn(b - 1)
                turn(NB - 1)
                pe.wait_ge(s_in, NB)
                pe.wait_ge(s_vin, NB)
                a.run(pe, a.pe, a.pe_tail)

            @block.scalar
            def _(act):
                act.wait_ge(s_ang, 1)
                nc.scalar.activation(trig[:, :, :, :], ang[:, :, :, :], ACT.Sin).then_inc(s_trig, 1)
                for b in range(NB):
                    act.wait_ge(s_v, b + 1)
                    nc.scalar.activation(a.v[:, b, :, 0:hd], ps[2 + b % 2][:, 0:C].rearrange("p (h d) -> p h d", h=H),
                                         ACT.Copy).then_inc(s_vin, 1)
                    act.wait_ge(s_t, b + 1)
                    bank = ps[4 + b % 2][:, :].rearrange("p (m c t) -> p m c t", m=2, c=KC)
                    nc.scalar.activation(a.qT[:, :, b * P:(b + 1) * P], bank[:, 0, :, :], ACT.Copy)
                    nc.scalar.activation(a.kT[:, :, b * P:(b + 1) * P], bank[:, 1, :, :], ACT.Copy).then_inc(s_in, 1)
                a.run(act, a.act, a.act_tail)

            @block.vector
            def _(dve):
                a.step = step = Chain(dve, a.s_step)
                dve.wait_ge(s_w, 16)
                pos = w["pos"].rearrange("p (b f) -> p b f", b=NB)
                step(nc.vector.tensor_tensor(ang[:, 0, :, :], pos, over(k.c["freq"], NB), ALU.mult))
                step(nc.vector.tensor_scalar(ang[:, 1, :, :], ang[:, 0, :, :], TWO_PI / 4, None, ALU.add))
                step(nc.vector.tensor_scalar(turns[:, :, :, :], ang[:, :, :, :], 1.0 / TWO_PI, ROUND,
                                             ALU.mult, ALU.add))
                step(nc.vector.tensor_scalar(turns[:, :, :, :], turns[:, :, :, :], ROUND, -TWO_PI,
                                             ALU.subtract, ALU.mult))
                step(nc.vector.tensor_tensor(ang[:, :, :, :], ang[:, :, :, :], turns[:, :, :, :], ALU.add))
                nc.vector.tensor_scalar(ang[:, :, :, :], ang[:, :, :, :], 3.1415925, -3.1415925, ALU.min,
                                        ALU.max).then_inc(s_ang, 1)
                dve.wait_ge(s_trig, 1)
                for n in range(2):
                    step(nc.vector.tensor_copy(cosd[:, :, :, n], trig[:, 1, :, :]))
                step(nc.vector.tensor_scalar(sind[:, :, :, 0], trig[:, 0, :, :], -1.0, None, ALU.mult))
                step(nc.vector.tensor_copy(sind[:, :, :, 1], trig[:, 0, :, :]))
                for b in range(NB):
                    q = ps[b % 2][:, :].rearrange("p (h f) -> p h f", f=hd)
                    q2 = ps[b % 2][:, :].rearrange("p (h f n) -> p h f n", f=PAIRS, n=2)
                    c2 = crossed[:, b % 2, :].rearrange("p (h f n) -> p h f n", f=PAIRS, n=2)
                    r = rot[:, b % 2, :].rearrange("p (h f) -> p h f", f=hd)
                    dve.wait_ge(s_qk, b + 1)
                    if b >= 2:
                        dve.wait_ge(s_t, b - 1)
                    step(nc.vector.tensor_tensor(r, q, over(cosd[:, b, :, :].rearrange("p f n -> p (f n)"), 2 * H),
                                                 ALU.mult))
                    step(nc.vector.tensor_tensor(c2[:, :, :, 0], q2[:, :, :, 1], over(sind[:, b, :, 0], 2 * H),
                                                 ALU.mult))
                    nc.vector.tensor_tensor(c2[:, :, :, 1], q2[:, :, :, 0], over(sind[:, b, :, 1], 2 * H),
                                            ALU.mult).then_inc(s_read, 1)
                    dve.wait_ge(s_read, b + 1)
                    nc.vector.tensor_tensor(rot[:, b % 2, :], rot[:, b % 2, :], crossed[:, b % 2, :],
                                            ALU.add).then_inc(s_rot, 1)
                dve.wait_ge(s_bias, 1)
                a.run(dve, a.dve, a.dve_tail)

            @block.gpsimd
            def _(pool):
                nc.gpsimd.memset(a.v[:, :, :, hd:hd + 1], 1.0).then_inc(s_ones, 1)
                pool.wait_ge(s_w, 16)
                nc.gpsimd.tensor_tensor(x[:, :, :], x[:, :, :], over(w["bout"], NB), ALU.add).then_inc(s_bias, 1)
                pool.wait_ge(s_in, NB)
                a.run(pool, a.pool, lambda eng: None)


def l0_ffn(k):
    nc, x, xn, ps = k.nc, k.x, k.xn, k.ps
    NH = 8
    H = NH * P
    MATS = ("gate", "val", "out")
    with Stage(k, "L0f") as st:
        img = st.sb("weights", [P, k.width["L0f"]])
        w = sbuf_views(img, *k.parts["L0f"])
        mats = img[:, 0:3 * KC * H]
        tern = st.sb("ternary", [P, 3 * KC * H], BF16)
        tgate = tern[:, 0:KC * H].rearrange("p (k n) -> p k n", k=KC)
        tval = tern[:, KC * H:2 * KC * H].rearrange("p (k n) -> p k n", k=KC)
        tout = tern[:, 2 * KC * H:].rearrange("p (k n) -> p k n", k=NH)
        magic = st.sb("magic", [P, 2])
        wsum = st.sb("wsum", [P, 3])
        gamma = st.sb("gamma_w", [P, 3])
        rgamma = st.sb("rgamma_w", [P, 3])
        identb = st.sb("identb", [P, P], BF16)
        gx = st.sb("gamma_x", [P, NB])
        rgx = st.sb("rgamma_x", [P, NB])
        xs = st.sb("x_scale", [P, NB])
        gscale = st.sb("gate_scale", [P, NB])
        vscale = st.sb("val_scale", [P, NB])
        xi = st.sb("x_int", [P, NB, C], BF16)
        xiT = st.sb("x_intT", [P, KC, TOK], BF16)
        g = st.sb("g", [P, 2, H])
        v = st.sb("v", [P, 2, H])
        hs = st.sb("h_rounded", [P, 2, H])
        hi = st.sb("h_int", [P, 2, H], BF16)
        hiT = st.sb("h_intT", [P, 2, H], BF16)
        gh = st.sb("gamma_h", [P, 2])
        rgh = st.sb("rgamma_h", [P, 2])
        hsc = st.sb("h_scale", [P, 2])
        osc = st.sb("out_scale", [P, 2])
        bank16 = [ps[i][:, :].bitcast(BF16) for i in range(8)]
        s_w, s_magic, s_wsum, s_tot = st.sem("w_loaded"), st.sem("magic_set"), st.sem("w_abs_sums"), st.sem("w_totals")
        s_rg, s_wr, s_wc, s_tern = st.sem("rgamma_ready"), st.sem("w_rounded"), st.sem("w_clipped"), st.sem("ternary_ready")
        s_xi, s_xiT, s_xiTc, s_idb = st.sem("x_int_ready"), st.sem("x_intT_psum"), st.sem("x_intT_ready"), st.sem("identb")
        s_gv, s_gread, s_g, s_silu = st.sem("gate_val_psum"), st.sem("gate_val_read"), st.sem("g_ready"), st.sem("silu_ready")
        s_h, s_scale, s_hr, s_hi = st.sem("h_ready"), st.sem("scales_ready"), st.sem("h_rounded"), st.sem("h_int_ready")
        s_hT, s_hTc, s_y, s_x = st.sem("hT_psum"), st.sem("hT_ready"), st.sem("y_psum"), st.sem("x_added")
        s_dve, s_bias = st.sem("dve_step"), st.sem("bias_added")
        with nc.Block() as block:

            @block.sync
            def _(sp):
                sp.dma_start(img[:, :], k.dram["L0f"]).then_inc(s_w, 16)

            @block.gpsimd
            def _(pool):
                nc.gpsimd.memset(magic[:, 0:1], ROUND).then_inc(s_magic, 1)
                nc.gpsimd.memset(magic[:, 1:2], -ROUND).then_inc(s_magic, 1)
                nc.gpsimd.tensor_copy(identb[:, :], k.ident).then_inc(s_idb, 1)
                pool.wait_ge(s_w, 16)
                nc.gpsimd.tensor_tensor(x[:, :, :], x[:, :, :], over(w["out_b"], NB), ALU.add).then_inc(s_bias, 1)

            @block.tensor
            def _(pe):
                pe.wait_ge(s_wsum, 3)
                nc.tensor.matmul(ps[7][:, 0:3], k.c["ones"], wsum[:, :], start=True, stop=True).then_inc(s_tot, 1)
                pe.wait_ge(s_idb, 1)
                pe.wait_ge(s_xi, 1)
                for kc in range(KC):
                    for b in range(NB):
                        mm = nc.tensor.transpose(bank16[kc][:, b * P:(b + 1) * P], xi[:, b, kc * P:(kc + 1) * P],
                                                 identb[:, :])
                    mm.then_inc(s_xiT, 1)
                pe.wait_ge(s_xiTc, 2)
                pe.wait_ge(s_tern, 3)
                with pe.Fori(0, NB // 2) as i:
                    for s in range(2):
                        pe.wait_ge(s_gread, i * 2 + s)
                        for kc in range(KC):
                            for n in range(2):
                                for bank, t in ((n, tgate), (2 + n, tval)):
                                    mm = nc.tensor.matmul(ps[bank][:, :],
                                                          xiT[:, kc, bass.ds(i * 2 * P + s * P, P)],
                                                          t[:, kc, n * HALF:(n + 1) * HALF],
                                                          start=(kc == 0), stop=(kc == KC - 1))
                        mm.then_inc(s_gv, 1)
                        pe.wait_ge(s_hi, i * 2 + s + 1)
                        for n in range(NH):
                            mm = nc.tensor.transpose(bank16[4 + s][:, n * P:(n + 1) * P],
                                                     hi[:, s, n * P:(n + 1) * P], identb[:, :])
                        mm.then_inc(s_hT, 1)
                        pe.wait_ge(s_hTc, i * 2 + s + 1)
                        pe.wait_ge(s_x, i * 2)
                        for n in range(NH):
                            mm = nc.tensor.matmul(ps[6 + s][:, 0:C], hiT[:, s, n * P:(n + 1) * P], tout[:, n, :],
                                                  start=(n == 0), stop=(n == NH - 1))
                        mm.then_inc(s_y, 1)

            @block.scalar
            def _(act):
                act.wait_ge(s_rg, 1)
                act.wait_ge(s_magic, 2)
                for m in range(3):
                    t = slice(m * KC * H, (m + 1) * KC * H)
                    nc.scalar.activation(mats[:, t], mats[:, t], ACT.Identity, bias=magic[:, 0:1],
                                         scale=rgamma[:, m:m + 1]).then_inc(s_wr, 1)
                for m in range(3):
                    t = slice(m * KC * H, (m + 1) * KC * H)
                    act.wait_ge(s_wc, m + 1)
                    nc.scalar.activation(tern[:, t], mats[:, t], ACT.Identity, bias=magic[:, 1:2]).then_inc(s_tern, 1)
                with act.Fori(0, NB // 2) as i:
                    for s in range(2):
                        act.wait_ge(s_g, i * 2 + s + 1)
                        nc.scalar.activation(g[:, s, :], g[:, s, :], ACT.Silu).then_inc(s_silu, 1)
                        act.wait_ge(s_scale, i * 2 + s + 1)
                        nc.scalar.activation(hs[:, s, :], g[:, s, :], ACT.Identity, bias=magic[:, 0:1],
                                             scale=hsc[:, s:s + 1]).then_inc(s_hr, 1)
                        act.wait_ge(s_hr, i * 2 + s + 1)
                        act.wait_ge(s_hT, i * 2 + s)
                        nc.scalar.activation(hi[:, s, :], hs[:, s, :], ACT.Identity,
                                             bias=magic[:, 1:2]).then_inc(s_hi, 1)
                        act.wait_ge(s_hT, i * 2 + s + 1)
                        nc.scalar.activation(hiT[:, s, :], bank16[4 + s], ACT.Copy).then_inc(s_hTc, 1)

            @block.vector
            def _(dve):
                step = Chain(dve, s_dve)
                step(nc.vector.tensor_reduce(gx[:, :], xn[:, :, :], AX.X, ALU.max, apply_absolute_value=True))
                step(nc.vector.tensor_scalar(gx[:, :], gx[:, :], 1e-5, None, ALU.max))
                step(nc.vector.reciprocal(rgx[:, :], gx[:, :]))
                step(nc.vector.tensor_scalar(xs[:, :], rgx[:, :], 127.0, None, ALU.mult))
                step(nc.vector.tensor_tensor(xn[:, :, :], xn[:, :, :], along(xs[:, :], C), ALU.mult))
                step(nc.vector.tensor_scalar(xn[:, :, :], xn[:, :, :], ROUND, -ROUND, ALU.add, ALU.add))
                nc.vector.tensor_scalar(xi[:, :, :], xn[:, :, :], -128.0, 127.0, ALU.max, ALU.min).then_inc(s_xi, 1)
                dve.wait_ge(s_w, 16)
                for m in range(3):
                    nc.vector.tensor_reduce(wsum[:, m:m + 1], mats[:, m * KC * H:(m + 1) * KC * H], AX.X, ALU.add,
                                            apply_absolute_value=True).then_inc(s_wsum, 1)
                dve.wait_ge(s_tot, 1)
                step(nc.vector.tensor_scalar(gamma[:, :], ps[7][:, 0:3], 1.0 / (H * C), 1e-5, ALU.mult, ALU.max))
                nc.vector.reciprocal(rgamma[:, :], gamma[:, :]).then_inc(s_rg, 1)
                step(nc.vector.tensor_scalar(gscale[:, :], gx[:, :], gamma[:, 0:1], 1.0 / 127.0, ALU.mult, ALU.mult))
                step(nc.vector.tensor_scalar(vscale[:, :], gx[:, :], gamma[:, 1:2], 1.0 / 127.0, ALU.mult, ALU.mult))
                for m in range(3):
                    t = slice(m * KC * H, (m + 1) * KC * H)
                    dve.wait_ge(s_wr, m + 1)
                    nc.vector.tensor_scalar(mats[:, t], mats[:, t], ROUND - 1.0, ROUND + 1.0, ALU.max,
                                            ALU.min).then_inc(s_wc, 1)
                for kc in range(KC):
                    dve.wait_ge(s_xiT, kc + 1)
                    nc.vector.tensor_copy(xiT[:, kc, :], bank16[kc]).then_inc(s_xiTc, 1)
                dve.wait_ge(s_bias, 1)

                def add_y(i, s):
                    nc.vector.scalar_tensor_tensor(x[:, bass.ds(i * 2 + s, 1), :].rearrange("p a n -> p (a n)"),
                                                   ps[6 + s][:, 0:C], osc[:, s:s + 1],
                                                   x[:, bass.ds(i * 2 + s, 1), :].rearrange("p a n -> p (a n)"),
                                                   ALU.mult, ALU.add).then_inc(s_x, 1)

                with dve.Fori(0, NB // 2) as i:
                    step.restart()
                    for s in range(2):
                        dve.wait_ge(s_gv, i * 2 + s + 1)
                        dve.wait_ge(s_hr, i * 2)
                        gs = slice(s, s + 1)
                        for n in range(2):
                            ins = nc.vector.scalar_tensor_tensor(
                                g[:, s, n * HALF:(n + 1) * HALF], ps[n][:, :], cur_scale(gscale, i, s),
                                w["gate_b"][:, n * HALF:(n + 1) * HALF], ALU.mult, ALU.add)
                        ins.then_inc(s_g, 1)
                        for n in range(2):
                            ins = nc.vector.scalar_tensor_tensor(
                                v[:, s, n * HALF:(n + 1) * HALF], ps[2 + n][:, :], cur_scale(vscale, i, s),
                                w["val_b"][:, n * HALF:(n + 1) * HALF], ALU.mult, ALU.add)
                        ins.then_inc(s_gread, 1)
                        dve.wait_ge(s_gread, i * 2 + s + 1)
                        dve.wait_ge(s_silu, i * 2 + s + 1)
                        step(nc.vector.tensor_tensor(g[:, s, :], g[:, s, :], v[:, s, :], ALU.mult))
                        step(nc.vector.tensor_reduce(gh[:, gs], g[:, s, :], AX.X, ALU.max, apply_absolute_value=True))
                        step(nc.vector.tensor_scalar(gh[:, gs], gh[:, gs], 1e-5, None, ALU.max))
                        step(nc.vector.reciprocal(rgh[:, gs], gh[:, gs]))
                        dve.wait_ge(s_x, i * 2 + s)
                        step(nc.vector.tensor_scalar(osc[:, gs], gh[:, gs], gamma[:, 2:3], 1.0 / 127.0,
                                                     ALU.mult, ALU.mult))
                        nc.vector.tensor_scalar(hsc[:, gs], rgh[:, gs], 127.0, None, ALU.mult).then_inc(s_scale, 1)
                        dve.wait_ge(s_y, i * 2 + s + 1)
                        add_y(i, s)


def cur_scale(scales, i, s):
    return scales[:, bass.ds(i * 2 + s, 1)]


def l1_attn(k):
    nc, x, xnT, ps = k.nc, k.x, k.xnT, k.ps
    H, NF = 16, 9
    F = 2 * H * NF
    CH = [(0, P), (P, 2 * P), (2 * P, F)]
    with Stage(k, "L1a") as st:
        img = st.sb("weights", [P, k.width["L1a"]])
        w = sbuf_views(img, *k.parts["L1a"])
        wq, wkv, woT, fwd, inv = (w[n].rearrange("p (k n) -> p k n", k=KC) for n in ("wq", "wkv", "woT", "fwd", "inv"))
        wf = st.sb("wf", [P, KC, 2, F])
        gw = st.sb("gw", [P, 3, C])
        spec = st.sb("spec", [P, NB, 2, F])
        sq = st.sb("squares", [P, 2, 2, F])
        ss = st.sb("square_sums", [P, NB, 2, H])
        rn = st.sb("rnorm", [P, NB, 2, H])
        t1 = st.sb("t1", [P, 2, 2, F // 2])
        t2 = st.sb("t2", [P, 2, 2, F // 2])
        pr = st.sb("product", [P, 2, F])
        prT = st.sb("productT", [P, 2, 3, P])
        s_w, s_wf, s_wfc = st.sem("w_loaded"), st.sem("wf_psum"), st.sem("wf_ready")
        s_sp, s_spc, s_sq, s_ss = st.sem("spec_psum"), st.sem("spec_ready"), st.sem("squared"), st.sem("sums_ready")
        s_inv, s_rn, s_n, s_cum = st.sem("inverse"), st.sem("rnorm_ready"), st.sem("normed"), st.sem("cum_psum")
        s_cread, s_pr, s_prT, s_prTc = st.sem("cum_read"), st.sem("product_ready"), st.sem("prT_psum"), st.sem("prT_ready")
        s_y, s_x, s_dve = st.sem("y_psum"), st.sem("x_added"), st.sem("dve_step")
        with nc.Block() as block:

            @block.sync
            def _(sp):
                sp.dma_start(img[:, :], k.dram["L1a"]).then_inc(s_w, 16)

            @block.tensor
            def _(pe):
                pe.wait_ge(s_w, 16)
                for m, wm in enumerate((wq, wkv)):
                    for c in range(KC):
                        for ko in range(KC):
                            mm = nc.tensor.matmul(ps[2 * m + c][:, 0:F], wm[:, ko, c * P:(c + 1) * P], fwd[:, ko, :],
                                                  start=(ko == 0), stop=(ko == KC - 1))
                        mm.then_inc(s_wf, 1)
                for n, (f0, f1) in enumerate(CH):
                    for kv in range(KC):
                        mm = nc.tensor.matmul(ps[4 + n][0:f1 - f0, 0:C], inv[:, kv, f0:f1], woT[:, kv, :],
                                              start=(kv == 0), stop=(kv == KC - 1))
                    mm.then_inc(s_wf, 1)
                pe.wait_ge(s_wfc, 7)
                for b in range(NB):
                    for m in range(2):
                        if b >= 2:
                            pe.wait_ge(s_spc, 2 * (b - 2) + m + 1)
                        for kc in range(KC):
                            mm = nc.tensor.matmul(ps[2 * (b % 2) + m][:, 0:F], xnT[:, kc, b * P:(b + 1) * P],
                                                  wf[:, kc, m, :], start=(kc == 0), stop=(kc == KC - 1))
                        mm.then_inc(s_sp, 1)

                def cumulate(b):
                    pe.wait_ge(s_n, b + 1)
                    if b >= 2:
                        pe.wait_ge(s_cread, b - 1)
                    nc.tensor.matmul(ps[4 + b % 2][:, 0:F], k.c["triu"], spec[:, b, 1, :], start=True,
                                     stop=True).then_inc(s_cum, 1)

                def turn(b):
                    pe.wait_ge(s_pr, b + 1)
                    if b >= 2:
                        pe.wait_ge(s_prTc, b - 1)
                    for n, (f0, f1) in enumerate(CH):
                        mm = nc.tensor.transpose(ps[6 + b % 2][0:f1 - f0, n * P:(n + 1) * P], pr[:, b % 2, f0:f1],
                                                 k.ident)
                    mm.then_inc(s_prT, 1)

                def out(b):
                    pe.wait_ge(s_prTc, b + 1)
                    if b >= 2:
                        pe.wait_ge(s_x, b - 1)
                    for n, (f0, f1) in enumerate(CH):
                        mm = nc.tensor.matmul(ps[b % 2][:, 0:C], prT[0:f1 - f0, b % 2, n, :], gw[0:f1 - f0, n, :],
                                              start=(n == 0), stop=(n == 2))
                    mm.then_inc(s_y, 1)

                pe.wait_ge(s_spc, 2 * NB)
                pe.wait_ge(s_sq, 2 * NB)
                for b in range(NB + 2):
                    if b < NB:
                        cumulate(b)
                    if 1 <= b <= NB:
                        turn(b - 1)
                    if b >= 2:
                        out(b - 2)

            @block.scalar
            def _(act):
                for n in range(4):
                    act.wait_ge(s_wf, n + 1)
                    nc.scalar.activation(wf[:, n % 2, n // 2, :], ps[n][:, 0:F], ACT.Copy).then_inc(s_wfc, 1)
                for n, (f0, f1) in enumerate(CH):
                    act.wait_ge(s_wf, 4 + n + 1)
                    nc.scalar.activation(gw[0:f1 - f0, n, :], ps[4 + n][0:f1 - f0, 0:C], ACT.Copy).then_inc(s_wfc, 1)
                for b in range(NB):
                    for m in range(2):
                        act.wait_ge(s_spc, 2 * b + m + 1)
                        if b >= 2:
                            act.wait_ge(s_ss, 2 * (b - 2) + m + 1)
                        nc.scalar.activation(sq[:, b % 2, m, :], spec[:, b, m, :], ACT.Square).then_inc(s_sq, 1)
                act.wait_ge(s_inv, 1)
                nc.scalar.activation(rn[:, :, :, :], ss[:, :, :, :], ACT.Sqrt).then_inc(s_rn, 1)
                for b in range(NB):
                    act.wait_ge(s_prT, b + 1)
                    if b >= 2:
                        act.wait_ge(s_y, b - 1)
                    nc.scalar.activation(prT[:, b % 2, 0:2, :], ps[6 + b % 2][:, 0:2 * P].rearrange(
                        "p (n t) -> p n t", n=2), ACT.Copy)
                    nc.scalar.activation(prT[0:F - 2 * P, b % 2, 2, :], ps[6 + b % 2][0:F - 2 * P, 2 * P:3 * P],
                                         ACT.Copy).then_inc(s_prTc, 1)

            @block.vector
            def _(dve):
                step = Chain(dve, s_dve)
                for b in range(NB):
                    for m in range(2):
                        dve.wait_ge(s_sp, 2 * b + m + 1)
                        nc.vector.tensor_copy(spec[:, b, m, :], ps[2 * (b % 2) + m][:, 0:F]).then_inc(s_spc, 1)
                        dve.wait_ge(s_sq, 2 * b + m + 1)
                        nc.vector.tensor_reduce(ss[:, b, m, :], sq[:, b % 2, m, :].rearrange(
                            "p (r h f) -> p h r f", r=2, h=H), AX.XY, ALU.add).then_inc(s_ss, 1)
                dve.wait_ge(s_ss, 2 * NB)
                dve.wait_ge(s_spc, 2 * NB)
                nc.vector.reciprocal(ss[:, :, :, :], ss[:, :, :, :]).then_inc(s_inv, 1)
                dve.wait_ge(s_rn, 1)

                def normalise(b):
                    for m in (1, 0):
                        s3 = spec[:, b, m, :].rearrange("p (r h f) -> p r h f", r=2, h=H)
                        ins = nc.vector.tensor_tensor(s3, s3, over(along(rn[:, b, m, :], NF), 2), ALU.mult)
                    ins.then_inc(s_n, 1)

                def add(b):
                    dve.wait_ge(s_y, b + 1)
                    nc.vector.tensor_tensor(x[:, b, :], x[:, b, :], ps[b % 2][:, 0:C], ALU.add).then_inc(s_x, 1)

                normalise(0)
                for b in range(NB):
                    if b + 1 < NB:
                        normalise(b + 1)
                    q = spec[:, b, 0, :].rearrange("p (r f) -> p r f", r=2)
                    c = ps[4 + b % 2][:, 0:F].rearrange("p (r f) -> p r f", r=2)
                    a1, a2, z = t1[:, b % 2, :, :], t2[:, b % 2, :, :], pr[:, b % 2, :].rearrange("p (r f) -> p r f", r=2)
                    dve.wait_ge(s_n, b + 1)
                    dve.wait_ge(s_cum, b + 1)
                    nc.vector.tensor_tensor(a1, q, c, ALU.mult)
                    nc.vector.tensor_tensor(a2[:, 0, :], q[:, 0, :], c[:, 1, :], ALU.mult)
                    nc.vector.tensor_tensor(a2[:, 1, :], q[:, 1, :], c[:, 0, :], ALU.mult).then_inc(s_cread, 1)
                    dve.wait_ge(s_cread, b + 1)
                    if b >= 2:
                        dve.wait_ge(s_prT, b - 1)
                    nc.vector.tensor_tensor(z[:, 0, :], a1[:, 0, :], a1[:, 1, :], ALU.subtract)
                    nc.vector.tensor_tensor(z[:, 1, :], a2[:, 0, :], a2[:, 1, :], ALU.add).then_inc(s_pr, 1)
                    if b >= 2:
                        add(b - 2)
                add(NB - 2)
                add(NB - 1)


def l1_xattn(k):
    nc, x, xnT, ctxT, ps = k.nc, k.x, k.xnT, k.ctxT, k.ps
    H = 16
    SCALE = P ** -0.5
    uses = [("q", 0), ("q", 1), ("k", 0), ("k", 1), ("n", 0), ("v", 0), ("v", 1), ("kt", 0), ("kt", 1),
            ("s", 0), ("s", 1), ("t", 0), ("t", 1), ("o", 0), ("o", 1), (None, 0)]
    with Stage(k, "L1x") as st:
        s_qread, s_kread, s_vread = st.sem("q_read"), st.sem("k_read"), st.sem("v_read")
        s_nread, s_ktread = st.sem("norms_read"), st.sem("kT_read")
        a = WideHeads(k, st, None)
        tr = a.turns = Turns(k, uses, {"q": s_qread, "k": s_kread, "v": s_vread, "n": s_nread, "kt": s_ktread,
                                       "s": a.s_exp, "t": a.s_pT, "o": a.s_oT})
        slot = [st.sb(f"head{s}", [P, 2 * P + 2 * P + C]) for s in range(2)]
        gg = st.sb("gains", [P, 2])
        gain = st.sb("gain", [P, 1])
        sq = st.sb("q_squares", [P, TOK])
        ksq = st.sb("k_squares", [P, TOK])
        kn = st.sb("k_normed", [P, TOK])
        ss = st.sb("square_sums", [P, 2, NB])
        rn = st.sb("rnorm", [P, 2, NB])
        tmp = st.sb("newton", [P, 2, NB])
        qs = st.sb("q_scale", [P, NB])
        s_g, s_load, s_gain = st.sem("gains_loaded"), [st.sem(f"head_loaded{s}") for s in range(2)], st.sem("gain_ready")
        s_q, s_kp, s_v, s_n, s_ktp = (st.sem(n) for n in ("q_psum", "k_psum", "v_psum", "norms_psum", "kT_psum"))
        s_sq, s_ksq, s_kn, s_dve = (st.sem(n) for n in ("q_squared", "k_squared", "k_normed", "dve_step"))

        def run(eng, body):
            for s in range(2):
                body(eng, s, s, 0)
            with eng.Fori(1, H // 2) as i:
                for s in range(2):
                    body(eng, i * 2 + s, s, i)

        with nc.Block() as block:

            @block.sync
            def _(sp):
                sp.dma_start(gg[:, :], k.dram["L1n"]).then_inc(s_g, 16)

                def head(sp, j, s, i):
                    if not isinstance(j, int):
                        sp.wait_ge(a.s_y, j * 2 - 2)
                        src = k.dram["L1x"][bass.ds(j, 1), :, :].rearrange("a p n -> (a p) n")
                    else:
                        src = k.dram["L1x"][j]
                    sp.dma_start(slot[s][:, :], src).then_inc(s_load[s], 16)

                run(sp, head)

            @block.tensor
            def _(pe):
                a.clear_sums(pe)

                def head(pe, j, s, i):
                    w = slot[s]
                    wq = w[:, 0:2 * P].rearrange("p (k n) -> p k n", k=KC)
                    wk, wv, wo = w[:, 2 * P:3 * P], w[:, 3 * P:4 * P], w[:, 4 * P:]
                    pe.wait_ge(s_load[s], i * 16 + 16)
                    for h in range(2):
                        tr.free(pe, j, ("q", h))
                        for kc in range(KC):
                            mm = nc.tensor.matmul(tr.bank(("q", h))[:, :], wq[:, kc, :],
                                                  xnT[:, kc, h * HALF:(h + 1) * HALF],
                                                  start=(kc == 0), stop=(kc == KC - 1))
                        mm.then_inc(s_q, 1)
                    def row_form(name, wm, sem):
                        for h in range(2):
                            tr.free(pe, j, (name, h))
                            for b in range(4):
                                g = 4 * h + b
                                mm = nc.tensor.matmul(tr.bank((name, h))[:, b * P:(b + 1) * P],
                                                      ctxT[:, g * P:(g + 1) * P], wm, start=True, stop=True)
                            mm.then_inc(sem, 1)

                    row_form("k", wk, s_kp)
                    tr.free(pe, j, ("n", 0))
                    pe.wait_ge(s_sq, j * 2 + 2)
                    for b in range(NB):
                        mm = nc.tensor.matmul(tr.bank(("n", 0))[:, b:b + 1], sq[:, b * P:(b + 1) * P],
                                              k.c["ones"][:, 0:1], start=True, stop=True)
                    mm.then_inc(s_n, 1)
                    row_form("v", wv, s_v)
                    for h in range(2):
                        tr.free(pe, j, ("kt", h))
                        pe.wait_ge(s_kn, j * 2 + h + 1)
                        for b in range(4):
                            g = 4 * h + b
                            mm = nc.tensor.transpose(tr.bank(("kt", h))[:, b * P:(b + 1) * P],
                                                     kn[:, g * P:(g + 1) * P], k.ident)
                        mm.then_inc(s_ktp, 1)
                    pe.wait_ge(s_ktread, j * 2 + 2)
                    pe.wait_ge(s_qread, j * 2 + 2)
                    pe.wait_ge(s_vread, j * 2 + 2)
                    a.pe(pe, j, j, "", wo)

                run(pe, head)

            @block.scalar
            def _(act):
                act.wait_ge(s_gain, 1)

                def head(act, j, s, i):
                    for h in range(2):
                        t = slice(h * HALF, (h + 1) * HALF)
                        act.wait_ge(s_q, j * 2 + h + 1)
                        if not isinstance(j, int) or j:
                            act.wait_ge(a.s_s, j * 2)
                            act.wait_ge(s_n, j)
                        nc.scalar.activation(sq[:, t], tr.bank(("q", h))[:, :], ACT.Square).then_inc(s_sq, 1)
                        nc.scalar.activation(a.qT[:, t], tr.bank(("q", h))[:, :], ACT.Copy).then_inc(s_qread, 1)
                    for h in range(2):
                        act.wait_ge(s_kp, j * 2 + h + 1)
                        nc.scalar.activation(ksq[:, h * HALF:(h + 1) * HALF], tr.bank(("k", h))[:, :],
                                             ACT.Square).then_inc(s_ksq, 1)
                    for h in range(2):
                        act.wait_ge(s_ktp, j * 2 + h + 1)
                        nc.scalar.activation(a.kT[:, h * HALF:(h + 1) * HALF], tr.bank(("kt", h))[:, :], ACT.Copy,
                                             scale=gain[:, 0:1]).then_inc(s_ktread, 1)
                    a.act(act, j, j, "", lambda b: qs[:, b:b + 1])

                run(act, head)

            @block.vector
            def _(dve):
                step = Chain(dve, s_dve)
                nc.vector.memset(a.zero[:, :], 0.0).then_inc(a.s_zero, 1)
                dve.wait_ge(s_g, 16)
                nc.vector.tensor_tensor(gain[:, :], gg[:, 0:1], gg[:, 1:2], ALU.mult).then_inc(s_gain, 1)

                def head(dve, j, s, i):
                    step.restart()
                    for h in range(2):
                        dve.wait_ge(s_ksq, j * 2 + h + 1)
                        step(nc.vector.tensor_reduce(ss[:, 1, 4 * h:4 * h + 4], ksq[:, h * HALF:(h + 1) * HALF].rearrange(
                            "p (b t) -> p b t", b=4), AX.X, ALU.add))
                    dve.wait_ge(s_n, j + 1)
                    nc.vector.tensor_copy(ss[:, 0, :], tr.bank(("n", 0))[:, 0:NB]).then_inc(s_nread, 1)
                    dve.wait_ge(s_nread, j + 1)
                    step(nc.vector.tensor_scalar(ss[:, :, :], ss[:, :, :], 1.0 / P, 1e-5, ALU.mult, ALU.add))
                    rsqrt(nc, step, ss[:, :, :], rn[:, :, :], tmp[:, :, :])
                    for h in range(2):
                        t = slice(h * HALF, (h + 1) * HALF)
                        nc.vector.tensor_tensor(kn[:, t].rearrange("p (b t) -> p b t", b=4),
                                                tr.bank(("k", h))[:, :].rearrange("p (b t) -> p b t", b=4),
                                                along(rn[:, 1, 4 * h:4 * h + 4], P), ALU.mult).then_inc(s_kn, 1)
                        dve.wait_ge(s_kn, j * 2 + h + 1)
                        dve.sem_inc(s_kread, 1)
                    dve.wait_ge(s_v, j * 2 + 1)
                    if not isinstance(j, int) or j:
                        dve.wait_ge(a.s_oTp, j * 2)
                    nc.vector.tensor_copy(a.v[:, 0:HALF], tr.bank(("v", 0))[:, :]).then_inc(s_vread, 1)
                    dve.wait_ge(s_v, j * 2 + 2)
                    nc.vector.tensor_copy(a.v[:, HALF:TOK], tr.bank(("v", 1))[:, :]).then_inc(s_vread, 1)
                    step(nc.vector.tensor_scalar(qs[:, :], rn[:, 0, :], SCALE, None, ALU.mult))
                    for h in range(2):
                        dve.wait_ge(a.s_s, j * 2 + h + 1)
                        step(nc.vector.tensor_reduce(a.mx[:, h, :], tr.bank(("s", h))[:, :].rearrange(
                            "p (b t) -> p b t", b=4), AX.X, ALU.max))
                        nc.vector.scalar_tensor_tensor(a.nb[:, h, :], a.mx[:, h, :], -1.0, qs[:, 4 * h:4 * h + 4],
                                                       ALU.mult, ALU.mult).then_inc(a.s_nb, 1)
                    for h in range(2):
                        a.dve_probs(dve, step, j, h)
                    for h in range(2):
                        a.dve_turned(dve, j, "", h)

                run(dve, head)
                dve.wait_ge(a.s_y, 2 * H)
                a.add(dve)


def l1_ffn(k):
    nc, x, xnT, ps = k.nc, k.x, k.xnT, k.ps
    E, NI = 8, 4
    I = NI * P
    with Stage(k, "L1f") as st:
        gate_w = st.sb("gate_w", [P, KC, E])
        slot = [st.sb(f"expert{s}", [P, 2 * KC * I + NI * C]) for s in range(2)]
        w1 = [t[:, 0:KC * I].rearrange("p (k n) -> p k n", k=KC) for t in slot]
        w3 = [t[:, KC * I:2 * KC * I].rearrange("p (k n) -> p k n", k=KC) for t in slot]
        w2 = [t[:, 2 * KC * I:].rearrange("p (k n) -> p k n", k=NI) for t in slot]
        weights = st.sb("weights", [P, NB, E])
        mine = st.sb("mine", [P, 2, NB])
        silu = st.sb("silu", [P, 2, HALF])
        hT = st.sb("hT", [P, 2, NI, HALF])
        r = Router(k, st, E, ps[7])
        s_gw, s_load = st.sem("gate_loaded"), [st.sem(f"expert_loaded{s}") for s in range(2)]
        s_h, s_silu, s_hT = st.sem("h_in_psum"), st.sem("silu_ready"), st.sem("hT_ready")
        s_y, s_acc, s_mine = st.sem("y_in_psum"), st.sem("y_added"), st.sem("mine_ready")
        s_tanh, s_dve = st.sem("tanh_ready"), st.sem("dve_step")
        U = 2 * NI
        with nc.Block() as block:

            @block.sync
            def _(sp):
                sp.dma_start(gate_w[:, :, :], k.dram["L1g"].rearrange("p (k n) -> p k n", k=KC)).then_inc(s_gw, 16)
                for s in range(2):
                    sp.dma_start(slot[s][:, :], k.dram["L1f"][s]).then_inc(s_load[s], 16)
                with sp.Fori(1, E // 2) as i:
                    for s in range(2):
                        sp.wait_ge(s_y, (i - 1) * 8 + 4 * s + 4)
                        sp.dma_start(slot[s][:, :], k.dram["L1f"][bass.ds(i * 2 + s, 1), :, :].rearrange(
                            "a p n -> (a p) n")).then_inc(s_load[s], 16)

            @block.tensor
            def _(pe):
                pe.wait_ge(s_gw, 16)
                r.matmuls(gate_w)
                with pe.Fori(0, E // 2) as i:
                    for s in range(2):
                        pe.wait_ge(s_load[s], i * 16 + 16)

                        def hidden(u):
                            h, n = u // NI, u % NI
                            done = i * (2 * U) + s * U + u
                            if s == 0 and u < 2:
                                pe.wait_ge(s_hT, i * (2 * U) + max(u - 1, 0) if u else i * (2 * U))
                            else:
                                pe.wait_ge(s_hT, done - 1)
                            for w, bank in ((w1, 0), (w3, 1)):
                                for kc in range(KC):
                                    mm = nc.tensor.matmul(ps[2 * (u % 2) + bank][:, :],
                                                          w[s][:, kc, n * P:(n + 1) * P],
                                                          xnT[:, kc, h * HALF:(h + 1) * HALF],
                                                          start=(kc == 0), stop=(kc == KC - 1))
                            mm.then_inc(s_h, 1)

                        def output(h):
                            pe.wait_ge(s_hT, i * (2 * U) + s * U + (h + 1) * NI)
                            for pair in range(2):
                                if s or h:
                                    pe.wait_ge(s_acc, i * 8 + s * 4 + h * 2 + pair - 1)
                                else:
                                    pe.wait_ge(s_acc, i * 8 + pair)
                                for j in range(2):
                                    t = pair * 2 + j
                                    for n in range(NI):
                                        mm = nc.tensor.matmul(ps[4 + pair][:, j * C:(j + 1) * C],
                                                              hT[:, h, n, t * P:(t + 1) * P], w2[s][:, n, :],
                                                              start=(n == 0), stop=(n == NI - 1))
                                mm.then_inc(s_y, 1)

                        for u in range(NI + 1):
                            hidden(u)
                        output(0)
                        for u in range(NI + 1, U):
                            hidden(u)
                        output(1)

            @block.scalar
            def _(act):
                act.wait_ge(r.s_logits, 1)
                nc.scalar.activation(r.z[:, :, :], r.logits, ACT.Tanh, scale=1.0 / 30.0).then_inc(s_tanh, 1)
                r.exponent(act, scale=30.0)
                with act.Fori(0, E // 2) as i:
                    for v in range(2 * U):
                        act.wait_ge(s_h, i * (2 * U) + v + 1)
                        if v >= 2:
                            act.wait_ge(s_hT, i * (2 * U) + v - 1)
                        nc.scalar.activation(silu[:, v % 2, :], ps[2 * (v % 2)][:, :], ACT.Silu).then_inc(s_silu, 1)

            @block.vector
            def _(dve):
                step = Chain(dve, s_dve)
                dve.wait_ge(s_tanh, 1)
                r.softmax(dve, step)
                r.top_two(step)
                r.masked(step, weights[:, :, :])
                with dve.Fori(0, E // 2) as i:
                    for s in range(2):
                        nc.vector.tensor_copy(mine[:, s, :], weights[:, :, bass.ds(i * 2 + s, 1)].rearrange(
                            "p b e -> p (b e)")).then_inc(s_mine, 1)

                        def hidden(u):
                            h, n = u // NI, u % NI
                            dve.wait_ge(s_silu, i * (2 * U) + s * U + u + 1)
                            if s or h:
                                dve.wait_ge(s_y, i * 8 + s * 4 + h * 2 - 2)
                            else:
                                dve.wait_ge(s_y, i * 8)
                            nc.vector.tensor_tensor(hT[:, h, n, :], silu[:, u % 2, :],
                                                    ps[2 * (u % 2) + 1][:, :], ALU.mult).then_inc(s_hT, 1)

                        def output(h):
                            for pair in range(2):
                                dve.wait_ge(s_y, i * 8 + s * 4 + h * 2 + pair + 1)
                                for j in range(2):
                                    b = 4 * h + 2 * pair + j
                                    ins = nc.vector.scalar_tensor_tensor(
                                        x[:, b, :], ps[4 + pair][:, j * C:(j + 1) * C], mine[:, s, b:b + 1],
                                        x[:, b, :], ALU.mult, ALU.add)
                                ins.then_inc(s_acc, 1)

                        for u in range(NI + 1):
                            hidden(u)
                        dve.wait_ge(s_mine, i * 2 + s + 1)
                        output(0)
                        for u in range(NI + 1, U):
                            hidden(u)
                        output(1)


def l2_attn(k):
    nc, x, xnT, ps = k.nc, k.x, k.xnT, k.ps
    with Stage(k, "L2a") as st:
        img = st.sb("weights", [P, k.width["L2a"]])
        w = sbuf_views(img, *k.parts["L2a"])
        w_qkv = w["w_qkv"].rearrange("p (k n) -> p k n", k=KC)
        w_out = w["w_out"].rearrange("p (k n) -> p k n", k=KC)
        decay = w["decay"]
        head_ones = k.c["head_ones16"]
        ed = st.sb("ed", [P, KC])
        dsum = st.sb("dsum", [P, KC])
        dec = st.sb("dec", [P, KC])
        decays = st.sb("decays", [P, KC, TOK])
        neg = st.sb("neg", [P, 2, 2 * HALF])
        expd = st.sb("expd", [P, 2, 2 * HALF])
        q = st.sb("q", [P, KC, TOK])
        kk = st.sb("kk", [P, KC, TOK])
        kv = st.sb("kv", [P, KC, TOK])
        ksum = st.sb("ksum", [P, KC, TOK])
        kvsum = st.sb("kvsum", [P, KC, TOK])
        s_w, s_qkv, s_neg, s_exp = st.sem("w_loaded"), st.sem("qkv_ready"), st.sem("neg_ready"), st.sem("exp_ready")
        s_free, s_ed, s_qks, s_den = st.sem("qkv_used"), st.sem("exp_decay"), st.sem("qks_ready"), st.sem("den_ready")
        s_o, s_y, s_dve = st.sem("o_ready"), st.sem("y_ready"), st.sem("dve_step")
        with nc.Block() as block:

            @block.sync
            def _(sp):
                sp.dma_start(img[:, :], k.dram["L2a"]).then_inc(s_w, 16)

            @block.tensor
            def _(pe):
                pe.wait_ge(s_w, 16)
                for u in range(4):
                    c, h = u // 2, u % 2
                    if u >= 2:
                        pe.wait_ge(s_free, u - 1)
                    for n, part in enumerate((1, 2, 0)):
                        col = part * C + c * P
                        for kc in range(KC):
                            mm = nc.tensor.matmul(ps[3 * (u % 2) + n][:, :], w_qkv[:, kc, col:col + P],
                                                  xnT[:, kc, h * HALF:(h + 1) * HALF],
                                                  start=(kc == 0), stop=(kc == KC - 1))
                    mm.then_inc(s_qkv, 1)
                for u in range(4):
                    c, h = u // 2, u % 2
                    pe.wait_ge(s_qks, u + 1)
                    if u == 2:
                        pe.wait_ge(s_o, 2)
                    nc.tensor.matmul(ps[6 + h][:, :], head_ones, kk[:, c, h * HALF:(h + 1) * HALF],
                                     start=True, stop=True).then_inc(s_den, 1)
                pe.wait_ge(s_o, 4)
                for b in range(NB):
                    for kc in range(KC):
                        mm = nc.tensor.matmul(ps[b // 2][:, (b % 2) * C:(b % 2 + 1) * C],
                                              q[:, kc, b * P:(b + 1) * P], w_out[:, kc, :],
                                              start=(kc == 0), stop=(kc == KC - 1))
                    if b % 2:
                        mm.then_inc(s_y, 1)

            @block.scalar
            def _(act):
                act.wait_ge(s_w, 16)
                nc.scalar.activation(ed[:, :], decay, ACT.Exp, scale=-1.0).then_inc(s_ed, 1)
                for u in range(4):
                    act.wait_ge(s_neg, 2 * (u + 1))
                    nc.scalar.activation(expd[:, u % 2, :], neg[:, u % 2, :], ACT.Exp).then_inc(s_exp, 1)

            @block.vector
            def _(dve):
                step = Chain(dve, s_dve)
                dve.wait_ge(s_ed, 1)
                step(nc.vector.tensor_scalar(dsum[:, :], ed[:, :], 1.0, None, ALU.add))
                step(nc.vector.reciprocal(dec[:, :], dsum[:, :]))
                step(nc.vector.memset(decays[:, :, :], 1.0))
                for c in range(KC):
                    step(nc.vector.tensor_scalar(decays[:, c, :], decays[:, c, :], dec[:, c:c + 1], None, ALU.mult))
                    step(nc.vector.memset(decays[:, c, 0:TOK:P], 0.0))

                def minus(u):
                    dve.wait_ge(s_qkv, u + 1)
                    if u >= 2:
                        dve.wait_ge(s_exp, u - 1)
                    nc.vector.tensor_scalar(neg[:, u % 2, 0:HALF], ps[3 * (u % 2)][:, :], 0.0, None,
                                            ALU.min).then_inc(s_neg, 1)
                    nc.vector.tensor_scalar(neg[:, u % 2, HALF:], ps[3 * (u % 2) + 2][:, :], 0.0, None,
                                            ALU.min).then_inc(s_neg, 1)

                minus(0)
                for u in range(4):
                    c, h = u // 2, u % 2
                    t = slice(h * HALF, (h + 1) * HALF)
                    if u < 3:
                        minus(u + 1)
                    dve.wait_ge(s_exp, u + 1)
                    step(nc.vector.scalar_tensor_tensor(kk[:, c, t], ps[3 * (u % 2)][:, :], 0.0,
                                                        expd[:, u % 2, 0:HALF], ALU.max, ALU.add))
                    step(nc.vector.tensor_tensor(kv[:, c, t], kk[:, c, t], ps[3 * (u % 2) + 1][:, :], ALU.mult))
                    nc.vector.scalar_tensor_tensor(q[:, c, t], ps[3 * (u % 2) + 2][:, :], 0.0,
                                                   expd[:, u % 2, HALF:], ALU.max, ALU.add).then_inc(s_free, 1)
                    if h == 1:
                        dve.wait_ge(s_free, u + 1)
                        step(nc.vector.tensor_tensor_scan(ksum[:, c, :], decays[:, c, :], kk[:, c, :], 0.0,
                                                          ALU.mult, ALU.add))
                        step(nc.vector.tensor_tensor_scan(kvsum[:, c, :], decays[:, c, :], kv[:, c, :], 0.0,
                                                          ALU.mult, ALU.add))
                        for hh in range(2):
                            tt = slice(hh * HALF, (hh + 1) * HALF)
                            nc.vector.tensor_tensor(kk[:, c, tt], q[:, c, tt], ksum[:, c, tt],
                                                    ALU.mult).then_inc(s_qks, 1)
                for u in range(4):
                    c, h = u // 2, u % 2
                    t = slice(h * HALF, (h + 1) * HALF)
                    dve.wait_ge(s_den, u + 1)
                    step(nc.vector.tensor_scalar(ksum[:, c, t], ps[6 + h][:, :], 1e-6, None, ALU.max))
                    step(nc.vector.reciprocal(ksum[:, c, t], ksum[:, c, t]))
                    step(nc.vector.tensor_tensor(kvsum[:, c, t], kvsum[:, c, t], ksum[:, c, t], ALU.mult))
                    nc.vector.tensor_tensor(q[:, c, t], q[:, c, t], kvsum[:, c, t], ALU.mult).then_inc(s_o, 1)
                for n in range(NB // 2):
                    dve.wait_ge(s_y, n + 1)
                    nc.vector.tensor_tensor(x[:, 2 * n:2 * n + 2, :], x[:, 2 * n:2 * n + 2, :],
                                            ps[n][:, :].rearrange("p (b n) -> p b n", b=2),
                                            ALU.add)


def l2_xattn(k):
    nc, x, xnT, ctxT, ps = k.nc, k.x, k.xnT, k.ctxT, k.ps
    H, hd, MAIN = 16, 16, P - 16
    with Stage(k, "L2x") as st:
        img = st.sb("weights", [P, k.width["L2x"]])
        w = sbuf_views(img, *k.parts["L2x"])
        wq, wo = (w[n].rearrange("p (k n) -> p k n", k=KC) for n in ("wq", "wo"))
        a = SmallHeads(k, st, H, hd, [(0, MAIN), (MAIN, P)], 1.0 / hd ** 0.5)
        a.w_out, a.in_head = wo, k.c["in_head16"]
        ctxm, ctxd = st.sb("ctx_main", [P, NB, P]), st.sb("ctx_dca", [P, NB, P])
        qk = st.sb("qk", [P, NB, 2 * C])
        sq = st.sb("squares", [P, 2, 2 * C])
        mean, var = st.sb("mean", [P, NB, 2 * H]), st.sb("var", [P, NB, 2 * H])
        rstd = st.sb("rstd", [P, NB, 2 * H])
        s_w, s_qk, s_v, s_ctx = st.sem("w_loaded"), st.sem("qk_psum"), st.sem("v_psum"), st.sem("ctx_split")
        s_read, s_cent, s_sq, s_var = st.sem("qk_read"), st.sem("centred"), st.sem("squares_ready"), st.sem("var_ready")
        s_rstd, s_ln, s_t, s_in = st.sem("rstd_ready"), st.sem("normed"), st.sem("qkT_psum"), st.sem("qkT_ready")
        s_vin, s_bias, s_sqread = st.sem("v_ready"), st.sem("bias_added"), st.sem("squares_read")
        with nc.Block() as block:

            @block.sync
            def _(sp):
                sp.dma_start(img[:, :], k.dram["L2x"]).then_inc(s_w, 16)

            @block.tensor
            def _(pe):
                pe.wait_ge(s_w, 16)
                pe.wait_ge(s_ctx, 4)
                for b in range(NB):
                    if b >= 2:
                        pe.wait_ge(s_read, b - 1)
                        pe.wait_ge(s_vin, b - 1)
                    bank, vb = ps[b % 2], ps[2 + b % 2]
                    for kc in range(KC):
                        nc.tensor.matmul(bank[:, 0:C], xnT[:, kc, b * P:(b + 1) * P], wq[:, kc, :],
                                         start=(kc == 0), stop=(kc == KC - 1))
                    nc.tensor.matmul(bank[:, C:2 * C], ctxm[:, b, :], w["wk"], start=True, stop=False)
                    nc.tensor.matmul(bank[:, C:2 * C], ctxd[:, b, :], w["wkd"], start=False,
                                     stop=True).then_inc(s_qk, 1)
                    nc.tensor.matmul(vb[:, 0:C], ctxm[:, b, :], w["wv"], start=True, stop=True)
                    nc.tensor.matmul(vb[:, C:2 * C], ctxd[:, b, :], w["wvd"], start=True, stop=True).then_inc(s_v, 1)
                for half in range(2):
                    for m in range(2):
                        for c in range(KC):
                            for j in range(4):
                                b = 4 * half + j
                                pe.wait_ge(s_ln, b + 1)
                                mm = nc.tensor.transpose(ps[4 + 2 * (m % 2) + c][:, j * P:(j + 1) * P],
                                                         qk[:, b, m * C + c * P:m * C + (c + 1) * P], k.ident)
                            mm.then_inc(s_t, 1)
                    if half == 0:
                        pe.wait_ge(s_in, 4)
                pe.wait_ge(s_in, 8)
                pe.wait_ge(s_vin, NB)
                a.run(pe, a.pe, a.pe_tail)

            @block.scalar
            def _(act):
                for b in range(NB):
                    act.wait_ge(s_cent, b + 1)
                    if b >= 2:
                        act.wait_ge(s_sqread, b - 1)
                    nc.scalar.activation(sq[:, b % 2, :], qk[:, b, :], ACT.Square).then_inc(s_sq, 1)
                act.wait_ge(s_var, 1)
                nc.scalar.activation(rstd[:, :, :], var[:, :, :], ACT.Sqrt).then_inc(s_rstd, 1)
                for half in range(2):
                    for m in range(2):
                        for c in range(KC):
                            act.wait_ge(s_t, 4 * half + 2 * m + c + 1)
                            bank = ps[4 + 2 * m + c][:, :].rearrange("p (b t) -> p b t", b=4)
                            dst = (a.kT if m else a.qT)[:, c, half * HALF:(half + 1) * HALF].rearrange(
                                "p (b t) -> p b t", b=4)
                            ranges = [(0, MAIN, 1), (MAIN, P, 2)] if m else [(0, P, 0)]
                            for t0, t1, n in ranges:
                                ins = nc.scalar.activation(dst[:, :, t0:t1], bank[:, :, t0:t1], ACT.Identity,
                                                           bias=w["nb"][:, n:n + 1], scale=w["nw"][:, n:n + 1])
                            ins.then_inc(s_in, 1)
                a.run(act, a.act, a.act_tail)

            @block.vector
            def _(dve):
                a.step = step = Chain(dve, a.s_step)
                dve.wait_ge(s_w, 16)
                for b in range(NB):
                    dve.wait_ge(s_qk, b + 1)
                    nc.vector.tensor_tensor(qk[:, b, :], ps[b % 2][:, :], w["bqk"], ALU.add).then_inc(s_read, 1)
                    dve.wait_ge(s_v, b + 1)
                    for m in range(2):
                        ins = nc.vector.tensor_tensor(
                            a.v[:, b, :, m * (hd + 1):m * (hd + 1) + hd],
                            ps[2 + b % 2][:, m * C:(m + 1) * C].rearrange("p (h d) -> p h d", h=H),
                            w["bvs"][:, m * C:(m + 1) * C].rearrange("p (h d) -> p h d", h=H), ALU.add)
                    ins.then_inc(s_vin, 1)
                    h3 = qk[:, b, :].rearrange("p (h d) -> p h d", d=hd)
                    dve.wait_ge(s_read, b + 1)
                    step(nc.vector.tensor_reduce(mean[:, b, :], h3, AX.X, ALU.add))
                    step(nc.vector.tensor_scalar(mean[:, b, :], mean[:, b, :], 1.0 / hd, None, ALU.mult))
                    nc.vector.tensor_tensor(h3, h3, along(mean[:, b, :], hd), ALU.subtract).then_inc(s_cent, 1)
                    if b:
                        dve.wait_ge(s_sq, b)
                        nc.vector.tensor_reduce(var[:, b - 1, :], sq[:, (b - 1) % 2, :].rearrange(
                            "p (h d) -> p h d", d=hd), AX.X, ALU.add).then_inc(s_sqread, 1)
                dve.wait_ge(s_sq, NB)
                step(nc.vector.tensor_reduce(var[:, NB - 1, :], sq[:, (NB - 1) % 2, :].rearrange(
                    "p (h d) -> p h d", d=hd), AX.X, ALU.add))
                dve.wait_ge(s_sqread, NB - 1)
                step(nc.vector.tensor_scalar(var[:, :, :], var[:, :, :], 1.0 / hd, 1e-6, ALU.mult, ALU.add))
                nc.vector.reciprocal(var[:, :, :], var[:, :, :]).then_inc(s_var, 1)
                dve.wait_ge(s_rstd, 1)
                for b in range(NB):
                    h3 = qk[:, b, :].rearrange("p (h d) -> p h d", d=hd)
                    nc.vector.tensor_tensor(h3, h3, along(rstd[:, b, :], hd), ALU.mult).then_inc(s_ln, 1)
                dve.wait_ge(s_bias, 3)
                a.run(dve, a.dve, a.dve_tail)

            @block.gpsimd
            def _(pool):
                ctx3 = ctxT[:, :].rearrange("p (b t) -> p b t", b=NB)
                nc.gpsimd.memset(ctxm[:, :, MAIN:P], 0.0).then_inc(s_ctx, 1)
                nc.gpsimd.memset(ctxd[:, :, 0:MAIN], 0.0).then_inc(s_ctx, 1)
                nc.gpsimd.tensor_copy(ctxm[:, :, 0:MAIN], ctx3[:, :, 0:MAIN]).then_inc(s_ctx, 1)
                nc.gpsimd.tensor_copy(ctxd[:, :, MAIN:P], ctx3[:, :, MAIN:P]).then_inc(s_ctx, 1)
                for m in range(2):
                    for b in range(NB):
                        ins = nc.gpsimd.tensor_copy(a.v[:, b, :, m * (hd + 1) + hd:(m + 1) * (hd + 1)],
                                                    over(k.c["key_parts"][:, m:m + 1], H))
                    ins.then_inc(s_bias, 1)
                pool.wait_ge(s_w, 16)
                nc.gpsimd.tensor_tensor(x[:, :, :], x[:, :, :], over(w["bo"], NB), ALU.add).then_inc(s_bias, 1)
                pool.wait_ge(s_in, 8)
                a.run(pool, a.pool, lambda eng: None)


def l2_ffn(k):
    nc, x, xnT, ps = k.nc, k.x, k.xnT, k.ps
    E, R = 6, 16
    A = R + E * R
    with Stage(k, "L2f") as st:
        img = st.sb("weights", [P, k.width["L2f"]])
        w = sbuf_views(img, *k.parts["L2f"])
        base, down, rout = (w[n].rearrange("p (k n) -> p k n", k=KC) for n in ("base", "down", "router"))
        up = w["up"][0:A, :]
        weights = st.sb("weights_e", [P, NB, E])
        h = st.sb("h", [P, NB, A])
        hT = st.sb("hT", [P, TOK])
        r = Router(k, st, E, ps[7])
        s_w, s_h, s_hw, s_hT, s_hTc = (st.sem(n) for n in ("w_loaded", "h_psum", "h_ready", "hT_psum", "hT_ready"))
        s_y, s_bias, s_dve = st.sem("y_psum"), st.sem("bias_added"), st.sem("dve_step")
        with nc.Block() as block:

            @block.sync
            def _(sp):
                sp.dma_start(img[:, :], k.dram["L2f"]).then_inc(s_w, 16)

            @block.gpsimd
            def _(pool):
                pool.wait_ge(s_w, 16)
                nc.gpsimd.tensor_tensor(x[:, :, :], x[:, :, :], over(w["b"], NB), ALU.add).then_inc(s_bias, 1)

            @block.tensor
            def _(pe):
                pe.wait_ge(s_w, 16)
                r.matmuls(rout)
                for b in range(NB):
                    for kc in range(KC):
                        mm = nc.tensor.matmul(ps[4 + b // 4][:, (b % 4) * A:(b % 4 + 1) * A],
                                              xnT[:, kc, b * P:(b + 1) * P], down[:, kc, :],
                                              start=(kc == 0), stop=(kc == KC - 1))
                    if b % 4 == 3:
                        mm.then_inc(s_h, 1)
                for half in range(2):
                    pe.wait_ge(s_hw, half + 1)
                    for b in range(4 * half, 4 * half + 4):
                        mm = nc.tensor.transpose(ps[4 + half][0:A, (b % 4) * P:(b % 4 + 1) * P], h[:, b, :], k.ident)
                    mm.then_inc(s_hT, 1)
                for b in range(NB):
                    pe.wait_ge(s_hTc, b // 4 + 1)
                    y = ps[b // 2][:, (b % 2) * C:(b % 2 + 1) * C]
                    for kc in range(KC):
                        nc.tensor.matmul(y, xnT[:, kc, b * P:(b + 1) * P], base[:, kc, :], start=(kc == 0), stop=False)
                    mm = nc.tensor.matmul(y, hT[0:A, b * P:(b + 1) * P], up, start=False, stop=True)
                    if b % 2:
                        mm.then_inc(s_y, 1)

            @block.scalar
            def _(act):
                r.exponent(act)
                for half in range(2):
                    act.wait_ge(s_hT, half + 1)
                    nc.scalar.activation(hT[0:A, half * HALF:(half + 1) * HALF], ps[4 + half][0:A, :],
                                         ACT.Copy).then_inc(s_hTc, 1)

            @block.vector
            def _(dve):
                step = Chain(dve, s_dve)
                dve.wait_ge(s_w, 16)
                dve.wait_ge(r.s_logits, 1)
                step(nc.vector.tensor_tensor(r.z[:, :, :], r.logits, over(w["b_router"], NB), ALU.add))
                r.softmax(dve, step)
                r.top_two(step)
                r.masked(step, weights[:, :, :])
                for half in range(2):
                    dve.wait_ge(s_h, half + 1)
                    hp = ps[4 + half][:, 0:4 * A].rearrange("p (b n) -> p b n", b=4)
                    bs = slice(4 * half, 4 * half + 4)
                    nc.vector.tensor_copy(h[:, bs, 0:R], hp[:, :, 0:R])
                    for b in range(4):
                        ins = nc.vector.tensor_tensor(
                            h[:, 4 * half + b, R:A].rearrange("p (e r) -> p e r", e=E),
                            hp[:, b, R:A].rearrange("p (e r) -> p e r", e=E),
                            along(weights[:, 4 * half + b, :], R), ALU.mult)
                    ins.then_inc(s_hw, 1)
                dve.wait_ge(s_bias, 1)
                for n in range(4):
                    dve.wait_ge(s_y, n + 1)
                    nc.vector.tensor_tensor(x[:, 2 * n:2 * n + 2, :], x[:, 2 * n:2 * n + 2, :],
                                            ps[n][:, :].rearrange("p (b n) -> p b n", b=2), ALU.add)


def l3_attn(k):
    nc, x, xnT, ps = k.nc, k.x, k.xnT, k.ps
    N, HD, NH, TAPS = 32, 64, 64, 4
    SLOT = 2 * KC * P + C + TAPS + 4
    triu, ones = k.c["triu"], k.c["ones"]
    with Stage(k, "L3a") as st:
        img = st.sb("weights", [P, k.width["L3a"]])
        w = sbuf_views(img, *k.parts["L3a"])
        wb, wc, wdt = (w[n].rearrange("p (k n) -> p k n", k=KC) for n in ("wb", "wc", "wdt"))
        slot = [st.sb(f"pair{s}", [P, SLOT]) for s in range(2)]
        wz = [t[:, 0:KC * P].rearrange("p (k n) -> p k n", k=KC) for t in slot]
        wx = [t[:, KC * P:2 * KC * P].rearrange("p (k n) -> p k n", k=KC) for t in slot]
        at = 2 * KC * P + C
        wo_raw = [t[:, 2 * KC * P:at] for t in slot]
        taps = [t[:, at:at + TAPS] for t in slot]
        cb = [t[:, at + TAPS:at + TAPS + 1] for t in slot]
        dcol = [t[:, at + TAPS + 1:at + TAPS + 2] for t in slot]
        nw = [t[:, at + TAPS + 2:at + TAPS + 3] for t in slot]
        zdt, az, dt, da = (st.sb(n, [P, NB, NH]) for n in ("z_dt", "abs_dt", "dt", "dA"))
        bT, cT = st.sb("bT", [P, TOK]), st.sb("cT", [P, TOK])
        cbm = st.sb("cb_masked", [P, NB, P])
        conv = st.sb("conv", [P, 2, NB, P])
        xT = st.sb("xT", [P, 2, TOK])
        sz = st.sb("silu_z", [P, 2, TOK])
        dac = st.sb("dA_pair", [P, 2, NB, 2])
        dtc = st.sb("dt_pair", [P, 2, NB, 2])
        wo = st.sb("wo", [P, 2, C])
        dcols = st.sb("d_pair", [P, 2, 1])
        rhs = st.sb("dA_steps", [P, 2 * NB, P])
        dec = st.sb("decays", [P, 2, NB, 2, P])
        dtx = st.sb("dtx", [P, 2, NB, 2, HD])
        yg = st.sb("y_gated", [P, 2, TOK])
        ysq = st.sb("y_squares", [P, TOK])
        sqsum = st.sb("square_sums", [P, TOK])
        zero = st.sb("zero", [P, P])
        ms, rms, tmp = (st.sb(n, [P, NB]) for n in ("mean_square", "rms", "newton"))
        S = {n: st.sem(n) for n in (
            "w_loaded", "dt_psum", "zdt", "abs_dt", "exp_dt", "exp1_dt", "log_dt", "bc_psum", "bc_first", "bc_conv",
            "bc_ready", "cb_psum", "cb_ready", "da_ready", "z_psum", "x_psum", "z_read", "x_scaled", "x_read",
            "x_conv", "x_ready", "xt_psum", "xt_read", "steps_ready", "diff_psum", "diff_read", "dec_ready",
            "y_psum", "y_read", "y_ready", "pair_small", "wo_ready", "out_done", "sq_ready", "sq_added",
            "ms_psum", "zero_set", "dve_step", "slot_read", "d_ready")}
        s_load = [st.sem(f"pair_loaded{s}") for s in range(2)]

        USES = [("x", 0), ("x", 1), ("z", 0), ("z", 1), ("y", 0), ("y", 1), ("d", 0), ("d", 1), ("d", 2), ("d", 3),
                ("t", 0), ("t", 1)]
        READ = {"x": "x_read", "z": "z_read", "y": "y_read", "d": "diff_read", "t": "xt_read"}
        COUNT = {"x": 2, "z": 2, "y": 2, "d": 4, "t": 2}

        def bank(name, n):
            return ps[4 + USES.index((name, n)) % 4]

        def free(pe, j, name, n):
            i = USES.index((name, n)) - 4
            passes = j
            if i < 0:
                i, passes = i + len(USES), j - 1
            name, n = USES[i]
            if name == "y":
                passes = passes - 1
                if isinstance(passes, int) and passes < 0:
                    name, n = USES[i - 4]
                    passes = passes + 1
            if isinstance(passes, int) and passes < 0:
                return
            pe.wait_ge(S[READ[name]], passes * COUNT[name] + n + 1)

        def conv_first(act, psum, dst, w3, bias):
            return nc.scalar.activation(dst, psum, ACT.Identity, bias=bias, scale=w3)

        def conv_tap(psum, dst, d, wcol):
            return nc.vector.scalar_tensor_tensor(dst[:, :, d:], psum[:, :, 0:P - d], wcol, dst[:, :, d:],
                                                  ALU.mult, ALU.add)

        def passes(eng, body, tail):
            body(eng, 0, 0, 0, False)
            body(eng, 1, 1, 0, True)
            with eng.Fori(1, N // 2) as i:
                for s in range(2):
                    body(eng, i * 2 + s, s, i, True)
            tail(eng)

        with nc.Block() as block:

            @block.sync
            def _(sp):
                sp.dma_start(img[:, :], k.dram["L3a"]).then_inc(S["w_loaded"], 16)

                def pair(sp, j, s, i, later):
                    if isinstance(j, int):
                        src = k.dram["L3p"][j]
                    else:
                        sp.wait_ge(S["slot_read"], j * 2 - 2)
                        src = k.dram["L3p"][bass.ds(j, 1), :, :].rearrange("a p n -> (a p) n")
                    sp.dma_start(slot[s][:, :], src).then_inc(s_load[s], 16)

                passes(sp, pair, lambda eng: None)

            @block.tensor
            def _(pe):
                pe.wait_ge(S["w_loaded"], 16)
                for b in range(NB):
                    for kc in range(KC):
                        mm = nc.tensor.matmul(ps[0][:, b * NH:(b + 1) * NH], xnT[:, kc, b * P:(b + 1) * P],
                                              wdt[:, kc, :], start=(kc == 0), stop=(kc == KC - 1))
                mm.then_inc(S["dt_psum"], 1)
                for m, wm in enumerate((wb, wc)):
                    for half in range(2):
                        for kc in range(KC):
                            mm = nc.tensor.matmul(ps[4 + 2 * m + half][:, :], wm[:, kc, :],
                                                  xnT[:, kc, half * HALF:(half + 1) * HALF],
                                                  start=(kc == 0), stop=(kc == KC - 1))
                        mm.then_inc(S["bc_psum"], 1)
                pe.wait_ge(S["bc_ready"], 2)
                pe.wait_ge(S["zdt"], 1)
                for b in range(NB):
                    mm = nc.tensor.matmul(ps[b // 4][:, (b % 4) * P:(b % 4 + 1) * P], bT[:, b * P:(b + 1) * P],
                                          cT[:, b * P:(b + 1) * P], start=True, stop=True)
                    if b % 4 == 3:
                        mm.then_inc(S["cb_psum"], 1)
                pe.wait_ge(S["cb_ready"], 2)
                pe.wait_ge(S["zero_set"], 2)
                for n in range(4):
                    nc.tensor.matmul(ps[n][:, :], zero[:, :], xnT[:, 0, 0:HALF], start=True, stop=False,
                                     skip_group_check=True)

                def make_y(pe, j, o):
                    pe.wait_ge(S["dec_ready"], j)
                    pe.wait_ge(S["xt_read"], j * 2)
                    for half in range(2):
                        if isinstance(j, int) and j == N:
                            pe.wait_ge(S["diff_read"], 4 * N)
                        else:
                            free(pe, j, "y", half)
                        for b in range(4):
                            g = 4 * half + b
                            for h in range(2):
                                mm = nc.tensor.matmul(
                                    bank("y", half)[h * HD:(h + 1) * HD, b * P:(b + 1) * P], dtx[:, o, g, h, :],
                                    dec[:, o, g, h, :], start=True, stop=True)
                        mm.then_inc(S["y_psum"], 1)

                def output(pe, j, o):
                    pe.wait_ge(S["wo_ready"], j)
                    for half in range(2):
                        pe.wait_ge(S["y_ready"], (j - 1) * 2 + half + 1)
                        for b in range(4):
                            g = 4 * half + b
                            mm = nc.tensor.matmul(ps[g // 2][:, (g % 2) * C:(g % 2 + 1) * C],
                                                  yg[:, o, g * P:(g + 1) * P], wo[:, o, :], start=False, stop=False,
                                                  skip_group_check=True)
                    mm.then_inc(S["out_done"], 1)

                def pair(pe, j, s, i, later):
                    pe.wait_ge(s_load[s], i * 16 + 16)
                    for name, wm, sem in (("x", wx[s], "x_psum"), ("z", wz[s], "z_psum")):
                        for half in range(2):
                            free(pe, j, name, half)
                            for kc in range(KC):
                                mm = nc.tensor.matmul(bank(name, half)[:, :], wm[:, kc, :],
                                                      xnT[:, kc, half * HALF:(half + 1) * HALF],
                                                      start=(kc == 0), stop=(kc == KC - 1))
                            mm.then_inc(S[sem], 1)
                    if later:
                        make_y(pe, j, 1 - s)
                    pe.wait_ge(S["steps_ready"], j + 1)
                    for n in range(4):
                        free(pe, j, "d", n)
                        nc.tensor.matmul(bank("d", n)[:, :], k.c["below"],
                                         rhs[:, 4 * n:4 * n + 4, :].rearrange("p m t -> p (m t)"),
                                         start=True, stop=True).then_inc(S["diff_psum"], 1)
                    if later:
                        output(pe, j, 1 - s)
                    for half in range(2):
                        free(pe, j, "t", half)
                        pe.wait_ge(S["x_ready"], j * 2 + half + 1)
                        for b in range(4):
                            g = 4 * half + b
                            mm = nc.tensor.transpose(bank("t", half)[:, b * P:(b + 1) * P],
                                                     xT[:, s, g * P:(g + 1) * P], k.ident)
                        mm.then_inc(S["xt_psum"], 1)

                def tail(pe):
                    make_y(pe, N, 1)
                    output(pe, N, 1)
                    pe.wait_ge(S["sq_added"], N)
                    pe.wait_ge(S["diff_read"], 4 * N)
                    for b in range(NB):
                        mm = nc.tensor.matmul(ps[6][:, b:b + 1], sqsum[:, b * P:(b + 1) * P], ones[:, 0:1],
                                              start=True, stop=True)
                    mm.then_inc(S["ms_psum"], 1)

                passes(pe, pair, tail)

            @block.scalar
            def _(act):
                act.wait_ge(S["w_loaded"], 16)
                act.wait_ge(S["abs_dt"], 1)
                nc.scalar.activation(az[:, :, :], az[:, :, :], ACT.Exp, scale=-1.0).then_inc(S["exp_dt"], 1)
                for m, dst in enumerate((bT, cT)):
                    cw = w["conv_bc"][:, m * (TAPS + 1):(m + 1) * (TAPS + 1)]
                    for half in range(2):
                        act.wait_ge(S["bc_psum"], 2 * m + half + 1)
                        conv_first(act, ps[4 + 2 * m + half][:, :],
                                   conv[:, m, 4 * half:4 * half + 4, :].rearrange("p b t -> p (b t)"),
                                   cw[:, 3:4], cw[:, 4:5]).then_inc(S["bc_first"], 1)
                act.wait_ge(S["exp1_dt"], 1)
                nc.scalar.activation(az[:, :, :], az[:, :, :], ACT.Ln).then_inc(S["log_dt"], 1)
                for m, dst in enumerate((bT, cT)):
                    act.wait_ge(S["bc_conv"], m + 1)
                    nc.scalar.activation(dst[:, :], conv[:, m, :, :].rearrange("p b t -> p (b t)"),
                                         ACT.Silu).then_inc(S["bc_ready"], 1)

                def pair(act, j, s, i, later):
                    act.wait_ge(s_load[s], i * 16 + 16)
                    for half in range(2):
                        act.wait_ge(S["x_psum"], j * 2 + half + 1)
                        conv_first(act, bank("x", half)[:, :],
                                   conv[:, s, 4 * half:4 * half + 4, :].rearrange("p b t -> p (b t)"),
                                   taps[s][:, 3:4], cb[s]).then_inc(S["x_scaled"], 1)
                    for half in range(2):
                        act.wait_ge(S["z_psum"], j * 2 + half + 1)
                        if not isinstance(j, int):
                            act.wait_ge(S["y_ready"], j * 2 - 2)
                        nc.scalar.activation(sz[:, s, half * HALF:(half + 1) * HALF], bank("z", half)[:, :],
                                             ACT.Silu).then_inc(S["z_read"], 1)
                    for half in range(2):
                        act.wait_ge(S["x_conv"], j * 2 + half + 1)
                        if not isinstance(j, int):
                            act.wait_ge(S["y_ready"], j * 2 - 2)
                        nc.scalar.activation(xT[:, s, half * HALF:(half + 1) * HALF],
                                             conv[:, s, 4 * half:4 * half + 4, :].rearrange("p b t -> p (b t)"),
                                             ACT.Silu).then_inc(S["x_ready"], 1)
                    d4 = dec[:, s, :, :, :].rearrange("p b h t -> p (b h t)")
                    for n in range(4):
                        act.wait_ge(S["diff_psum"], j * 4 + n + 1)
                        if not isinstance(j, int):
                            act.wait_ge(S["y_psum"], j * 2 - 2)
                        nc.scalar.activation(d4[:, n * HALF:(n + 1) * HALF], bank("d", n)[:, :],
                                             ACT.Exp).then_inc(S["diff_read"], 1)

                passes(act, pair, lambda eng: None)

            @block.vector
            def _(dve):
                step = Chain(dve, S["dve_step"])
                nc.vector.memset(zero[:, :], 0.0).then_inc(S["zero_set"], 1)
                dve.wait_ge(S["w_loaded"], 16)
                dve.wait_ge(S["dt_psum"], 1)
                nc.vector.tensor_tensor(zdt[:, :, :], ps[0][:, :].rearrange("p (b h) -> p b h", b=NB),
                                        over(w["dt_bias"], NB), ALU.add).then_inc(S["zdt"], 1)
                dve.wait_ge(S["zdt"], 1)
                nc.vector.scalar_tensor_tensor(az[:, :, :], zdt[:, :, :], -1.0, zdt[:, :, :], ALU.mult,
                                               ALU.max).then_inc(S["abs_dt"], 1)
                for m in range(2):
                    cw = w["conv_bc"][:, m * (TAPS + 1):(m + 1) * (TAPS + 1)]
                    for half in range(2):
                        dve.wait_ge(S["bc_first"], 2 * m + half + 1)
                        p3 = ps[4 + 2 * m + half][:, :].rearrange("p (b t) -> p b t", b=4)
                        for d in (1, 2, 3):
                            ins = conv_tap(p3, conv[:, m, 4 * half:4 * half + 4, :], d, cw[:, 3 - d:4 - d])
                            if (half, d) == (1, 3):
                                ins.then_inc(S["bc_conv"], 1)
                            else:
                                step(ins)
                dve.wait_ge(S["exp_dt"], 1)
                nc.vector.tensor_scalar(az[:, :, :], az[:, :, :], 1.0, None, ALU.add).then_inc(S["exp1_dt"], 1)
                dve.wait_ge(S["log_dt"], 1)
                step(nc.vector.scalar_tensor_tensor(dt[:, :, :], zdt[:, :, :], 0.0, az[:, :, :], ALU.max, ALU.add))
                nc.vector.tensor_tensor(da[:, :, :], dt[:, :, :], over(w["A"], NB), ALU.mult).then_inc(S["da_ready"], 1)
                for half in range(2):
                    dve.wait_ge(S["cb_psum"], half + 1)
                    nc.vector.tensor_tensor(cbm[:, 4 * half:4 * half + 4, :],
                                            ps[half][:, :].rearrange("p (b t) -> p b t", b=4), over(triu, 4),
                                            ALU.mult).then_inc(S["cb_ready"], 1)
                dve.wait_ge(S["cb_ready"], 2)

                def gate(dve, j, o):
                    dve.wait_ge(S["d_ready"], j)
                    for half in range(2):
                        t = slice(half * HALF, (half + 1) * HALF)
                        dve.wait_ge(S["y_psum"], (j - 1) * 2 + half + 1)
                        if not (isinstance(j, int) and j < 3):
                            dve.wait_ge(S["out_done"], j - 2)
                            dve.wait_ge(S["sq_added"], j - 2)
                        nc.vector.scalar_tensor_tensor(yg[:, o, t], xT[:, o, t], dcols[:, o, :],
                                                       bank("y", half)[:, :], ALU.mult,
                                                       ALU.add).then_inc(S["y_read"], 1)
                        dve.wait_ge(S["y_read"], (j - 1) * 2 + half + 1)
                        nc.vector.tensor_tensor(yg[:, o, t], yg[:, o, t], sz[:, o, t],
                                                ALU.mult).then_inc(S["y_ready"], 1)

                def pair(dve, j, s, i, later):
                    step.restart()
                    for half in range(2):
                        dve.wait_ge(S["x_scaled"], j * 2 + half + 1)
                        p3 = bank("x", half)[:, :].rearrange("p (b t) -> p b t", b=4)
                        c4 = conv[:, s, 4 * half:4 * half + 4, :]
                        for d in (1, 2):
                            step(conv_tap(p3, c4, d, taps[s][:, 3 - d:4 - d]))
                        conv_tap(p3, c4, 3, taps[s][:, 0:1]).then_inc(S["x_read"], 1)
                        dve.wait_ge(S["x_read"], j * 2 + half + 1)
                        dve.sem_inc(S["x_conv"], 1)
                    if later:
                        gate(dve, j, 1 - s)
                    dve.wait_ge(S["diff_read"], j * 4 + 4)
                    for h in range(2):
                        ins = nc.vector.tensor_tensor(dec[:, s, :, h, :], dec[:, s, :, h, :], cbm[:, :, :], ALU.mult)
                    ins.then_inc(S["dec_ready"], 1)
                    dve.wait_ge(S["pair_small"], j * 2 + 2)
                    for half in range(2):
                        dve.wait_ge(S["xt_psum"], j * 2 + half + 1)
                        bs = slice(4 * half, 4 * half + 4)
                        nc.vector.tensor_tensor(dtx[:, s, bs, :, :],
                                                bank("t", half)[:, :].rearrange("p (b h d) -> p b h d", b=4, h=2),
                                                along(dtc[:, s, bs, :], HD), ALU.mult).then_inc(S["xt_read"], 1)

                def tail(dve):
                    step.restart()
                    gate(dve, N, 1)
                    dve.wait_ge(S["ms_psum"], 1)
                    step(nc.vector.tensor_scalar(ms[:, :], ps[6][:, 0:NB], 1.0 / (N * P), 1e-5, ALU.mult, ALU.add))
                    rsqrt(nc, step, ms[:, :], rms[:, :], tmp[:, :])
                    dve.wait_ge(S["out_done"], N)
                    for b in range(NB):
                        nc.vector.scalar_tensor_tensor(x[:, b, :], ps[b // 2][:, (b % 2) * C:(b % 2 + 1) * C],
                                                       rms[:, b:b + 1], x[:, b, :], ALU.mult, ALU.add)

                passes(dve, pair, tail)

            @block.gpsimd
            def _(pool):
                nc.gpsimd.memset(sqsum[:, :], 0.0).then_inc(S["zero_set"], 1)
                pool.wait_ge(S["zero_set"], 1)
                pool.wait_ge(S["da_ready"], 1)

                def squares(pool, j, o):
                    pool.wait_ge(S["y_ready"], (j - 1) * 2 + 2)
                    if not (isinstance(j, int) and j < 2):
                        pool.wait_ge(S["sq_added"], j - 1)
                    nc.gpsimd.tensor_tensor(ysq[:, :], yg[:, o, :], yg[:, o, :], ALU.mult).then_inc(S["sq_ready"], 1)
                    pool.wait_ge(S["sq_ready"], j)
                    nc.gpsimd.tensor_tensor(sqsum[:, :], sqsum[:, :], ysq[:, :], ALU.add).then_inc(S["sq_added"], 1)

                def pair(pool, j, s, i, later):
                    if not isinstance(j, int):
                        pool.wait_ge(S["xt_read"], j * 2 - 2)
                        pool.wait_ge(S["out_done"], j - 1)
                        pool.wait_ge(S["y_read"], j * 2 - 2)
                    hs = slice(j * 2, j * 2 + 2) if isinstance(j, int) else bass.ds(j * 2, 2)
                    nc.gpsimd.tensor_copy(dac[:, s, :, :], da[:, :, hs]).then_inc(S["pair_small"], 1)
                    nc.gpsimd.tensor_copy(dtc[:, s, :, :], dt[:, :, hs]).then_inc(S["pair_small"], 1)
                    pool.wait_ge(S["pair_small"], j * 2 + 2)
                    if later:
                        pool.wait_ge(S["diff_psum"], j * 4)
                    dsel = dac[:, s, :, :].rearrange("p b h -> p (b h)")
                    nc.gpsimd.tensor_tensor(rhs[:, :, :], along(dsel, P), over(triu, 2 * NB),
                                            ALU.mult).then_inc(S["steps_ready"], 1)
                    pool.wait_ge(s_load[s], i * 16 + 16)
                    nc.gpsimd.tensor_tensor(wo[:, s, :], wo_raw[s], nw[s].to_broadcast([P, C]),
                                            ALU.mult).then_inc(S["wo_ready"], 1)
                    nc.gpsimd.tensor_copy(dcols[:, s, :], dcol[s]).then_inc(S["d_ready"], 1)
                    pool.wait_ge(S["x_ready"], j * 2 + 2)
                    pool.wait_ge(S["z_read"], j * 2 + 2)
                    pool.wait_ge(S["wo_ready"], j + 1)
                    pool.wait_ge(S["d_ready"], j + 1)
                    pool.sem_inc(S["slot_read"], 2)
                    if later:
                        squares(pool, j, 1 - s)

                passes(pool, pair, lambda pool: squares(pool, N, 1))


def l3_xattn(k):
    nc, x, xnT, ctxT, ps = k.nc, k.x, k.xnT, k.ctxT, k.ps
    H = 8
    SCALE = P ** -0.5
    uses = [("k", 0), ("k", 1), ("v", 0), ("v", 1)]
    for tag in "ab":
        uses += [(n + tag, h) for n in "qsto" for h in range(2)]
    with Stage(k, "L3x") as st:
        s_kread, s_vread, s_qread, s_sread = (st.sem(n) for n in ("k_read", "v_read", "q_read", "s_read"))
        a = WideHeads(k, st, None)
        tr = a.turns = UnitTurns(k, uses, {"k": s_kread, "v": s_vread, "q": s_qread, "s": s_sread, "t": a.s_pT,
                                           "o": a.s_oT})
        a.sm = st.sb("masked_scores", [P, 2, HALF])
        a.scored = lambda tr, tag, h: a.sm[:, h, :]
        slot = [st.sb(f"head{s}", [P, 4 * P + 2 * P + 2 * C]) for s in range(2)]
        mask8 = st.sb("mask8", [P, TOK], U8)
        maskc8 = st.sb("maskc8", [P, NB], U8)
        neg = st.sb("neg", [P, TOK])
        keep = st.sb("keep", [P, NB])
        s_m, s_load, s_mask = st.sem("mask_loaded"), [st.sem(f"head_loaded{s}") for s in range(2)], st.sem("mask_ready")
        s_q, s_kp, s_v, s_dve = (st.sem(n) for n in ("q_psum", "k_psum", "v_psum", "dve_step"))

        def run(eng, body):
            for s in range(2):
                body(eng, s, s, 0)
            with eng.Fori(1, H // 2) as i:
                for s in range(2):
                    body(eng, i * 2 + s, s, i)

        with nc.Block() as block:

            @block.sync
            def _(sp):
                sp.dma_start(mask8[:, :], k.dram["mask"]).then_inc(s_m, 16)
                sp.dma_start(maskc8[:, :], k.dram["maskT"]).then_inc(s_m, 16)

                def head(sp, j, s, i):
                    if not isinstance(j, int):
                        sp.wait_ge(a.s_y, j * 4 - 4)
                        src = k.dram["L3x"][bass.ds(j, 1), :, :].rearrange("a p n -> (a p) n")
                    else:
                        src = k.dram["L3x"][j]
                    sp.dma_start(slot[s][:, :], src).then_inc(s_load[s], 16)

                run(sp, head)

            @block.gpsimd
            def _(pool):
                pool.wait_ge(s_m, 32)
                nc.gpsimd.tensor_copy(neg[:, :], mask8[:, :]).then_inc(s_mask, 1)
                nc.gpsimd.tensor_copy(keep[:, :], maskc8[:, :]).then_inc(s_mask, 1)
                pool.wait_ge(s_mask, 2)
                nc.gpsimd.tensor_scalar(neg[:, :], neg[:, :], 1.0, BIG, ALU.subtract, ALU.mult).then_inc(s_mask, 1)

            @block.tensor
            def _(pe):
                a.clear_sums(pe)

                def head(pe, j, s, i):
                    w = slot[s]
                    wq = w[:, 0:4 * P].rearrange("p (k n) -> p k n", k=KC)
                    wk, wv = w[:, 4 * P:5 * P], w[:, 5 * P:6 * P]
                    wo = w[:, 6 * P:].rearrange("p (q n) -> p q n", q=2)
                    pe.wait_ge(s_load[s], i * 16 + 16)
                    for h in range(2):
                        tr.free(pe, j, ("k", h))
                        nc.tensor.matmul(tr.bank(("k", h))[:, :], wk, ctxT[:, h * HALF:(h + 1) * HALF],
                                         start=True, stop=True).then_inc(s_kp, 1)
                    for h in range(2):
                        tr.free(pe, j, ("v", h))
                        for b in range(4):
                            g = 4 * h + b
                            mm = nc.tensor.matmul(tr.bank(("v", h))[:, b * P:(b + 1) * P],
                                                  ctxT[:, g * P:(g + 1) * P], wv, start=True, stop=True)
                        mm.then_inc(s_v, 1)
                    for n, tag in enumerate("ab"):
                        for h in range(2):
                            tr.free(pe, j, ("q" + tag, h))
                            for kc in range(KC):
                                mm = nc.tensor.matmul(tr.bank(("q" + tag, h))[:, :], wq[:, kc, n * P:(n + 1) * P],
                                                      xnT[:, kc, h * HALF:(h + 1) * HALF],
                                                      start=(kc == 0), stop=(kc == KC - 1))
                            mm.then_inc(s_q, 1)
                        pe.wait_ge(s_kread, j * 2 + 2)
                        pe.wait_ge(s_vread, j * 2 + 2)
                        pe.wait_ge(s_qread, (j * 2 + n) * 2 + 2)
                        a.pe(pe, j, j * 2 + n, tag, wo[:, n, :])

                run(pe, head)

            @block.scalar
            def _(act):
                def head(act, j, s, i):
                    later = not isinstance(j, int) or j > 0
                    for h in range(2):
                        act.wait_ge(s_kp, j * 2 + h + 1)
                        if later:
                            act.wait_ge(a.s_s, j * 4)
                        nc.scalar.activation(a.kT[:, h * HALF:(h + 1) * HALF], tr.bank(("k", h))[:, :],
                                             ACT.Copy).then_inc(s_kread, 1)
                    for n, tag in enumerate("ab"):
                        u = j * 2 + n
                        for h in range(2):
                            act.wait_ge(s_q, u * 2 + h + 1)
                            if later or n:
                                act.wait_ge(a.s_s, u * 2)
                            nc.scalar.activation(a.qT[:, h * HALF:(h + 1) * HALF], tr.bank(("q" + tag, h))[:, :],
                                                 ACT.Copy).then_inc(s_qread, 1)
                        a.act(act, j, u, tag, lambda b: SCALE)

                run(act, head)

            @block.vector
            def _(dve):
                step = Chain(dve, s_dve)
                nc.vector.memset(a.zero[:, :], 0.0).then_inc(a.s_zero, 1)
                dve.wait_ge(s_mask, 3)

                def head(dve, j, s, i):
                    step.restart()
                    for h in range(2):
                        dve.wait_ge(s_v, j * 2 + h + 1)
                        if not isinstance(j, int) or j:
                            dve.wait_ge(a.s_oTp, j * 4)
                        nc.vector.tensor_tensor(a.v[:, h * HALF:(h + 1) * HALF].rearrange("p (b t) -> p b t", b=4),
                                                tr.bank(("v", h))[:, :].rearrange("p (b t) -> p b t", b=4),
                                                along(keep[:, 4 * h:4 * h + 4], P), ALU.mult).then_inc(s_vread, 1)
                    for n, tag in enumerate("ab"):
                        u = j * 2 + n
                        for h in range(2):
                            dve.wait_ge(a.s_s, u * 2 + h + 1)
                            sm = a.sm[:, h, :]
                            nc.vector.tensor_tensor(sm, tr.bank(("s" + tag, h))[:, :],
                                                    neg[:, h * HALF:(h + 1) * HALF], ALU.add).then_inc(s_sread, 1)
                            dve.wait_ge(s_sread, u * 2 + h + 1)
                            step(nc.vector.tensor_reduce(a.mx[:, h, :], sm.rearrange("p (b t) -> p b t", b=4),
                                                         AX.X, ALU.max))
                            nc.vector.tensor_scalar(a.nb[:, h, :], a.mx[:, h, :], -SCALE, None,
                                                    ALU.mult).then_inc(a.s_nb, 1)
                        for h in range(2):
                            a.dve_probs(dve, step, u, h)
                        for h in range(2):
                            a.dve_turned(dve, u, tag, h)

                run(dve, head)
                dve.wait_ge(a.s_y, 4 * H)
                a.add(dve)


class UnitTurns(Turns):

    def __init__(self, k, uses, sems):
        assert len(uses) % 4 == 0
        self.k, self.uses, self.sems = k, uses, sems

    def free(self, pe, j, use):
        at = self.uses.index(use)
        (name, n), earlier = self.uses[at - 4], at < 4
        if earlier and isinstance(j, int) and j == 0:
            return
        per = 4 if len(name) == 2 else 2
        n += 2 * (name[1:] == "b")
        pe.wait_ge(self.sems[name[0]], (j - 1 if earlier else j) * per + n + 1)


def l3_ffn(k):
    nc, x, xnT, ps = k.nc, k.x, k.xnT, k.ps
    HID = [1, 2, 3, 4, 1, 2, 3, 4]
    E, NCH = len(HID), sum(HID)
    first = [sum(HID[:e]) for e in range(E)] + [NCH]
    sizes = HID + [1]
    with Stage(k, "L3f") as st:
        img = st.sb("weights", [P, k.width["L3f"]])
        w = sbuf_views(img, *k.parts["L3f"])
        down, rout, core = (w[n].rearrange("p (k n) -> p k n", k=KC) for n in ("down", "router", "core"))
        w1 = w["w1"].rearrange("p (c n) -> p c n", c=NCH + 1)
        w2 = w["w2"].rearrange("p (c n) -> p c n", c=NCH + 1)
        b1 = w["b1"]
        gh = st.sb("gelu_hT", [P, TOK])
        hb = st.sb("hT", [P, 2, HALF])
        gx = st.sb("gelu_xT", [P, KC, TOK])
        u = st.sb("u", [P, 2, 4, TOK])
        u0 = st.sb("u0", [P, NCH])
        u0e = st.sb("u0_by_expert", [P, NCH, E])
        d = st.sb("idle_out", [E, P])
        gates = st.sb("gates", [P, NB, E + 1])
        idle = st.sb("idle_weights", [P, NB, E])
        idleT = st.sb("idle_weightsT", [E, TOK])
        b2sum = st.sb("b2_sum", [P, P])
        gdiff, gexp, g1, g2 = (st.sb(n, [P, NB]) for n in ("gdiff", "gexp", "g1", "g2"))
        acc = st.sb("acc", [P, NB, P])
        accT = st.sb("accT", [P, TOK])
        r = Router(k, st, E, ps[7])
        s_w, s_h, s_hc, s_gh, s_gx = (st.sem(n) for n in ("w_loaded", "h_psum", "h_read", "gelu_h", "gelu_x"))
        s_u0, s_u0e, s_dp, s_d = (st.sem(n) for n in ("u0", "u0_placed", "idle_psum", "idle_ready"))
        s_it, s_itc, s_c, s_acc0 = (st.sem(n) for n in ("idleT_psum", "idleT_ready", "corr_psum", "acc_started"))
        s_gd, s_ge, s_idle, s_up, s_u = (st.sem(n) for n in ("gate_diff", "gate_exp", "idle_w", "u_psum", "u_ready"))
        s_y, s_yr, s_at, s_atc, s_o = (st.sem(n) for n in ("y_psum", "y_read", "accT_psum", "accT_ready", "out_psum"))
        s_bias, s_dve = st.sem("bias_added"), st.sem("dve_step")
        done = [2 * sum(sizes[:e]) for e in range(E + 2)]

        def hidden_units():
            n = 0
            for e in range(E + 1):
                for c in range(sizes[e]):
                    for half in range(2):
                        yield e, c, half, n
                        n += 1

        with nc.Block() as block:

            @block.sync
            def _(sp):
                sp.dma_start(img[:, :], k.dram["L3f"]).then_inc(s_w, 16)

            @block.gpsimd
            def _(pool):
                nc.gpsimd.memset(u0e[:, :, :], 0.0).then_inc(s_bias, 1)
                pool.wait_ge(s_w, 16)
                nc.gpsimd.tensor_tensor(x[:, :, :], x[:, :, :], over(w["up_b"], NB), ALU.add).then_inc(s_bias, 1)
                pool.wait_ge(s_bias, 2)
                nc.gpsimd.tensor_tensor(x[:, :, :], x[:, :, :], over(w["core_b"], NB), ALU.add).then_inc(s_bias, 1)
                pool.wait_ge(s_u0, 1)
                for e in range(E):
                    ins = nc.gpsimd.tensor_copy(u0e[:, first[e]:first[e] + HID[e], e], u0[:, first[e]:first[e] + HID[e]])
                ins.then_inc(s_u0e, 1)

            @block.tensor
            def _(pe):
                pe.wait_ge(s_w, 16)
                r.matmuls(rout)
                for half in range(2):
                    for kc in range(KC):
                        mm = nc.tensor.matmul(ps[half][:, :], down[:, kc, :], xnT[:, kc, half * HALF:(half + 1) * HALF],
                                              start=(kc == 0), stop=(kc == KC - 1))
                    mm.then_inc(s_h, 1)
                pe.wait_ge(s_u0e, 1)
                for c in range(NCH):
                    mm = nc.tensor.matmul(ps[6][0:E, 0:P], u0e[:, c, :], w2[:, c, :], start=(c == 0),
                                          stop=(c == NCH - 1))
                mm.then_inc(s_dp, 1)
                pe.wait_ge(s_idle, 1)
                for b in range(NB):
                    if b % 4 == 0:
                        pe.wait_ge(s_gh, 2)
                    mm = nc.tensor.transpose(ps[4 + b // 4][0:E, (b % 4) * P:(b % 4 + 1) * P], idle[:, b, :], k.ident)
                    if b % 4 == 3:
                        mm.then_inc(s_it, 1)
                pe.wait_ge(s_itc, 2)
                pe.wait_ge(s_d, 1)
                for b in range(NB):
                    mm = nc.tensor.matmul(ps[4 + b // 4][:, (b % 4) * P:(b % 4 + 1) * P], idleT[:, b * P:(b + 1) * P],
                                          d[:, :], start=True, stop=True)
                    if b % 4 == 3:
                        mm.then_inc(s_c, 1)
                pe.wait_ge(s_acc0, 2)

                def out(e):
                    pe.wait_ge(s_u, done[e + 1])
                    for half in range(2):
                        if e >= 2:
                            pe.wait_ge(s_yr, 2 * (e - 2) + half + 1)
                        bank = ps[4 + 2 * (e % 2) + half]
                        for j in range(4):
                            b = 4 * half + j
                            for c in range(sizes[e]):
                                mm = nc.tensor.matmul(bank[:, j * P:(j + 1) * P], u[:, e % 2, c, b * P:(b + 1) * P],
                                                      w2[:, first[e] + c, :], start=(c == 0), stop=(c == sizes[e] - 1))
                        mm.then_inc(s_y, 1)

                for e, c, half, n in hidden_units():
                    if n >= 4:
                        pe.wait_ge(s_u, n - 3)
                    nc.tensor.matmul(ps[n % 4][:, :], w1[:, first[e] + c, :], gh[:, half * HALF:(half + 1) * HALF],
                                     start=True, stop=True).then_inc(s_up, 1)
                    if e and c == 0 and half == 1:
                        out(e - 1)
                out(E)
                for b in range(NB):
                    if b % 4 == 0:
                        pe.wait_ge(s_yr, 2 * E + b // 4 + 1)
                        pe.wait_ge(s_u, done[E + 1])
                    mm = nc.tensor.transpose(ps[b // 4][:, (b % 4) * P:(b % 4 + 1) * P], acc[:, b, :], k.ident)
                    if b % 4 == 3:
                        mm.then_inc(s_at, 1)
                pe.wait_ge(s_gx, 1)
                for b in range(NB):
                    pe.wait_ge(s_atc, b // 4 + 1)
                    y = ps[4 + b // 2][:, (b % 2) * C:(b % 2 + 1) * C]
                    nc.tensor.matmul(y, accT[:, b * P:(b + 1) * P], w["up"], start=True, stop=False)
                    for kc in range(KC):
                        mm = nc.tensor.matmul(y, gx[:, kc, b * P:(b + 1) * P], core[:, kc, :], start=False,
                                              stop=(kc == KC - 1))
                    if b % 2:
                        mm.then_inc(s_o, 1)

            @block.scalar
            def _(act):
                act.wait_ge(s_w, 16)
                r.exponent(act)
                act.wait_ge(s_gd, 1)
                nc.scalar.activation(gexp[:, :], gdiff[:, :], ACT.Exp).then_inc(s_ge, 1)
                nc.scalar.activation(u0[:, :], b1[:, 0:NCH], ACT.Gelu).then_inc(s_u0, 1)
                for half in range(2):
                    act.wait_ge(s_h, half + 1)
                    nc.scalar.activation(hb[:, half, :], ps[half][:, :], ACT.Identity,
                                         bias=w["down_b"]).then_inc(s_hc, 1)
                for half in range(2):
                    act.wait_ge(s_hc, half + 1)
                    nc.scalar.activation(gh[:, half * HALF:(half + 1) * HALF], hb[:, half, :],
                                         ACT.Gelu).then_inc(s_gh, 1)
                nc.scalar.activation(gx[:, :, :], xnT[:, :, :], ACT.Gelu).then_inc(s_gx, 1)
                for e, c, half, n in hidden_units():
                    act.wait_ge(s_up, n + 1)
                    if e >= 2:
                        act.wait_ge(s_y, 2 * (e - 2) + 2)
                    nc.scalar.activation(u[:, e % 2, c, half * HALF:(half + 1) * HALF], ps[n % 4][:, :], ACT.Gelu,
                                         bias=b1[:, first[e] + c:first[e] + c + 1]).then_inc(s_u, 1)
                for half in range(2):
                    act.wait_ge(s_at, half + 1)
                    nc.scalar.activation(accT[:, half * HALF:(half + 1) * HALF], ps[half][:, :],
                                         ACT.Copy).then_inc(s_atc, 1)

            @block.vector
            def _(dve):
                step = Chain(dve, s_dve)
                dve.wait_ge(s_w, 16)
                dve.wait_ge(r.s_logits, 1)
                step(nc.vector.tensor_tensor(r.z[:, :, :], r.logits, over(w["b_router"], NB), ALU.add))
                step(nc.vector.tensor_tensor(r.z[:, :, :], r.z[:, :, :], over(k.c["cost"], NB), ALU.subtract))
                r.softmax(dve, step)
                r.top_two(step)
                nc.vector.tensor_tensor(gdiff[:, :], r.top2[:, :], r.top1[:, :], ALU.subtract).then_inc(s_gd, 1)
                dve.wait_ge(s_ge, 1)
                step(nc.vector.tensor_scalar(g2[:, :], gexp[:, :], 1.0, None, ALU.add))
                step(nc.vector.reciprocal(g1[:, :], g2[:, :]))
                step(nc.vector.tensor_tensor(g2[:, :], gexp[:, :], g1[:, :], ALU.mult))
                step(nc.vector.memset(gates[:, :, E:E + 1], 0.1))
                step(nc.vector.tensor_tensor(r.first[:, :, :], r.first[:, :, :], along(g1[:, :], E), ALU.mult))
                step(nc.vector.tensor_tensor(r.second[:, :, :], r.second[:, :, :], along(g2[:, :], E), ALU.mult))
                step(nc.vector.tensor_tensor(gates[:, :, 0:E], r.first[:, :, :], r.second[:, :, :], ALU.add))
                nc.vector.tensor_scalar(idle[:, :, :], gates[:, :, 0:E], -1.0, 1.0, ALU.mult,
                                        ALU.add).then_inc(s_idle, 1)
                b2 = w["b2"].rearrange("p (e l) -> p e l", e=E + 1)
                step(nc.vector.tensor_reduce(b2sum[:, :], b2[:, 0:E, :].rearrange("p e l -> p l e"), AX.X, ALU.add))
                step(nc.vector.scalar_tensor_tensor(b2sum[:, :], b2[:, E, :], 0.1, b2sum[:, :], ALU.mult, ALU.add))
                dve.wait_ge(s_dp, 1)
                nc.vector.tensor_copy(d[:, :], ps[6][0:E, 0:P]).then_inc(s_d, 1)
                for half in range(2):
                    dve.wait_ge(s_it, half + 1)
                    nc.vector.tensor_copy(idleT[:, half * HALF:(half + 1) * HALF], ps[4 + half][0:E, :]).then_inc(s_itc, 1)
                for half in range(2):
                    dve.wait_ge(s_c, half + 1)
                    nc.vector.tensor_tensor(acc[:, 4 * half:4 * half + 4, :],
                                            ps[4 + half][:, :].rearrange("p (b l) -> p b l", b=4),
                                            over(b2sum[:, :], 4), ALU.add).then_inc(s_acc0, 1)
                dve.wait_ge(s_acc0, 2)
                for e in range(E + 1):
                    for half in range(2):
                        dve.wait_ge(s_y, 2 * e + half + 1)
                        if e:
                            dve.wait_ge(s_yr, 2 * (e - 1) + half + 1)
                        for j in range(4):
                            b = 4 * half + j
                            ins = nc.vector.scalar_tensor_tensor(
                                acc[:, b, :], ps[4 + 2 * (e % 2) + half][:, j * P:(j + 1) * P], gates[:, b, e:e + 1],
                                acc[:, b, :], ALU.mult, ALU.add)
                        ins.then_inc(s_yr, 1)
                dve.wait_ge(s_bias, 3)
                for n in range(4):
                    dve.wait_ge(s_o, n + 1)
                    nc.vector.tensor_tensor(x[:, 2 * n:2 * n + 2, :], x[:, 2 * n:2 * n + 2, :],
                                            ps[4 + n][:, :].rearrange("p (b n) -> p b n", b=2), ALU.add)


STAGES = [l0_attn, l0_xattn, l0_ffn, l1_attn, l1_xattn, l1_ffn, l2_attn, l2_xattn, l2_ffn, l3_attn, l3_xattn, l3_ffn]


def program(nc, dram, parts, width, out):
    k = K()
    k.nc, k.dram, k.parts, k.width = nc, dram, parts, width
    with ExitStack() as ctx:
        k.ps = [ctx.enter_context(nc.psum_tensor(f"bank{i}", [P, HALF], F32)) for i in range(8)]
        k.x = ctx.enter_context(nc.sbuf_tensor("x", [P, NB, C], F32))
        k.xn = ctx.enter_context(nc.sbuf_tensor("xn", [P, NB, C], F32))
        k.xnT = ctx.enter_context(nc.sbuf_tensor("xnT", [P, KC, TOK], F32))
        k.ctxT = ctx.enter_context(nc.sbuf_tensor("ctxT", [P, TOK], F32))
        const = ctx.enter_context(nc.sbuf_tensor("const", [P, width["const"]], F32))
        k.c = sbuf_views(const, *parts["const"])
        k.ident = k.c["ident"]
        with Stage(k, "begin") as st:
            s_in = st.sem("inputs_loaded")
            with nc.Block() as block:

                @block.sync
                def _(sp):
                    sp.dma_start(k.x[:, :, :], dram["x"]).then_inc(s_in, 16)
                    sp.dma_start(k.ctxT[:, :], dram["ctxT"]).then_inc(s_in, 16)
                    sp.dma_start(const[:, :], dram["const"]).then_inc(s_in, 16)
                    sp.wait_ge(s_in, 48)
        for n, stage in enumerate(STAGES):
            if FIRST <= n <= LAST:
                layernorm(k, n)
                stage(k)
        with Stage(k, "end") as st:
            s_out = st.sem("output_stored")
            with nc.Block() as block:

                @block.sync
                def _(sp):
                    sp.dma_start(out, k.x[:, :, :]).then_inc(s_out, 16)
                    sp.wait_ge(s_out, 16)



def rows(a):
    a = np.asarray(a)
    return a.reshape(-1, P, a.shape[1]).transpose(1, 0, 2).reshape(P, -1)


def cols(v):
    return np.asarray(v).reshape(-1, P).T


def each(v):
    return np.broadcast_to(np.asarray(v).reshape(1, -1), (P, np.asarray(v).size))


def constants():
    i = np.arange(P)
    c = {"ident": np.eye(P), "ones": np.ones((P, P)), "triu": (i[:, None] <= i[None, :]) * 1.0,
         "causal": np.where(i[None, :] <= i[:, None], 0.0, -BIG),
         "causalT": np.where(i[:, None] <= i[None, :], 0.0, -BIG),
         "head_ones16": (i[:, None] // 16 == i[None, :] // 16) * 1.0,
         "in_head16": (i[:, None] // 16 == np.arange(8)[None, :]) * 1.0,
         "in_head8": (i[:, None] // 8 == np.arange(16)[None, :]) * 1.0,
         "iota": each(np.arange(8.0)), "iota_far": each(np.arange(8.0) + 100.0)}
    return {n: np.asarray(a, np.float32) for n, a in c.items()}


def images(i):
    im = {"const": constants()}
    im["L2a"] = {"w_qkv": rows(i["L2_attn_w_qkv"]), "w_out": rows(i["L2_attn_w_out"]),
                 "decay": cols(np.repeat(np.asarray(i["L2_attn_decay_param"]), 16))}
    im["L0a"] = {"wq": rows(i["L0_attn_Wq"].T), "wk": rows(i["L0_attn_Wk"].T), "wv": rows(i["L0_attn_Wv"].T),
                 "wp": rows(i["L0_attn_Wp"].T), "bq": cols(i["L0_attn_bq"]), "bk": cols(i["L0_attn_bk"]),
                 "bv": each(i["L0_attn_bv"]), "bp": each(i["L0_attn_bp"])}
    im["const"]["freq"] = np.tile(np.array([1.0, 10000.0 ** -0.5], np.float32), (P, 2))
    im["L0x"] = {"wq": rows(i["L0_xattn_Wq"]), "wkv": np.asarray(i["L0_xattn_Wkv"]),
                 "wout": rows(i["L0_xattn_Wout"]), "bout": each(i["L0_xattn_bout"]),
                 "pos": np.repeat(np.asarray(i["fside_BxSx2_0"]).transpose(1, 0, 2), 2, axis=2).reshape(P, -1)}
    im["L0f"] = {"gate_w": rows(i["L0_ffn_gate_w"].T), "val_w": rows(i["L0_ffn_val_w"].T),
                 "out_w": rows(i["L0_ffn_out_w"].T), "gate_b": each(i["L0_ffn_gate_b"]),
                 "val_b": each(i["L0_ffn_val_b"]), "out_b": each(i["L0_ffn_out_b"])}
    n, f = np.arange(16), np.arange(9)
    turn = 2 * np.pi * n[:, None] * f[None, :] / 16
    both = np.where((f == 0) | (f == 8), 1.0, 2.0 ** 0.5)
    wave = np.stack([np.cos(turn) * both, -np.sin(turn) * both], 1)
    fwd = np.zeros((16, 16, 2, 16, 9), np.float32)
    for h in range(16):
        fwd[h, :, :, h, :] = wave
    fwd = fwd.reshape(C, 288)
    im["L1a"] = {"wq": rows(i["L1_attn_W_q"]), "wkv": rows(i["L1_attn_W_kv"]),
                 "woT": rows(np.asarray(i["L1_attn_W_o"]).T), "fwd": rows(fwd),
                 "inv": rows(np.asarray(wave_inverse(), np.float32))}
    im["L1n"] = {"gq": cols(i["L1_xattn_gq"]), "gk": cols(i["L1_xattn_gk"])}
    im["L1g"] = {"w_gate": rows(i["L1_ffn_w_gate"])}
    main_rows = (np.arange(P) < P - 16)[:, None]
    im["const"]["key_parts"] = np.concatenate([main_rows, ~main_rows], 1).astype(np.float32)
    heads = np.arange(512).reshape(16, 2, 16)
    kcols, vcols = heads[:, 0].ravel(), heads[:, 1].ravel()
    wkv = np.concatenate([np.asarray(i["L2_xattn_Wk"]), np.asarray(i["L2_xattn_Wv"])], 1)
    bkv = np.concatenate([np.asarray(i["L2_xattn_bk"]), np.asarray(i["L2_xattn_bv"])])
    wd, bd = np.asarray(i["L2_xattn_Wkv_dca"]), np.asarray(i["L2_xattn_bkv_dca"])
    zero = np.zeros((), np.float32)
    im["L2x"] = {"wq": rows(i["L2_xattn_Wq"]), "wo": rows(i["L2_xattn_Wo"]),
                 "wk": wkv[:, kcols], "wv": wkv[:, vcols], "wkd": wd[:, :C], "wvd": wd[:, C:],
                 "bqk": np.concatenate([each(i["L2_xattn_bq"]), np.where(main_rows, bkv[kcols], bd[:C])], 1),
                 "bvs": np.concatenate([np.where(main_rows, bkv[vcols], zero), np.where(main_rows, zero, bd[C:])], 1),
                 "nw": np.stack([np.tile(np.asarray(i[f"L2_xattn_{n}_w"]), 8) for n in ("qn", "kn", "kn_dca")], 1),
                 "nb": np.stack([np.tile(np.asarray(i[f"L2_xattn_{n}_b"]), 8) for n in ("qn", "kn", "kn_dca")], 1),
                 "bo": each(i["L2_xattn_bo"])}
    ar, br = np.asarray(i["L2_ffn_A_r"]), np.asarray(i["L2_ffn_B_r"])
    down = np.concatenate([np.asarray(i["L2_ffn_A_s"]), ar.transpose(1, 0, 2).reshape(C, -1)], 1)
    up = np.concatenate([np.asarray(i["L2_ffn_B_s"]), br.reshape(-1, C), np.zeros((16, C), np.float32)])
    im["L2f"] = {"base": rows(i["L2_ffn_W_base"]), "down": rows(down), "up": up,
                 "router": rows(i["L2_ffn_W_router"]), "b": each(i["L2_ffn_b_base"]),
                 "b_router": each(i["L2_ffn_b_router"])}
    n = np.arange(P)
    im["const"]["below"] = (n[:, None] > n[None, :]).astype(np.float32)
    w_in, cw = np.asarray(i["L3_attn_W_in"]), np.asarray(i["L3_attn_conv_w"])
    cwb = np.concatenate([cw, np.asarray(i["L3_attn_conv_b"])[:, None]], 1)
    im["L3a"] = {"wb": rows(w_in[:, 8192:8320]), "wc": rows(w_in[:, 8320:8448]), "wdt": rows(w_in[:, 8448:]),
                 "dt_bias": each(i["L3_attn_dt_bias"]), "A": each(i["L3_attn_A"]),
                 "conv_bc": np.concatenate([cwb[4096:4224], cwb[4224:4352]], 1)}
    experts = [f"e{e}" for e in range(8)] + ["shared"]
    p3 = {n: [np.asarray(i[f"L3_ffn_{e}_{n}"]) for e in experts] for n in ("w1", "b1", "w2", "b2")}
    w1 = np.concatenate(p3["w1"], 1)
    im["const"]["cost"] = each(np.float32(1e-7) * np.array([2 * 128 * h for h in (128, 256, 384, 512) * 2], np.float32))
    im["L3f"] = {"down": rows(i["L3_ffn_down_w"]), "router": rows(i["L3_ffn_router_w"]),
                 "core": rows(i["L3_ffn_core_w"]), "up": np.asarray(i["L3_ffn_up_w"]), "w1": w1,
                 "w2": rows(np.concatenate(p3["w2"])), "b1": cols(np.concatenate(p3["b1"])),
                 "b2": each(np.concatenate(p3["b2"])), "down_b": cols(i["L3_ffn_down_b"]),
                 "up_b": each(i["L3_ffn_up_b"]), "core_b": each(i["L3_ffn_core_b"]),
                 "b_router": each(i["L3_ffn_router_b"])}
    return im


def kernel(**inputs):
    import concourse.bacc as bacc
    from concourse.bass_utils import run_bass_kernel_spmd

    im = images(inputs)
    arrays = {n: np.concatenate(list(parts.values()), axis=-1) for n, parts in im.items()}
    arrays["x"] = np.asarray(inputs["x"]).transpose(1, 0, 2)
    arrays["ctxT"] = np.asarray(inputs["ctx_1024"]).reshape(TOK, P).T
    arrays["L1x"] = np.stack([np.concatenate(
        [rows(np.asarray(inputs["L1_xattn_Wq"])[:, h * P:(h + 1) * P]),
         np.asarray(inputs["L1_xattn_Wk"])[:, h * P:(h + 1) * P], np.asarray(inputs["L1_xattn_Wv"])[:, h * P:(h + 1) * P],
         np.asarray(inputs["L1_xattn_Wo"])[h * P:(h + 1) * P]], 1) for h in range(16)])
    arrays["L1f"] = np.stack([np.concatenate([rows(inputs[f"L1_ffn_{n}"][e]) for n in ("w1", "w3", "w2")], 1)
                              for e in range(8)])
    w_in, w_out = np.asarray(inputs["L3_attn_W_in"]), np.asarray(inputs["L3_attn_W_out"])
    small = np.concatenate([np.asarray(inputs["L3_attn_conv_w"])[:4096], np.asarray(inputs["L3_attn_conv_b"])[:4096, None],
                            np.repeat(np.asarray(inputs["L3_attn_D"]), 64)[:, None],
                            np.asarray(inputs["L3_attn_norm_w"])[:, None], np.zeros((4096, 1), np.float32)], 1)
    arrays["L3p"] = np.stack([np.concatenate([rows(w_in[:, c * P:(c + 1) * P]),
                                              rows(w_in[:, 4096 + c * P:4096 + (c + 1) * P]),
                                              w_out[c * P:(c + 1) * P], small[c * P:(c + 1) * P]], 1)
                              for c in range(32)])
    arrays["L3x"] = np.stack([np.concatenate(
        [rows(np.asarray(inputs["L3_xattn_Wq"])[:, h * C:(h + 1) * C]),
         np.asarray(inputs["L3_xattn_Wk"])[:, h * P:(h + 1) * P], np.asarray(inputs["L3_xattn_Wv"])[:, h * P:(h + 1) * P],
         rows(np.asarray(inputs["L3_xattn_Wo"])[h * C:(h + 1) * C])], 1) for h in range(8)])
    mask = np.asarray(inputs["mask_BxS2_bf1"]).view(np.uint8)
    arrays["mask"] = np.broadcast_to(mask.reshape(1, TOK), (P, TOK))
    arrays["maskT"] = mask.T
    arrays = {n: np.ascontiguousarray(a) for n, a in arrays.items()}
    parts = {n: (list(p), {m: a.shape[-1] for m, a in p.items()}) for n, p in im.items()}
    width = {n: arrays[n].shape[-1] for n in im}
    nc = bacc.Bacc("TRN2", target_bir_lowering=False, num_devices=1)
    dram = {n: nc.dram_tensor(f"in_{n}", a.shape, mybir.dt.from_np(a.dtype), kind="ExternalInput").ap()
            for n, a in arrays.items()}
    out = nc.dram_tensor("out_x", (P, NB, C), F32, kind="ExternalOutput").ap()
    program(nc, dram, parts, width, out)
    r = run_bass_kernel_spmd(nc, [{f"in_{n}": a for n, a in arrays.items()}], core_ids=[0])
    return np.ascontiguousarray(r.results[0]["out_x"].reshape(P, NB, C).transpose(1, 0, 2))


def wave_inverse():
    n, f = np.arange(16), np.arange(9)
    turn = 2 * np.pi * n[:, None] * f[None, :] / 16
    part = np.stack([np.cos(turn), -np.sin(turn)], 1) / 16
    inv = np.zeros((16, 16, 2, 16, 9))
    for h in range(16):
        inv[h, :, :, h, :] = part
    return inv.reshape(C, 288)
```

```python
from contextlib import ExitStack

import numpy as np

import concourse.bass as bass
from concourse import mybir

FIRST, LAST = 0, 11

P = 128
NB = 8
C = 256
KC = C // P
TOK = NB * P
HALF = TOK // 2
F32 = mybir.dt.float32
BF16 = mybir.dt.bfloat16
F32R = mybir.dt.float32r
U8 = mybir.dt.uint8
ALU = mybir.AluOpType
ACT = mybir.ActivationFunctionType
AX = mybir.AxisListType
BIG = 1.0e30
ROUND = 12582912.0
TWO_PI = 6.283185307179586


class Chain:

    def __init__(self, eng, sem):
        self.eng, self.sem, self.n = eng, sem, 0

    def __call__(self, ins):
        self.n += 1
        ins.then_inc(self.sem, 1)
        self.eng.wait_ge(self.sem, self.n)

    def restart(self):
        self.eng.sem_clear(self.sem)
        self.n = 0


class Stage:

    def __init__(self, k, name, weights=None):
        self.k, self.nc, self.name, self.sems = k, k.nc, name, []
        if weights is not None:
            self.sems += [weights.s_img, *weights.s_slot]

    def __enter__(self):
        self.ctx = ExitStack()
        return self

    def sb(self, name, shape, dt=F32):
        return self.ctx.enter_context(self.nc.sbuf_tensor(f"{self.name}_{name}", shape, dt))

    def sem(self, name):
        s = self.nc.alloc_semaphore(f"{self.name}_{name}")
        self.sems.append(s)
        return s

    def __exit__(self, *e):
        if e[0] is None:
            for s in self.sems:
                self.nc.gpsimd.sem_clear(s)
            self.nc.all_engine_barrier()
            for s in self.sems:
                self.nc.release_semaphore(s)
            self.ctx.close()
        return False


class K:
    pass


class Weights:

    def __init__(self, k, n):
        image, slotted = WEIGHTS[n]
        self.k, self.image, self.slotted = k, image, slotted
        arena, at = k.arena[n % 2], k.width[image] if image else 0
        self.img = arena[:, 0:at]
        self.slot = []
        if slotted:
            w = k.dram[slotted].shape[-1]
            self.slot = [arena[:, at + s * w:at + (s + 1) * w] for s in range(2)]
        self.arena, self.end = arena, at + (2 * w if slotted else 0)
        self.s_img = k.nc.alloc_semaphore(f"image_loaded_{n}")
        self.s_slot = [k.nc.alloc_semaphore(f"slot{s}_loaded_{n}") for s in range(2)]

    def spare(self, *shape):
        n = int(np.prod(shape))
        at, self.end = self.end, self.end + n
        assert self.end <= self.arena.shape[1]
        axes = "abcd"[:len(shape)]
        return self.arena[:, at:at + n].rearrange(f"p ({' '.join(axes)}) -> p {' '.join(axes)}",
                                                  **dict(zip(axes, shape)))

    def load(self, sp):
        if self.image:
            sp.dma_start(self.img, self.k.dram[self.image]).then_inc(self.s_img, 16)
        for s, t in enumerate(self.slot):
            sp.dma_start(t, self.k.dram[self.slotted][s]).then_inc(self.s_slot[s], 16)


def sbuf_views(tile, names, widths):
    out, at = {}, 0
    for n in names:
        out[n] = tile[:, at:at + widths[n]]
        at += widths[n]
    return out


def layernorm(k, tag, after, eps=1e-5):
    nc, x, xn, xnT, ps = k.nc, k.x, k.xn, k.xnT, k.ps
    with Stage(k, f"ln{tag}") as st:
        stats = st.sb("stats", [P, NB, 6])
        mv = st.sb("mv", [P, NB, 2])
        inv = st.sb("inv", [P, NB])
        rstd = st.sb("rstd", [P, NB])
        s_stats, s_mv, s_rstd = st.sem("stats_done"), st.sem("mean_var_done"), st.sem("rstd_done")
        s_inv = st.sem("inverse_variance")
        s_xn, s_xnT, s_copied = st.sem("xn_done"), st.sem("xnT_in_psum"), st.sem("xnT_copied")
        with nc.Block() as block:

            @block.sync
            def _(sp):
                if after is not None:
                    after.load(sp)

            @block.vector
            def _(dve):
                for b in range(NB):
                    nc.vector.bn_stats(stats[:, b, :], x[:, b, :]).then_inc(s_stats, 1)
                for b in range(NB):
                    dve.wait_ge(s_stats, b + 1)
                    nc.vector.bn_aggr(mv[:, b, :], stats[:, b, :]).then_inc(s_mv, 1)
                dve.wait_ge(s_mv, NB)
                nc.vector.tensor_scalar(inv[:, :], mv[:, :, 1], eps, None, ALU.add).then_inc(s_inv, 1)
                dve.wait_ge(s_inv, 1)
                nc.vector.reciprocal(inv[:, :], inv[:, :]).then_inc(s_inv, 1)
                dve.wait_ge(s_rstd, 1)
                for b in range(NB):
                    nc.vector.tensor_scalar(xn[:, b, :], x[:, b, :], mv[:, b, 0:1], rstd[:, b:b + 1],
                                            ALU.subtract, ALU.mult).then_inc(s_xn, 1)
                for u in range(2, 4):
                    dve.wait_ge(s_xnT, 4 * (u + 1))
                    nc.vector.tensor_copy(xnT[:, u % 2, (u // 2) * HALF:(u // 2 + 1) * HALF],
                                          ps[u][:, :]).then_inc(s_copied, 1)

            @block.scalar
            def _(act):
                act.wait_ge(s_inv, 2)
                nc.scalar.activation(rstd[:, :], inv[:, :], ACT.Sqrt).then_inc(s_rstd, 1)
                for u in range(0, 2):
                    act.wait_ge(s_xnT, 4 * (u + 1))
                    nc.scalar.activation(xnT[:, u % 2, (u // 2) * HALF:(u // 2 + 1) * HALF],
                                         ps[u][:, :], ACT.Copy).then_inc(s_copied, 1)

            @block.tensor
            def _(pe):
                for u in range(4):
                    for j in range(4):
                        b = 4 * (u // 2) + j
                        pe.wait_ge(s_xn, b + 1)
                        nc.tensor.transpose(ps[u][:, j * P:(j + 1) * P],
                                            xn[:, b, (u % 2) * P:(u % 2 + 1) * P],
                                            k.ident).then_inc(s_xnT, 1)


def along(ap, n):
    return ap.unsqueeze(len(ap.shape)).to_broadcast([*ap.shape, n])


def over(ap, n):
    return ap.unsqueeze(1).to_broadcast([ap.shape[0], n, *ap.shape[1:]])


def since(eng, sem, n):
    if not (isinstance(n, int) and n <= 0):
        eng.wait_ge(sem, n)


class Router:

    def __init__(self, k, st, E, bank):
        self.k, self.E = k, E
        t = lambda name, *shape: st.sb(name, [P, NB, *shape])
        self.logits = bank[:, 0:NB * E].rearrange("p (b e) -> p b e", b=NB)
        self.z, self.e, self.probs = t("z", E), t("e", E), t("probs", E)
        self.m, self.s, self.r = t("zmax"), t("zsum"), t("zrec")
        self.eq, self.cand, self.left = t("eq", E), t("cand", E), t("left", E)
        self.first, self.second = t("first", E), t("second", E)
        self.at, self.top1, self.top2 = t("at"), t("top1"), t("top2")
        self.s_logits, self.s_z, self.s_e = st.sem("logits_ready"), st.sem("z_ready"), st.sem("z_exp_ready")

    def matmuls(self, w):
        nc = self.k.nc
        for b in range(NB):
            for kc in range(KC):
                mm = nc.tensor.matmul(self.logits[:, b, :], self.k.xnT[:, kc, b * P:(b + 1) * P],
                                      w[:, kc, :], start=(kc == 0), stop=(kc == KC - 1))
        mm.then_inc(self.s_logits, 1)

    def exponent(self, act, scale=1.0):
        act.wait_ge(self.s_z, 1)
        self.k.nc.scalar.activation(self.e[:, :, :], self.z[:, :, :], ACT.Exp, scale=scale).then_inc(self.s_e, 1)

    def softmax(self, dve, step):
        nc, E = self.k.nc, self.E
        step(nc.vector.tensor_reduce(self.m[:, :], self.z[:, :, :], AX.X, ALU.max))
        nc.vector.tensor_tensor(self.z[:, :, :], self.z[:, :, :], along(self.m[:, :], E),
                                ALU.subtract).then_inc(self.s_z, 1)
        dve.wait_ge(self.s_e, 1)
        step(nc.vector.tensor_reduce(self.s[:, :], self.e[:, :, :], AX.X, ALU.add))
        step(nc.vector.reciprocal(self.r[:, :], self.s[:, :]))
        step(nc.vector.tensor_tensor(self.probs[:, :, :], self.e[:, :, :], along(self.r[:, :], E), ALU.mult))

    def pick(self, step, probs, top, onehot):
        nc, E, c = self.k.nc, self.E, self.k.c
        step(nc.vector.tensor_reduce(top[:, :], probs[:, :, :], AX.X, ALU.max))
        step(nc.vector.tensor_tensor(self.eq[:, :, :], probs[:, :, :], along(top[:, :], E), ALU.is_equal))
        step(nc.vector.scalar_tensor_tensor(self.cand[:, :, :], self.eq[:, :, :], -100.0,
                                            over(c["iota_far"][:, 0:E], NB), ALU.mult, ALU.add))
        step(nc.vector.tensor_reduce(self.at[:, :], self.cand[:, :, :], AX.X, ALU.min))
        step(nc.vector.tensor_tensor(onehot[:, :, :], over(c["iota"][:, 0:E], NB), along(self.at[:, :], E),
                                     ALU.is_equal))

    def top_two(self, step):
        nc = self.k.nc
        self.pick(step, self.probs, self.top1, self.first)
        step(nc.vector.scalar_tensor_tensor(self.left[:, :, :], self.first[:, :, :], -2.0, self.probs[:, :, :],
                                            ALU.mult, ALU.add))
        self.pick(step, self.left, self.top2, self.second)

    def masked(self, step, weights):
        nc = self.k.nc
        step(nc.vector.tensor_tensor(self.eq[:, :, :], self.first[:, :, :], self.second[:, :, :], ALU.add))
        step(nc.vector.tensor_tensor(weights, self.probs[:, :, :], self.eq[:, :, :], ALU.mult))


class SmallHeads:

    def __init__(self, k, st, H, hd, parts, scale, mask=None, turn=True):
        self.k, self.nc, self.H, self.hd, self.scale, self.mask, self.turn = k, k.nc, H, hd, scale, mask, turn
        self.parts = parts
        self.VW = len(parts) * (hd + 1)
        self.G = H // 4
        self.HC = H // KC
        self.qT, self.kT = st.sb("qT", [P, KC, TOK]), st.sb("kT", [P, KC, TOK])
        self.v = st.sb("v", [P, NB, H, self.VW])
        self.qb = st.sb("qb", [P, KC, P])
        self.km = st.sb("km", [P, H, P])
        self.sm = st.sb("sm", [P, 2, 4, P])
        self.mx = st.sb("mx", [P, 2, 4, len(parts)])
        self.p = st.sb("p", [P, 2, 4 * P])
        self.pT = st.sb("pT", [P, 2, 4 * P])
        self.rec = st.sb("rec", [P, H, len(parts)])
        self.on = st.sb("on", [P, H, hd])
        self.on2 = st.sb("on2", [P, H, hd])
        self.onT = st.sb("onT", [P, KC, P])
        n = ("qb_ready", "km_ready", "scores_psum", "scores_read", "shifted", "exp_ready", "pT_psum", "pT_ready",
             "pv_done", "o_read", "o_norm", "oT_psum", "oT_ready", "y_psum", "y_added", "attn_step", "max_ready",
             "masked")
        (self.s_qb, self.s_km, self.s_s, self.s_sread, self.s_sm, self.s_p, self.s_pTp, self.s_pT, self.s_pv,
         self.s_oread, self.s_on, self.s_oTp, self.s_oT, self.s_y, self.s_x, self.s_step, self.s_mx,
         self.s_masked) = (st.sem(m) for m in n)

    def run(self, eng, body, tail):
        body(eng, 0, False)
        body(eng, 1, True)
        with eng.Fori(2, NB) as j:
            body(eng, j, True)
        tail(eng)


    def scores(self, pe, j, g):
        c = g // (self.G // KC)
        if g % (self.G // KC) == 0:
            pe.wait_ge(self.s_km, j * KC + c + 1)
            if c == 0:
                pe.wait_ge(self.s_qb, j + 1)
        done = j * self.G + g
        since(pe, self.s_sread, done - 1)
        rhs = self.km[:, 4 * g:4 * g + 4, :].rearrange("p h t -> p (h t)")
        self.nc.tensor.matmul(self.k.ps[g % 2][:, :], self.qb[:, c, :], rhs, start=True, stop=True).then_inc(self.s_s, 1)

    def turn_probs(self, pe, j, g):
        done = j * self.G + g
        pe.wait_ge(self.s_p, done + 1)
        since(pe, self.s_pT, done - 1)
        for h in range(4):
            mm = self.nc.tensor.transpose(self.k.ps[2 + g % 2][:, h * P:(h + 1) * P],
                                          self.p[:, g % 2, h * P:(h + 1) * P], self.k.ident)
        mm.then_inc(self.s_pTp, 1)

    def o_bank(self, h):
        per = self.H if self.H * self.VW <= HALF else self.H // 2
        return self.k.ps[4 + h // per], (h % per) * self.VW

    def values(self, pe, j, g):
        pe.wait_ge(self.s_pT, j * self.G + g + 1)
        if g == 0:
            since(pe, self.s_oread, j)
        for h in range(4 * g, 4 * g + 4):
            bank, at = self.o_bank(h)
            mm = self.nc.tensor.matmul(bank[:, at:at + self.VW], self.pT[:, g % 2, (h % 4) * P:(h % 4 + 1) * P],
                                       self.v[:, bass.ds(j, 1), h, :].rearrange("p a n -> p (a n)"),
                                       start=True, stop=True)
        mm.then_inc(self.s_pv, 1)

    def turn_out(self, pe, j):
        pe.wait_ge(self.s_on, j)
        for c in range(KC):
            mm = self.nc.tensor.transpose(self.k.ps[6][:, c * P:(c + 1) * P],
                                          self.on[:, c * self.HC:(c + 1) * self.HC, :].rearrange("p h d -> p (h d)"),
                                          self.k.ident)
        mm.then_inc(self.s_oTp, 1)

    def project(self, pe, j):
        since(pe, self.s_x, j - 1)
        if self.turn:
            pe.wait_ge(self.s_oT, j)
        else:
            pe.wait_ge(self.s_on, j)
        for c in range(KC):
            if self.turn:
                lhsT = self.onT[:, c, :]
            else:
                lhsT = self.on[:, :, :].rearrange("p h d -> p (h d)")[:, c:C:KC]
            mm = self.nc.tensor.matmul(self.k.ps[6][:, C:2 * C], lhsT, self.w_out[:, c, :],
                                       start=(c == 0), stop=(c == KC - 1))
        mm.then_inc(self.s_y, 1)

    def pe(self, pe, j, prev):
        G = self.G
        self.scores(pe, j, 0)
        self.scores(pe, j, 1)
        if prev and self.turn:
            self.turn_out(pe, j)
        for g in range(G):
            self.turn_probs(pe, j, g)
            if g + 2 < G:
                self.scores(pe, j, g + 2)
            if g == 0 and prev:
                self.project(pe, j)
            if g:
                self.values(pe, j, g - 1)
        self.values(pe, j, G - 1)

    def pe_tail(self, pe):
        if self.turn:
            self.turn_out(pe, NB)
        self.project(pe, NB)


    def act(self, act, j, prev):
        nc, G, ps = self.nc, self.G, self.k.ps
        for g in range(G + 1):
            if g < G:
                done = j * G + g
                act.wait_ge(self.s_sm, done + 1)
                since(act, self.s_pTp, done - 1)
                nc.scalar.activation(self.p[:, g % 2, :], self.sm[:, g % 2, :, :].rearrange("p h t -> p (h t)"),
                                     ACT.Exp, scale=self.scale).then_inc(self.s_p, 1)
            if g == 0 and prev and self.turn:
                self.copy_out(act, j)
            if g:
                done = j * G + g - 1
                act.wait_ge(self.s_pTp, done + 1)
                since(act, self.s_pv, done - 1)
                nc.scalar.activation(self.pT[:, (g - 1) % 2, :], ps[2 + (g - 1) % 2][:, :],
                                     ACT.Copy).then_inc(self.s_pT, 1)

    def copy_out(self, act, j):
        act.wait_ge(self.s_oTp, j)
        since(act, self.s_y, j - 1)
        self.nc.scalar.activation(self.onT[:, :, :], self.k.ps[6][:, 0:C].rearrange("p (c t) -> p c t", c=KC),
                                  ACT.Copy).then_inc(self.s_oT, 1)

    def act_tail(self, act):
        if self.turn:
            self.copy_out(act, NB)


    def softmax(self, dve, j, g):
        nc, k = self.nc, self.k
        done = j * self.G + g
        s = self.k.ps[g % 2][:, :].rearrange("p (h t) -> p h t", h=4)
        sm, mx = self.sm[:, g % 2, :, :], self.mx[:, g % 2, :, :]
        dve.wait_ge(self.s_s, done + 1)
        since(dve, self.s_p, done - 1)
        if self.mask is not None:
            nc.vector.tensor_tensor(sm, s, over(self.mask, 4), ALU.add).then_inc(self.s_sread, 1)
            dve.wait_ge(self.s_sread, done + 1)
            s = sm
        n = len(self.parts)
        for i, (a, b) in enumerate(self.parts):
            nc.vector.tensor_reduce(mx[:, :, i], s[:, :, a:b], AX.X, ALU.max).then_inc(self.s_mx, 1)
        for i, (a, b) in enumerate(self.parts):
            dve.wait_ge(self.s_mx, done * n + i + 1)
            ins = nc.vector.tensor_tensor(sm[:, :, a:b], s[:, :, a:b], along(mx[:, :, i], b - a), ALU.subtract)
        if self.mask is None:
            ins.then_inc(self.s_sread, 1)
            dve.wait_ge(self.s_sread, done + 1)
            dve.sem_inc(self.s_sm, 1)
        else:
            ins.then_inc(self.s_sm, 1)

    def normalise(self, dve, j):
        nc, n = self.nc, len(self.parts)
        dve.wait_ge(self.s_pv, j * self.G)
        if self.turn:
            since(dve, self.s_oTp, j - 1)
        else:
            since(dve, self.s_y, j - 1)
        banks = 1 if self.H * self.VW <= HALF else 2
        hb = self.H // banks
        D = self.hd + 1
        step = self.step
        for b in range(banks):
            o = self.k.ps[4 + b][:, 0:hb * self.VW].rearrange("p (h a d) -> p h a d", h=hb, a=n)
            hs = slice(b * hb, (b + 1) * hb)
            step(nc.vector.reciprocal(self.rec[:, hs, :], o[:, :, :, self.hd]))
            step(nc.vector.tensor_tensor(self.on[:, hs, :], o[:, :, 0, 0:self.hd],
                                         along(self.rec[:, hs, 0], self.hd), ALU.mult))
            if n == 2:
                step(nc.vector.tensor_tensor(self.on2[:, hs, :], o[:, :, 1, 0:self.hd],
                                             along(self.rec[:, hs, 1], self.hd), ALU.mult))
                step(nc.vector.tensor_tensor(self.on[:, hs, :], self.on[:, hs, :], self.on2[:, hs, :], ALU.add))
        dve.sem_inc(self.s_on, 1)
        dve.sem_inc(self.s_oread, 1)

    def add(self, dve, j):
        self.nc_add(dve, j)

    def nc_add(self, dve, j):
        xb = self.k.x[:, bass.ds(j - 1, 1), :].rearrange("p a n -> p (a n)")
        dve.wait_ge(self.s_y, j)
        self.nc.vector.tensor_tensor(xb, xb, self.k.ps[6][:, C:2 * C], ALU.add).then_inc(self.s_x, 1)

    def dve(self, dve, j, prev):
        self.step.restart()
        if prev:
            self.normalise(dve, j)
        for g in range(self.G):
            self.softmax(dve, j, g)
            if g == 1 and prev:
                self.nc_add(dve, j)

    def dve_tail(self, dve):
        self.step.restart()
        self.normalise(dve, NB)
        self.nc_add(dve, NB)


    def pool(self, pool, j, prev):
        nc, G = self.nc, self.G
        for c in range(KC):
            if prev:
                pool.wait_ge(self.s_s, j * G - (KC - 1 - c) * (G // KC))
            if c == 0:
                if prev:
                    pool.wait_ge(self.s_s, j * G)
                nc.gpsimd.tensor_copy(self.qb[:, :, :], self.qT[:, :, bass.ds(j * P, P)]).then_inc(self.s_qb, 1)
            hs = slice(c * self.HC, (c + 1) * self.HC)
            nc.gpsimd.tensor_tensor(self.km[:, hs, :],
                                    over(self.kT[:, c, bass.ds(j * P, P)], self.HC),
                                    along(self.in_head, P), ALU.mult).then_inc(self.s_km, 1)


class Turns:

    def __init__(self, k, uses, readers, late, N):
        assert len(uses) % 4 == 0
        self.k, self.uses, self.readers, self.late, self.N = k, uses, readers, late, N

    def bank(self, use):
        return self.k.ps[4 + self.uses.index(use) % 4]

    def free(self, pe, j, use):
        at, made = self.uses.index(use), j
        while True:
            at -= 4
            if at < 0:
                at, made = at + len(self.uses), made - 1
            name, n = self.uses[at]
            late = name is not None and name in self.late
            if isinstance(made, int) and made < 0:
                return
            if name is None or isinstance(made, int) and (made == 0 if late else made == self.N):
                continue
            sem, signals, before = self.readers[name]
            pe.wait_ge(sem, (made - 1 if late else made) * signals + before + n + 1)
            return


def passes(eng, N, body):
    for s in range(2):
        body(eng, s, s, 0)
    with eng.Fori(1, N // 2) as i:
        for s in range(2):
            body(eng, i * 2 + s, s, i)
    body(eng, N, 0, N // 2)


class WideHeads:

    def __init__(self, k, st, turns):
        self.k, self.nc, self.turns = k, k.nc, turns
        self.qT, self.kT = st.sb("qT", [P, TOK]), st.sb("kT", [P, TOK])
        self.v = st.sb("v", [P, 2, TOK])
        self.mx = st.sb("mx", [P, 2, 4])
        self.nb = st.sb("minus_max", [P, 2, 4])
        self.p = st.sb("p", [P, 2, HALF])
        self.sum = st.sb("sum", [P, 2, 4])
        self.pT = st.sb("pT", [P, 2, HALF])
        self.oT = st.sb("oT", [P, 2, HALF])
        self.zero = st.sb("zero", [P, P])
        n = ("s_psum", "bias_ready", "exp_done", "probs_ready", "pT_psum", "pT_ready", "oT_psum", "oT_ready", "y_added",
             "zero_set", "back_step")
        (self.s_s, self.s_nb, self.s_exp, self.s_p, self.s_pTp, self.s_pT, self.s_oTp, self.s_oT, self.s_y,
         self.s_zero, self.s_step) = (st.sem(m) for m in n)

    def clear_sums(self, pe):
        pe.wait_ge(self.s_zero, 1)
        for n in range(4):
            self.nc.tensor.matmul(self.k.ps[n][:, :], self.zero[:, :], self.k.xnT[:, 0, 0:HALF], start=True,
                                  stop=False, skip_group_check=True)


    def scores(self, pe, j, tag):
        nc, tr = self.nc, self.turns
        for h in range(2):
            tr.free(pe, j, ("s" + tag, h))
            for b in range(4):
                t = slice((4 * h + b) * P, (4 * h + b + 1) * P)
                mm = nc.tensor.matmul(tr.bank(("s" + tag, h))[:, b * P:(b + 1) * P], self.qT[:, t], self.kT[:, t],
                                      start=True, stop=True)
            mm.then_inc(self.s_s, 1)

    def turn_probs(self, pe, j, u, tag):
        nc, tr = self.nc, self.turns
        for h in range(2):
            tr.free(pe, j, ("t" + tag, h))
            pe.wait_ge(self.s_p, u * 2 + h + 1)
            for b in range(4):
                mm = nc.tensor.transpose(tr.bank(("t" + tag, h))[:, b * P:(b + 1) * P],
                                         self.p[:, h, b * P:(b + 1) * P], self.k.ident)
            mm.then_inc(self.s_pTp, 1)

    def values(self, pe, j, u, tag, v):
        nc, tr = self.nc, self.turns
        for h in range(2):
            tr.free(pe, j, ("o" + tag, h))
            pe.wait_ge(self.s_pT, u * 2 + h + 1)
            for b in range(4):
                t = slice((4 * h + b) * P, (4 * h + b + 1) * P)
                mm = nc.tensor.matmul(tr.bank(("o" + tag, h))[:, b * P:(b + 1) * P], v[:, t],
                                      self.pT[:, h, b * P:(b + 1) * P], start=True, stop=True)
            mm.then_inc(self.s_oTp, 1)

    def project(self, pe, u, wo):
        nc = self.nc
        for h in range(2):
            pe.wait_ge(self.s_oT, u * 2 + h + 1)
            for b in range(4):
                g = 4 * h + b
                mm = nc.tensor.matmul(self.k.ps[g // 2][:, (g % 2) * C:(g % 2 + 1) * C],
                                      self.oT[:, h, b * P:(b + 1) * P], wo, start=False, stop=False,
                                      skip_group_check=True)
            mm.then_inc(self.s_y, 1)


    def exponent(self, act, u, tag, scale):
        nc, tr = self.nc, self.turns
        for h in range(2):
            act.wait_ge(self.s_nb, u * 2 + h + 1)
            for b in range(4):
                src = self.scored(tr, tag, h)
                ins = nc.scalar.activation(self.p[:, h, b * P:(b + 1) * P], src[:, b * P:(b + 1) * P], ACT.Exp,
                                           bias=self.nb[:, h, b:b + 1], scale=scale(4 * h + b),
                                           accum_out=self.sum[:, h, b:b + 1])
            ins.then_inc(self.s_exp, 1)

    def copy_out(self, act, u, tag):
        nc, tr = self.nc, self.turns
        for h in range(2):
            act.wait_ge(self.s_oTp, u * 2 + h + 1)
            since(act, self.s_y, 2 * u - 1 + h)
            nc.scalar.activation(self.oT[:, h, :], tr.bank(("o" + tag, h))[:, :], ACT.Copy).then_inc(self.s_oT, 1)

    def scored(self, tr, tag, h):
        return tr.bank(("s" + tag, h))

    def dve_probs(self, dve, step, u, h):
        nc = self.nc
        dve.wait_ge(self.s_exp, u * 2 + h + 1)
        step(nc.vector.reciprocal(self.sum[:, h, :], self.sum[:, h, :]))
        p3 = self.p[:, h, :].rearrange("p (b t) -> p b t", b=4)
        nc.vector.tensor_tensor(p3, p3, along(self.sum[:, h, :], P), ALU.mult).then_inc(self.s_p, 1)

    def dve_turned(self, dve, u, tag, h):
        dve.wait_ge(self.s_pTp, u * 2 + h + 1)
        self.nc.vector.tensor_copy(self.pT[:, h, :], self.turns.bank(("t" + tag, h))[:, :]).then_inc(self.s_pT, 1)

    def add(self, dve):
        x = self.k.x
        for n in range(4):
            self.nc.vector.tensor_tensor(x[:, 2 * n:2 * n + 2, :], x[:, 2 * n:2 * n + 2, :],
                                         self.k.ps[n][:, :].rearrange("p (b n) -> p b n", b=2), ALU.add)


def rsqrt(nc, step, v, y, t):
    I32 = mybir.dt.int32
    step(nc.vector.tensor_scalar(t.bitcast(I32), v.bitcast(I32), 1, None, ALU.logical_shift_right))
    step(nc.vector.tensor_scalar(y.bitcast(I32), t.bitcast(I32), -1.0, 1597463007.0, ALU.mult, ALU.add))
    for _ in range(4):
        step(nc.vector.tensor_tensor(t, y, y, ALU.mult))
        step(nc.vector.scalar_tensor_tensor(t, t, -0.5, v, ALU.mult, ALU.mult))
        step(nc.vector.scalar_tensor_tensor(y, t, 1.5, y, ALU.add, ALU.mult))


def l0_attn(k):
    nc, x, xnT, ps = k.nc, k.x, k.xnT, k.ps
    H, hd = 16, 16
    with Stage(k, "L0a", k.now) as st:
        img = k.now.img
        w = sbuf_views(img, *k.parts["L0a"])
        wq, wk, wv, wp = (w[n].rearrange("p (k n) -> p k n", k=KC) for n in ("wq", "wk", "wv", "wp"))
        a = SmallHeads(k, st, H, hd, [(0, P)], 1.0 / hd ** 0.5, mask=k.c["causal"], turn=False)
        a.w_out, a.in_head = wp, k.c["in_head16"]
        s_w = k.now.s_img
        s_qk, s_v = st.sem("qk_psum"), st.sem("v_psum")
        s_in, s_bias, s_ones, s_vin = st.sem("qk_ready"), st.sem("bias_added"), st.sem("ones_set"), st.sem("v_ready")
        with nc.Block() as block:

            @block.tensor
            def _(pe):
                pe.wait_ge(s_w, 16)
                for n, wm in enumerate((wq, wk)):
                    for c in range(KC):
                        for h in range(2):
                            bank = 4 * n + 2 * c + h
                            for kc in range(KC):
                                mm = nc.tensor.matmul(ps[bank][:, :], wm[:, kc, c * P:(c + 1) * P],
                                                      xnT[:, kc, h * HALF:(h + 1) * HALF],
                                                      start=(kc == 0), stop=(kc == KC - 1))
                            mm.then_inc(s_qk, 1)
                for n in range(4):
                    pe.wait_ge(s_in, n + 1)
                    for b in (2 * n, 2 * n + 1):
                        for kc in range(KC):
                            mm = nc.tensor.matmul(ps[n][:, (b % 2) * C:(b % 2 + 1) * C],
                                                  xnT[:, kc, b * P:(b + 1) * P], wv[:, kc, :],
                                                  start=(kc == 0), stop=(kc == KC - 1))
                    mm.then_inc(s_v, 1)
                pe.wait_ge(s_in, 8)
                pe.wait_ge(s_vin, 4)
                a.run(pe, a.pe, a.pe_tail)

            @block.scalar
            def _(act):
                for n, (dst, b) in enumerate(((a.qT, w["bq"]), (a.kT, w["bk"]))):
                    for c in range(KC):
                        for h in range(2):
                            act.wait_ge(s_qk, 4 * n + 2 * c + h + 1)
                            nc.scalar.activation(dst[:, c, h * HALF:(h + 1) * HALF], ps[4 * n + 2 * c + h][:, :],
                                                 ACT.Identity, bias=b[:, c:c + 1]).then_inc(s_in, 1)
                a.run(act, a.act, a.act_tail)

            @block.vector
            def _(dve):
                a.step = Chain(dve, a.s_step)
                dve.wait_ge(s_w, 16)
                for n in range(4):
                    dve.wait_ge(s_v, n + 1)
                    for j in range(2):
                        ins = nc.vector.tensor_tensor(
                            a.v[:, 2 * n + j, :, 0:hd],
                            ps[n][:, j * C:(j + 1) * C].rearrange("p (h d) -> p h d", h=H),
                            w["bv"].rearrange("p (h d) -> p h d", h=H), ALU.add)
                    ins.then_inc(s_vin, 1)
                dve.wait_ge(s_bias, 1)
                a.run(dve, a.dve, a.dve_tail)

            @block.gpsimd
            def _(pool):
                nc.gpsimd.memset(a.v[:, :, :, hd:hd + 1], 1.0).then_inc(s_ones, 1)
                pool.wait_ge(s_w, 16)
                nc.gpsimd.tensor_tensor(x[:, :, :], x[:, :, :], over(w["bp"], NB), ALU.add).then_inc(s_bias, 1)
                pool.wait_ge(s_in, 8)
                a.run(pool, a.pool, lambda eng: None)


def l0_xattn(k):
    nc, x, xnT, ctxT, ps = k.nc, k.x, k.xnT, k.ctxT, k.ps
    H, hd = 32, 8
    PAIRS = hd // 2
    with Stage(k, "L0x", k.now) as st:
        img = k.now.img
        w = sbuf_views(img, *k.parts["L0x"])
        wq, wout = (w[n].rearrange("p (k n) -> p k n", k=KC) for n in ("wq", "wout"))
        wk, wv = w["wkv"][:, 0:C], w["wkv"][:, C:2 * C]
        a = SmallHeads(k, st, H, hd, [(0, P)], 1.0 / hd ** 0.5)
        a.w_out, a.in_head = wout, k.c["in_head8"]
        ang = st.sb("ang", [P, 2, NB, PAIRS])
        turns = st.sb("turns", [P, 2, NB, PAIRS])
        trig = st.sb("trig", [P, 2, NB, PAIRS])
        cosd = st.sb("cosd", [P, NB, PAIRS, 2])
        sind = st.sb("sind", [P, NB, PAIRS, 2])
        rot = st.sb("rot", [P, 2, 2 * C])
        crossed = st.sb("crossed", [P, 2, 2 * C])
        s_w = k.now.s_img
        s_qk, s_v = st.sem("qk_psum"), st.sem("v_psum")
        s_ang, s_trig, s_read, s_rot = st.sem("angles"), st.sem("trig_ready"), st.sem("qk_read"), st.sem("rotated")
        s_t, s_in, s_vin = st.sem("qkT_psum"), st.sem("qkT_ready"), st.sem("v_ready")
        s_ones, s_bias = st.sem("ones_set"), st.sem("bias_added")
        with nc.Block() as block:

            @block.tensor
            def _(pe):
                pe.wait_ge(s_w, 16)

                def turn(b):
                    pe.wait_ge(s_rot, b + 1)
                    if b >= 2:
                        pe.wait_ge(s_in, b - 1)
                    for n in range(4):
                        mm = nc.tensor.transpose(ps[4 + b % 2][:, n * P:(n + 1) * P],
                                                 rot[:, b % 2, n * P:(n + 1) * P], k.ident)
                    mm.then_inc(s_t, 1)

                for b in range(NB):
                    t = slice(b * P, (b + 1) * P)
                    if b >= 2:
                        pe.wait_ge(s_read, b - 1)
                        pe.wait_ge(s_vin, b - 1)
                    for kc in range(KC):
                        nc.tensor.matmul(ps[b % 2][:, 0:C], xnT[:, kc, t], wq[:, kc, :], start=(kc == 0),
                                         stop=(kc == KC - 1))
                    nc.tensor.matmul(ps[b % 2][:, C:2 * C], ctxT[:, t], wk, start=True, stop=True).then_inc(s_qk, 1)
                    nc.tensor.matmul(ps[2 + b % 2][:, 0:C], ctxT[:, t], wv, start=True, stop=True).then_inc(s_v, 1)
                    if b:
                        turn(b - 1)
                turn(NB - 1)
                pe.wait_ge(s_in, NB)
                pe.wait_ge(s_vin, NB)
                a.run(pe, a.pe, a.pe_tail)

            @block.scalar
            def _(act):
                act.wait_ge(s_ang, 1)
                nc.scalar.activation(trig[:, :, :, :], ang[:, :, :, :], ACT.Sin).then_inc(s_trig, 1)
                for b in range(NB):
                    act.wait_ge(s_v, b + 1)
                    nc.scalar.activation(a.v[:, b, :, 0:hd], ps[2 + b % 2][:, 0:C].rearrange("p (h d) -> p h d", h=H),
                                         ACT.Copy).then_inc(s_vin, 1)
                    act.wait_ge(s_t, b + 1)
                    bank = ps[4 + b % 2][:, :].rearrange("p (m c t) -> p m c t", m=2, c=KC)
                    nc.scalar.activation(a.qT[:, :, b * P:(b + 1) * P], bank[:, 0, :, :], ACT.Copy)
                    nc.scalar.activation(a.kT[:, :, b * P:(b + 1) * P], bank[:, 1, :, :], ACT.Copy).then_inc(s_in, 1)
                a.run(act, a.act, a.act_tail)

            @block.vector
            def _(dve):
                a.step = step = Chain(dve, a.s_step)
                dve.wait_ge(s_w, 16)
                pos = w["pos"].rearrange("p (b f) -> p b f", b=NB)
                step(nc.vector.tensor_tensor(ang[:, 0, :, :], pos, over(k.c["freq"], NB), ALU.mult))
                step(nc.vector.tensor_scalar(ang[:, 1, :, :], ang[:, 0, :, :], TWO_PI / 4, None, ALU.add))
                step(nc.vector.tensor_scalar(turns[:, :, :, :], ang[:, :, :, :], 1.0 / TWO_PI, ROUND,
                                             ALU.mult, ALU.add))
                step(nc.vector.tensor_scalar(turns[:, :, :, :], turns[:, :, :, :], ROUND, -TWO_PI,
                                             ALU.subtract, ALU.mult))
                step(nc.vector.tensor_tensor(ang[:, :, :, :], ang[:, :, :, :], turns[:, :, :, :], ALU.add))
                nc.vector.tensor_scalar(ang[:, :, :, :], ang[:, :, :, :], 3.1415925, -3.1415925, ALU.min,
                                        ALU.max).then_inc(s_ang, 1)
                dve.wait_ge(s_trig, 1)
                for n in range(2):
                    step(nc.vector.tensor_copy(cosd[:, :, :, n], trig[:, 1, :, :]))
                step(nc.vector.tensor_scalar(sind[:, :, :, 0], trig[:, 0, :, :], -1.0, None, ALU.mult))
                step(nc.vector.tensor_copy(sind[:, :, :, 1], trig[:, 0, :, :]))
                for b in range(NB):
                    q = ps[b % 2][:, :].rearrange("p (h f) -> p h f", f=hd)
                    q2 = ps[b % 2][:, :].rearrange("p (h f n) -> p h f n", f=PAIRS, n=2)
                    c2 = crossed[:, b % 2, :].rearrange("p (h f n) -> p h f n", f=PAIRS, n=2)
                    r = rot[:, b % 2, :].rearrange("p (h f) -> p h f", f=hd)
                    dve.wait_ge(s_qk, b + 1)
                    if b >= 2:
                        dve.wait_ge(s_t, b - 1)
                    step(nc.vector.tensor_tensor(r, q, over(cosd[:, b, :, :].rearrange("p f n -> p (f n)"), 2 * H),
                                                 ALU.mult))
                    step(nc.vector.tensor_tensor(c2[:, :, :, 0], q2[:, :, :, 1], over(sind[:, b, :, 0], 2 * H),
                                                 ALU.mult))
                    nc.vector.tensor_tensor(c2[:, :, :, 1], q2[:, :, :, 0], over(sind[:, b, :, 1], 2 * H),
                                            ALU.mult).then_inc(s_read, 1)
                    dve.wait_ge(s_read, b + 1)
                    nc.vector.tensor_tensor(rot[:, b % 2, :], rot[:, b % 2, :], crossed[:, b % 2, :],
                                            ALU.add).then_inc(s_rot, 1)
                dve.wait_ge(s_bias, 1)
                a.run(dve, a.dve, a.dve_tail)

            @block.gpsimd
            def _(pool):
                nc.gpsimd.memset(a.v[:, :, :, hd:hd + 1], 1.0).then_inc(s_ones, 1)
                pool.wait_ge(s_w, 16)
                nc.gpsimd.tensor_tensor(x[:, :, :], x[:, :, :], over(w["bout"], NB), ALU.add).then_inc(s_bias, 1)
                pool.wait_ge(s_in, NB)
                a.run(pool, a.pool, lambda eng: None)


def l0_ffn(k):
    nc, x, xn, ps = k.nc, k.x, k.xn, k.ps
    NH = 8
    H = NH * P
    MATS = ("gate", "val", "out")
    with Stage(k, "L0f", k.now) as st:
        img = k.now.img
        w = sbuf_views(img, *k.parts["L0f"])
        mats = img[:, 0:3 * KC * H]
        tern = st.sb("ternary", [P, 3 * KC * H], BF16)
        tgate = tern[:, 0:KC * H].rearrange("p (k n) -> p k n", k=KC)
        tval = tern[:, KC * H:2 * KC * H].rearrange("p (k n) -> p k n", k=KC)
        tout = tern[:, 2 * KC * H:].rearrange("p (k n) -> p k n", k=NH)
        magic = st.sb("magic", [P, 2])
        wsum = st.sb("wsum", [P, 3])
        gamma = st.sb("gamma_w", [P, 3])
        rgamma = st.sb("rgamma_w", [P, 3])
        identb = st.sb("identb", [P, P], BF16)
        gx = st.sb("gamma_x", [P, NB])
        rgx = st.sb("rgamma_x", [P, NB])
        xs = st.sb("x_scale", [P, NB])
        gscale = st.sb("gate_scale", [P, NB])
        vscale = st.sb("val_scale", [P, NB])
        xi = st.sb("x_int", [P, NB, C], BF16)
        xiT = st.sb("x_intT", [P, KC, TOK], BF16)
        g = st.sb("g", [P, 2, H])
        v = st.sb("v", [P, 2, H])
        hs = st.sb("h_rounded", [P, 2, H])
        hi = st.sb("h_int", [P, 2, H], BF16)
        hiT = st.sb("h_intT", [P, 2, H], BF16)
        gh = st.sb("gamma_h", [P, 2])
        rgh = st.sb("rgamma_h", [P, 2])
        hsc = st.sb("h_scale", [P, 2])
        osc = st.sb("out_scale", [P, 2])
        bank16 = [ps[i][:, :].bitcast(BF16) for i in range(8)]
        s_w = k.now.s_img
        s_magic, s_wsum, s_tot = st.sem("magic_set"), st.sem("w_abs_sums"), st.sem("w_totals")
        s_rg, s_wr, s_wc, s_tern = st.sem("rgamma_ready"), st.sem("w_rounded"), st.sem("w_clipped"), st.sem("ternary_ready")
        s_xi, s_xiT, s_xiTc, s_idb = st.sem("x_int_ready"), st.sem("x_intT_psum"), st.sem("x_intT_ready"), st.sem("identb")
        s_gv, s_gread, s_g, s_silu = st.sem("gate_val_psum"), st.sem("gate_val_read"), st.sem("g_ready"), st.sem("silu_ready")
        s_h, s_scale, s_hr, s_hi = st.sem("h_ready"), st.sem("scales_ready"), st.sem("h_rounded"), st.sem("h_int_ready")
        s_hT, s_hTc, s_y, s_x = st.sem("hT_psum"), st.sem("hT_ready"), st.sem("y_psum"), st.sem("x_added")
        s_dve, s_bias = st.sem("dve_step"), st.sem("bias_added")

        def batches(eng, front, back, back_first=False):

            def both(n, s):
                if back_first:
                    back(eng, n, 1 - s)
                front(eng, n, s)
                if not back_first:
                    back(eng, n, 1 - s)

            front(eng, 0, 0)
            both(1, 1)
            with eng.Fori(1, NB // 2) as i:
                for s in range(2):
                    both(i * 2 + s, s)
            back(eng, NB, 1)

        with nc.Block() as block:

            @block.gpsimd
            def _(pool):
                nc.gpsimd.memset(magic[:, 0:1], ROUND).then_inc(s_magic, 1)
                nc.gpsimd.memset(magic[:, 1:2], -ROUND).then_inc(s_magic, 1)
                nc.gpsimd.tensor_copy(identb[:, :], k.ident).then_inc(s_idb, 1)
                pool.wait_ge(s_w, 16)
                nc.gpsimd.tensor_tensor(x[:, :, :], x[:, :, :], over(w["out_b"], NB), ALU.add).then_inc(s_bias, 1)

            @block.tensor
            def _(pe):
                pe.wait_ge(s_wsum, 3)
                nc.tensor.matmul(ps[7][:, 0:3], k.c["ones"], wsum[:, :], start=True, stop=True).then_inc(s_tot, 1)
                pe.wait_ge(s_idb, 1)
                pe.wait_ge(s_xi, 1)
                for kc in range(KC):
                    for b in range(NB):
                        mm = nc.tensor.transpose(bank16[kc][:, b * P:(b + 1) * P], xi[:, b, kc * P:(kc + 1) * P],
                                                 identb[:, :])
                    mm.then_inc(s_xiT, 1)
                pe.wait_ge(s_xiTc, 2)
                pe.wait_ge(s_tern, 3)

                def front(pe, n, s):
                    if not (isinstance(n, int) and n == 0):
                        pe.wait_ge(s_gread, n)
                    xs_at = bass.ds(n * P, P)
                    for kc in range(KC):
                        for h in range(2):
                            for bank, t in ((h, tgate), (2 + h, tval)):
                                mm = nc.tensor.matmul(ps[bank][:, :], xiT[:, kc, xs_at],
                                                      t[:, kc, h * HALF:(h + 1) * HALF],
                                                      start=(kc == 0), stop=(kc == KC - 1))
                    mm.then_inc(s_gv, 1)

                def back(pe, n, s):
                    pe.wait_ge(s_hi, n)
                    for c in range(NH):
                        mm = nc.tensor.transpose(bank16[4 + s][:, c * P:(c + 1) * P],
                                                 hi[:, s, c * P:(c + 1) * P], identb[:, :])
                    mm.then_inc(s_hT, 1)
                    pe.wait_ge(s_hTc, n)
                    if not (isinstance(n, int) and n < 3):
                        pe.wait_ge(s_x, n - 2)
                    for c in range(NH):
                        mm = nc.tensor.matmul(ps[6 + s][:, 0:C], hiT[:, s, c * P:(c + 1) * P], tout[:, c, :],
                                              start=(c == 0), stop=(c == NH - 1))
                    mm.then_inc(s_y, 1)

                batches(pe, front, back)

            @block.scalar
            def _(act):
                act.wait_ge(s_rg, 1)
                act.wait_ge(s_magic, 2)
                for m in range(3):
                    t = slice(m * KC * H, (m + 1) * KC * H)
                    nc.scalar.activation(mats[:, t], mats[:, t], ACT.Identity, bias=magic[:, 0:1],
                                         scale=rgamma[:, m:m + 1]).then_inc(s_wr, 1)
                for m in range(3):
                    t = slice(m * KC * H, (m + 1) * KC * H)
                    act.wait_ge(s_wc, m + 1)
                    nc.scalar.activation(tern[:, t], mats[:, t], ACT.Identity, bias=magic[:, 1:2]).then_inc(s_tern, 1)

                def front(act, n, s):
                    act.wait_ge(s_g, n + 1)
                    nc.scalar.activation(g[:, s, :], g[:, s, :], ACT.Silu).then_inc(s_silu, 1)
                    act.wait_ge(s_scale, n + 1)
                    nc.scalar.activation(hs[:, s, :], g[:, s, :], ACT.Identity, bias=magic[:, 0:1],
                                         scale=hsc[:, s:s + 1]).then_inc(s_hr, 1)
                    act.wait_ge(s_hr, n + 1)
                    if not (isinstance(n, int) and n < 2):
                        act.wait_ge(s_hT, n - 1)
                    nc.scalar.activation(hi[:, s, :], hs[:, s, :], ACT.Identity,
                                         bias=magic[:, 1:2]).then_inc(s_hi, 1)

                def back(act, n, s):
                    act.wait_ge(s_hT, n)
                    nc.scalar.activation(hiT[:, s, :], bank16[4 + s], ACT.Copy).then_inc(s_hTc, 1)

                batches(act, front, back, back_first=True)

            @block.vector
            def _(dve):
                step = Chain(dve, s_dve)
                step(nc.vector.tensor_reduce(gx[:, :], xn[:, :, :], AX.X, ALU.max, apply_absolute_value=True))
                step(nc.vector.tensor_scalar(gx[:, :], gx[:, :], 1e-5, None, ALU.max))
                step(nc.vector.reciprocal(rgx[:, :], gx[:, :]))
                step(nc.vector.tensor_scalar(xs[:, :], rgx[:, :], 127.0, None, ALU.mult))
                step(nc.vector.tensor_tensor(xn[:, :, :], xn[:, :, :], along(xs[:, :], C), ALU.mult))
                step(nc.vector.tensor_scalar(xn[:, :, :], xn[:, :, :], ROUND, -ROUND, ALU.add, ALU.add))
                nc.vector.tensor_scalar(xi[:, :, :], xn[:, :, :], -128.0, 127.0, ALU.max, ALU.min).then_inc(s_xi, 1)
                dve.wait_ge(s_w, 16)
                for m in range(3):
                    nc.vector.tensor_reduce(wsum[:, m:m + 1], mats[:, m * KC * H:(m + 1) * KC * H], AX.X, ALU.add,
                                            apply_absolute_value=True).then_inc(s_wsum, 1)
                dve.wait_ge(s_tot, 1)
                step(nc.vector.tensor_scalar(gamma[:, :], ps[7][:, 0:3], 1.0 / (H * C), 1e-5, ALU.mult, ALU.max))
                nc.vector.reciprocal(rgamma[:, :], gamma[:, :]).then_inc(s_rg, 1)
                step(nc.vector.tensor_scalar(gscale[:, :], gx[:, :], gamma[:, 0:1], 1.0 / 127.0, ALU.mult, ALU.mult))
                step(nc.vector.tensor_scalar(vscale[:, :], gx[:, :], gamma[:, 1:2], 1.0 / 127.0, ALU.mult, ALU.mult))
                for m in range(3):
                    t = slice(m * KC * H, (m + 1) * KC * H)
                    dve.wait_ge(s_wr, m + 1)
                    nc.vector.tensor_scalar(mats[:, t], mats[:, t], ROUND - 1.0, ROUND + 1.0, ALU.max,
                                            ALU.min).then_inc(s_wc, 1)
                for kc in range(KC):
                    dve.wait_ge(s_xiT, kc + 1)
                    nc.vector.tensor_copy(xiT[:, kc, :], bank16[kc]).then_inc(s_xiTc, 1)
                dve.wait_ge(s_bias, 1)

                def front(dve, n, s):
                    step.restart()
                    dve.wait_ge(s_gv, n + 1)
                    if not (isinstance(n, int) and n < 2):
                        dve.wait_ge(s_hr, n - 1)
                    gs = slice(s, s + 1)
                    for h in range(2):
                        ins = nc.vector.scalar_tensor_tensor(
                            g[:, s, h * HALF:(h + 1) * HALF], ps[h][:, :], gscale[:, bass.ds(n, 1)],
                            w["gate_b"][:, h * HALF:(h + 1) * HALF], ALU.mult, ALU.add)
                    ins.then_inc(s_g, 1)
                    for h in range(2):
                        ins = nc.vector.scalar_tensor_tensor(
                            v[:, s, h * HALF:(h + 1) * HALF], ps[2 + h][:, :], vscale[:, bass.ds(n, 1)],
                            w["val_b"][:, h * HALF:(h + 1) * HALF], ALU.mult, ALU.add)
                    ins.then_inc(s_gread, 1)
                    dve.wait_ge(s_gread, n + 1)
                    dve.wait_ge(s_silu, n + 1)
                    step(nc.vector.tensor_tensor(g[:, s, :], g[:, s, :], v[:, s, :], ALU.mult))
                    step(nc.vector.tensor_reduce(gh[:, gs], g[:, s, :], AX.X, ALU.max, apply_absolute_value=True))
                    step(nc.vector.tensor_scalar(gh[:, gs], gh[:, gs], 1e-5, None, ALU.max))
                    step(nc.vector.reciprocal(rgh[:, gs], gh[:, gs]))
                    nc.vector.tensor_scalar(hsc[:, gs], rgh[:, gs], 127.0, None, ALU.mult).then_inc(s_scale, 1)
                    if not (isinstance(n, int) and n < 2):
                        dve.wait_ge(s_x, n - 1)
                    step(nc.vector.tensor_scalar(osc[:, gs], gh[:, gs], gamma[:, 2:3], 1.0 / 127.0,
                                                 ALU.mult, ALU.mult))

                def back(dve, n, s):
                    xb = x[:, bass.ds(n - 1, 1), :].rearrange("p a n -> p (a n)")
                    dve.wait_ge(s_y, n)
                    nc.vector.scalar_tensor_tensor(xb, ps[6 + s][:, 0:C], osc[:, s:s + 1], xb,
                                                   ALU.mult, ALU.add).then_inc(s_x, 1)

                batches(dve, front, back)


def l1_attn(k):
    nc, x, xnT, ps = k.nc, k.x, k.xnT, k.ps
    H, NF = 16, 9
    F = 2 * H * NF
    CH = [(0, P), (P, 2 * P), (2 * P, F)]
    with Stage(k, "L1a", k.now) as st:
        img = k.now.img
        w = sbuf_views(img, *k.parts["L1a"])
        wq, wkv, woT, fwd, inv = (w[n].rearrange("p (k n) -> p k n", k=KC) for n in ("wq", "wkv", "woT", "fwd", "inv"))
        wf = st.sb("wf", [P, KC, 2, F])
        gw = st.sb("gw", [P, 3, C])
        spec = st.sb("spec", [P, NB, 2, F])
        sq = st.sb("squares", [P, 2, 2, F])
        ss = st.sb("square_sums", [P, NB, 2, H])
        rn = st.sb("rnorm", [P, NB, 2, H])
        t1 = st.sb("t1", [P, 2, 2, F // 2])
        t2 = st.sb("t2", [P, 2, 2, F // 2])
        pr = st.sb("product", [P, 2, F])
        prT = st.sb("productT", [P, 2, 3, P])
        s_w = k.now.s_img
        s_wf, s_wfc = st.sem("wf_psum"), st.sem("wf_ready")
        s_sp, s_spc, s_sq, s_ss = st.sem("spec_psum"), st.sem("spec_ready"), st.sem("squared"), st.sem("sums_ready")
        s_inv, s_rn, s_n, s_cum = st.sem("inverse"), st.sem("rnorm_ready"), st.sem("normed"), st.sem("cum_psum")
        s_cread, s_pr, s_prT, s_prTc = st.sem("cum_read"), st.sem("product_ready"), st.sem("prT_psum"), st.sem("prT_ready")
        s_y, s_x, s_dve = st.sem("y_psum"), st.sem("x_added"), st.sem("dve_step")
        with nc.Block() as block:

            @block.tensor
            def _(pe):
                pe.wait_ge(s_w, 16)
                for m, wm in enumerate((wq, wkv)):
                    for c in range(KC):
                        for ko in range(KC):
                            mm = nc.tensor.matmul(ps[2 * m + c][:, 0:F], wm[:, ko, c * P:(c + 1) * P], fwd[:, ko, :],
                                                  start=(ko == 0), stop=(ko == KC - 1))
                        mm.then_inc(s_wf, 1)
                for n, (f0, f1) in enumerate(CH):
                    for kv in range(KC):
                        mm = nc.tensor.matmul(ps[4 + n][0:f1 - f0, 0:C], inv[:, kv, f0:f1], woT[:, kv, :],
                                              start=(kv == 0), stop=(kv == KC - 1))
                    mm.then_inc(s_wf, 1)
                pe.wait_ge(s_wfc, 7)
                for b in range(NB):
                    for m in range(2):
                        if b >= 2:
                            pe.wait_ge(s_spc, 2 * (b - 2) + m + 1)
                        for kc in range(KC):
                            mm = nc.tensor.matmul(ps[2 * (b % 2) + m][:, 0:F], xnT[:, kc, b * P:(b + 1) * P],
                                                  wf[:, kc, m, :], start=(kc == 0), stop=(kc == KC - 1))
                        mm.then_inc(s_sp, 1)

                def cumulate(b):
                    pe.wait_ge(s_n, b + 1)
                    if b >= 2:
                        pe.wait_ge(s_cread, b - 1)
                    nc.tensor.matmul(ps[4 + b % 2][:, 0:F], k.c["triu"], spec[:, b, 1, :], start=True,
                                     stop=True).then_inc(s_cum, 1)

                def turn(b):
                    pe.wait_ge(s_pr, b + 1)
                    if b >= 2:
                        pe.wait_ge(s_prTc, b - 1)
                    for n, (f0, f1) in enumerate(CH):
                        mm = nc.tensor.transpose(ps[6 + b % 2][0:f1 - f0, n * P:(n + 1) * P], pr[:, b % 2, f0:f1],
                                                 k.ident)
                    mm.then_inc(s_prT, 1)

                def out(b):
                    pe.wait_ge(s_prTc, b + 1)
                    if b >= 2:
                        pe.wait_ge(s_x, b - 1)
                    for n, (f0, f1) in enumerate(CH):
                        mm = nc.tensor.matmul(ps[b % 2][:, 0:C], prT[0:f1 - f0, b % 2, n, :], gw[0:f1 - f0, n, :],
                                              start=(n == 0), stop=(n == 2))
                    mm.then_inc(s_y, 1)

                pe.wait_ge(s_spc, 2 * NB)
                pe.wait_ge(s_sq, 2 * NB)
                for b in range(NB + 2):
                    if b < NB:
                        cumulate(b)
                    if 1 <= b <= NB:
                        turn(b - 1)
                    if b >= 2:
                        out(b - 2)

            @block.scalar
            def _(act):
                for n in range(4):
                    act.wait_ge(s_wf, n + 1)
                    nc.scalar.activation(wf[:, n % 2, n // 2, :], ps[n][:, 0:F], ACT.Copy).then_inc(s_wfc, 1)
                for n, (f0, f1) in enumerate(CH):
                    act.wait_ge(s_wf, 4 + n + 1)
                    nc.scalar.activation(gw[0:f1 - f0, n, :], ps[4 + n][0:f1 - f0, 0:C], ACT.Copy).then_inc(s_wfc, 1)
                for b in range(NB):
                    for m in range(2):
                        act.wait_ge(s_spc, 2 * b + m + 1)
                        if b >= 2:
                            act.wait_ge(s_ss, 2 * (b - 2) + m + 1)
                        nc.scalar.activation(sq[:, b % 2, m, :], spec[:, b, m, :], ACT.Square).then_inc(s_sq, 1)
                act.wait_ge(s_inv, 1)
                nc.scalar.activation(rn[:, :, :, :], ss[:, :, :, :], ACT.Sqrt).then_inc(s_rn, 1)
                for b in range(NB):
                    act.wait_ge(s_prT, b + 1)
                    if b >= 2:
                        act.wait_ge(s_y, b - 1)
                    nc.scalar.activation(prT[:, b % 2, 0:2, :], ps[6 + b % 2][:, 0:2 * P].rearrange(
                        "p (n t) -> p n t", n=2), ACT.Copy)
                    nc.scalar.activation(prT[0:F - 2 * P, b % 2, 2, :], ps[6 + b % 2][0:F - 2 * P, 2 * P:3 * P],
                                         ACT.Copy).then_inc(s_prTc, 1)

            @block.vector
            def _(dve):
                step = Chain(dve, s_dve)
                for b in range(NB):
                    for m in range(2):
                        dve.wait_ge(s_sp, 2 * b + m + 1)
                        nc.vector.tensor_copy(spec[:, b, m, :], ps[2 * (b % 2) + m][:, 0:F]).then_inc(s_spc, 1)
                        dve.wait_ge(s_sq, 2 * b + m + 1)
                        nc.vector.tensor_reduce(ss[:, b, m, :], sq[:, b % 2, m, :].rearrange(
                            "p (r h f) -> p h r f", r=2, h=H), AX.XY, ALU.add).then_inc(s_ss, 1)
                dve.wait_ge(s_ss, 2 * NB)
                dve.wait_ge(s_spc, 2 * NB)
                nc.vector.reciprocal(ss[:, :, :, :], ss[:, :, :, :]).then_inc(s_inv, 1)
                dve.wait_ge(s_rn, 1)

                def normalise(b):
                    for m in (1, 0):
                        s3 = spec[:, b, m, :].rearrange("p (r h f) -> p r h f", r=2, h=H)
                        ins = nc.vector.tensor_tensor(s3, s3, over(along(rn[:, b, m, :], NF), 2), ALU.mult)
                    ins.then_inc(s_n, 1)

                def add(b):
                    dve.wait_ge(s_y, b + 1)
                    nc.vector.tensor_tensor(x[:, b, :], x[:, b, :], ps[b % 2][:, 0:C], ALU.add).then_inc(s_x, 1)

                normalise(0)
                for b in range(NB):
                    if b + 1 < NB:
                        normalise(b + 1)
                    q = spec[:, b, 0, :].rearrange("p (r f) -> p r f", r=2)
                    c = ps[4 + b % 2][:, 0:F].rearrange("p (r f) -> p r f", r=2)
                    a1, a2, z = t1[:, b % 2, :, :], t2[:, b % 2, :, :], pr[:, b % 2, :].rearrange("p (r f) -> p r f", r=2)
                    dve.wait_ge(s_n, b + 1)
                    dve.wait_ge(s_cum, b + 1)
                    nc.vector.tensor_tensor(a1, q, c, ALU.mult)
                    nc.vector.tensor_tensor(a2[:, 0, :], q[:, 0, :], c[:, 1, :], ALU.mult)
                    nc.vector.tensor_tensor(a2[:, 1, :], q[:, 1, :], c[:, 0, :], ALU.mult).then_inc(s_cread, 1)
                    dve.wait_ge(s_cread, b + 1)
                    if b >= 2:
                        dve.wait_ge(s_prT, b - 1)
                    nc.vector.tensor_tensor(z[:, 0, :], a1[:, 0, :], a1[:, 1, :], ALU.subtract)
                    nc.vector.tensor_tensor(z[:, 1, :], a2[:, 0, :], a2[:, 1, :], ALU.add).then_inc(s_pr, 1)
                    if b >= 2:
                        add(b - 2)
                add(NB - 2)
                add(NB - 1)


def l1_xattn(k):
    nc, x, xnT, ctxT, ps = k.nc, k.x, k.xnT, k.ctxT, k.ps
    H = 16
    SCALE = P ** -0.5
    uses = [("s", 0), ("s", 1), ("q", 0), ("q", 1), ("k", 0), ("k", 1), ("t", 0), ("t", 1),
            ("n", 0), ("v", 0), ("v", 1), (None, 0), ("o", 0), ("o", 1), ("kt", 0), ("kt", 1)]
    with Stage(k, "L1x", k.now) as st:
        s_qread, s_kread, s_vread = st.sem("q_read"), st.sem("k_read"), st.sem("v_read")
        s_nread, s_ktread = st.sem("norms_read"), st.sem("kT_read")
        a = WideHeads(k, st, None)
        tr = a.turns = Turns(k, uses, {"q": (s_qread, 2, 0), "k": (s_kread, 2, 0), "v": (s_vread, 2, 0),
                                       "n": (s_nread, 1, 0), "kt": (s_ktread, 2, 0), "s": (a.s_exp, 2, 0),
                                       "t": (a.s_pT, 2, 0), "o": (a.s_oT, 2, 0)}, "sto", H)
        slot = k.now.slot
        gg = k.now.img
        gain = st.sb("gain", [P, 1])
        sq = st.sb("q_squares", [P, TOK])
        ksq = st.sb("k_squares", [P, TOK])
        kn = st.sb("k_normed", [P, TOK])
        ss = st.sb("square_sums", [P, 2, NB])
        rn = st.sb("rnorm", [P, 2, NB])
        tmp = st.sb("newton", [P, 2, NB])
        qs = st.sb("q_scale", [P, NB])
        s_g, s_load, s_gain = k.now.s_img, k.now.s_slot, st.sem("gain_ready")
        s_wo = [st.sem(f"wo_loaded{s}") for s in range(2)]
        s_q, s_kp, s_v, s_n, s_ktp = (st.sem(n) for n in ("q_psum", "k_psum", "v_psum", "norms_psum", "kT_psum"))
        s_sq, s_ksq, s_kn, s_dve = (st.sem(n) for n in ("q_squared", "k_squared", "k_normed", "dve_step"))

        with nc.Block() as block:

            @block.sync
            def _(sp):
                for s in range(2):
                    sp.sem_inc(s_wo[s], 16)
                with sp.Fori(1, H // 2) as i:
                    for s in range(2):
                        src = k.dram["L1x"][bass.ds(i * 2 + s, 1), :, :].rearrange("a p n -> (a p) n")
                        sp.wait_ge(s_v, (i * 2 + s) * 2 - 2)
                        sp.dma_start(slot[s][:, 0:4 * P], src[:, 0:4 * P]).then_inc(s_load[s], 16)
                        sp.wait_ge(a.s_y, (i * 2 + s) * 2 - 2)
                        sp.dma_start(slot[s][:, 4 * P:], src[:, 4 * P:]).then_inc(s_wo[s], 16)

            @block.tensor
            def _(pe):
                a.clear_sums(pe)

                def head(pe, j, s, i):
                    w = slot[s]
                    wq = w[:, 0:2 * P].rearrange("p (k n) -> p k n", k=KC)
                    wk, wv = w[:, 2 * P:3 * P], w[:, 3 * P:4 * P]
                    first, last = isinstance(j, int) and j == 0, isinstance(j, int) and j == H

                    def row_form(name, wm, sem):
                        for h in range(2):
                            tr.free(pe, j, (name, h))
                            for b in range(4):
                                g = 4 * h + b
                                mm = nc.tensor.matmul(tr.bank((name, h))[:, b * P:(b + 1) * P],
                                                      ctxT[:, g * P:(g + 1) * P], wm, start=True, stop=True)
                            mm.then_inc(sem, 1)

                    if not first:
                        pe.wait_ge(s_ktread, j * 2)
                        pe.wait_ge(s_qread, j * 2)
                        a.scores(pe, j, "")
                    if not last:
                        pe.wait_ge(s_load[s], i * 16 + 16)
                        for h in range(2):
                            tr.free(pe, j, ("q", h))
                            for kc in range(KC):
                                mm = nc.tensor.matmul(tr.bank(("q", h))[:, :], wq[:, kc, :],
                                                      xnT[:, kc, h * HALF:(h + 1) * HALF],
                                                      start=(kc == 0), stop=(kc == KC - 1))
                            mm.then_inc(s_q, 1)
                        row_form("k", wk, s_kp)
                    if not first:
                        a.turn_probs(pe, j, j - 1, "")
                    if not last:
                        tr.free(pe, j, ("n", 0))
                        pe.wait_ge(s_sq, j * 2 + 2)
                        for b in range(NB):
                            mm = nc.tensor.matmul(tr.bank(("n", 0))[:, b:b + 1], sq[:, b * P:(b + 1) * P],
                                                  k.c["ones"][:, 0:1], start=True, stop=True)
                        mm.then_inc(s_n, 1)
                        row_form("v", wv, s_v)
                    if not first:
                        pe.wait_ge(s_vread, j * 2)
                        a.values(pe, j, j - 1, "", a.v[:, 1 - s, :])
                    if not last:
                        for h in range(2):
                            tr.free(pe, j, ("kt", h))
                            pe.wait_ge(s_kn, j * 2 + h + 1)
                            for b in range(4):
                                g = 4 * h + b
                                mm = nc.tensor.transpose(tr.bank(("kt", h))[:, b * P:(b + 1) * P],
                                                         kn[:, g * P:(g + 1) * P], k.ident)
                            mm.then_inc(s_ktp, 1)
                    if not first:
                        pe.wait_ge(s_wo[1 - s], (i + s) * 16)
                        a.project(pe, j - 1, slot[1 - s][:, 4 * P:])

                passes(pe, H, head)

            @block.scalar
            def _(act):
                act.wait_ge(s_gain, 1)

                def head(act, j, s, i):
                    first, last = isinstance(j, int) and j == 0, isinstance(j, int) and j == H
                    if not first:
                        a.exponent(act, j - 1, "", lambda b: qs[:, b:b + 1])
                    if not last:
                        for h in range(2):
                            t = slice(h * HALF, (h + 1) * HALF)
                            act.wait_ge(s_q, j * 2 + h + 1)
                            if not first:
                                act.wait_ge(a.s_s, j * 2)
                                act.wait_ge(s_n, j)
                            nc.scalar.activation(sq[:, t], tr.bank(("q", h))[:, :], ACT.Square).then_inc(s_sq, 1)
                            nc.scalar.activation(a.qT[:, t], tr.bank(("q", h))[:, :], ACT.Copy).then_inc(s_qread, 1)
                        for h in range(2):
                            act.wait_ge(s_kp, j * 2 + h + 1)
                            nc.scalar.activation(ksq[:, h * HALF:(h + 1) * HALF], tr.bank(("k", h))[:, :],
                                                 ACT.Square).then_inc(s_ksq, 1)
                            nc.scalar.activation(kn[:, h * HALF:(h + 1) * HALF], tr.bank(("k", h))[:, :],
                                                 ACT.Copy).then_inc(s_kread, 1)
                        for h in range(2):
                            act.wait_ge(s_v, j * 2 + h + 1)
                            nc.scalar.activation(a.v[:, s, h * HALF:(h + 1) * HALF], tr.bank(("v", h))[:, :],
                                                 ACT.Copy).then_inc(s_vread, 1)
                    if not first:
                        a.copy_out(act, j - 1, "")
                    if not last:
                        for h in range(2):
                            act.wait_ge(s_ktp, j * 2 + h + 1)
                            nc.scalar.activation(a.kT[:, h * HALF:(h + 1) * HALF], tr.bank(("kt", h))[:, :], ACT.Copy,
                                                 scale=gain[:, 0:1]).then_inc(s_ktread, 1)

                passes(act, H, head)

            @block.vector
            def _(dve):
                step = Chain(dve, s_dve)
                nc.vector.memset(a.zero[:, :], 0.0).then_inc(a.s_zero, 1)
                dve.wait_ge(s_g, 16)
                nc.vector.tensor_tensor(gain[:, :], gg[:, 0:1], gg[:, 1:2], ALU.mult).then_inc(s_gain, 1)

                def head(dve, j, s, i):
                    first, last = isinstance(j, int) and j == 0, isinstance(j, int) and j == H
                    step.restart()
                    if not first:
                        for h in range(2):
                            dve.wait_ge(a.s_s, j * 2 + h - 1)
                            step(nc.vector.tensor_reduce(a.mx[:, h, :], tr.bank(("s", h))[:, :].rearrange(
                                "p (b t) -> p b t", b=4), AX.X, ALU.max))
                            nc.vector.scalar_tensor_tensor(a.nb[:, h, :], a.mx[:, h, :], -1.0, qs[:, 4 * h:4 * h + 4],
                                                           ALU.mult, ALU.mult).then_inc(a.s_nb, 1)
                        for h in range(2):
                            a.dve_probs(dve, step, j - 1, h)
                    if not last:
                        for h in range(2):
                            dve.wait_ge(s_ksq, j * 2 + h + 1)
                            step(nc.vector.tensor_reduce(
                                ss[:, 1, 4 * h:4 * h + 4],
                                ksq[:, h * HALF:(h + 1) * HALF].rearrange("p (b t) -> p b t", b=4), AX.X, ALU.add))
                    if not first:
                        for h in range(2):
                            a.dve_turned(dve, j - 1, "", h)
                    if not last:
                        dve.wait_ge(s_n, j + 1)
                        nc.vector.tensor_copy(ss[:, 0, :], tr.bank(("n", 0))[:, 0:NB]).then_inc(s_nread, 1)
                        dve.wait_ge(s_nread, j + 1)
                        step(nc.vector.tensor_scalar(ss[:, :, :], ss[:, :, :], 1.0 / P, 1e-5, ALU.mult, ALU.add))
                        rsqrt(nc, step, ss[:, :, :], rn[:, :, :], tmp[:, :, :])
                        for h in range(2):
                            k3 = kn[:, h * HALF:(h + 1) * HALF].rearrange("p (b t) -> p b t", b=4)
                            dve.wait_ge(s_kread, j * 2 + h + 1)
                            nc.vector.tensor_tensor(k3, k3, along(rn[:, 1, 4 * h:4 * h + 4], P),
                                                    ALU.mult).then_inc(s_kn, 1)
                        step(nc.vector.tensor_scalar(qs[:, :], rn[:, 0, :], SCALE, None, ALU.mult))

                passes(dve, H, head)
                dve.wait_ge(a.s_y, 2 * H)
                a.add(dve)


def l1_ffn(k):
    nc, x, xnT, ps = k.nc, k.x, k.xnT, k.ps
    E, NI = 8, 4
    I = NI * P
    W13, W2 = 2 * KC * I, NI * C
    with Stage(k, "L1f", k.now) as st:
        gate_w = k.now.img.rearrange("p (k n) -> p k n", k=KC)
        slot = k.now.slot
        high, low = ([st.sb(f"{n}{s}", [P, W13 + W2], F32R)[:, :] for s in range(2)] for n in ("high", "low"))
        halves = [(high[s], low[s]) for s in range(2)]
        w1, w3 = ([[t[:, m * KC * I:(m + 1) * KC * I].rearrange("p (k n) -> p k n", k=KC) for t in pair]
                   for pair in halves] for m in range(2))
        w2 = [[t[:, W13:].rearrange("p (k n) -> p k n", k=NI) for t in pair] for pair in halves]
        xh, xl = (st.sb(f"xnT_{n}", [P, KC, TOK], F32R) for n in ("high", "low"))
        weights = st.sb("weights", [P, NB, E])
        mine = st.sb("mine", [P, 2, NB])
        silu = st.sb("silu", [P, 2, HALF])
        hf = st.sb("hidden", [P, 2, HALF])
        hh, hl = (st.sb(f"hT_{n}", [P, 2, NI, HALF], F32R) for n in ("high", "low"))
        r = Router(k, st, E, ps[7])
        s_gw, s_load = k.now.s_img, k.now.s_slot
        s_h, s_silu, s_hT = st.sem("h_in_psum"), st.sem("silu_ready"), st.sem("hT_ready")
        s_y, s_acc, s_mine = st.sem("y_in_psum"), st.sem("y_added"), st.sem("mine_ready")
        s_hf, s_hh, s_high, s_split = (st.sem(n) for n in ("hidden_ready", "hT_high", "w_high", "w_split"))
        s_xh, s_xl = st.sem("x_high"), st.sem("x_low")
        s_tanh, s_dve = st.sem("tanh_ready"), st.sem("dve_step")
        U = 2 * NI
        FREE_UNITS, FREE_SUMS, FREE_HALVES = 2, 2, 4
        PASSES = ((0, 0), (0, 1), (1, 0))

        def experts(eng, start, hidden, output):

            def expert(e, s):
                start(eng, e, s)
                hidden(eng, e, s, 0)
                if not (isinstance(e, int) and e == 0):
                    output(eng, e - 1, 1 - s, 1)
                for u in range(1, NI + 1):
                    hidden(eng, e, s, u)
                output(eng, e, s, 0)
                for u in range(NI + 1, U):
                    hidden(eng, e, s, u)

            for s in range(2):
                expert(s, s)
            with eng.Fori(1, E // 2) as i:
                for s in range(2):
                    expert(i * 2 + s, s)
            output(eng, E - 1, 1, 1)

        with nc.Block() as block:

            @block.sync
            def _(sp):
                with sp.Fori(1, E // 2) as i:
                    for s in range(2):
                        sp.wait_ge(s_y, (i - 1) * 8 + 4 * s + 4 + FREE_HALVES)
                        sp.dma_start(slot[s], k.dram["L1f"][bass.ds(i * 2 + s, 1), :, :].rearrange(
                            "a p n -> (a p) n")).then_inc(s_load[s], 16)

            @block.gpsimd
            def _(pool):

                def split(i, s):
                    pool.wait_ge(s_load[s], i * 16 + 16)
                    for n, (a, b) in enumerate(((0, W13), (W13, W13 + W2))):
                        nc.gpsimd.tensor_tensor(high[s][:, a:b], slot[s][:, a:b],
                                                k.c["zero"].to_broadcast([P, b - a]), ALU.add).then_inc(s_high, 1)
                        pool.wait_ge(s_high, (i * 2 + s) * 2 + n + 1)
                        nc.gpsimd.tensor_tensor(low[s][:, a:b], slot[s][:, a:b], high[s][:, a:b].bitcast(F32),
                                                ALU.subtract).then_inc(s_split, 1)

                for s in range(2):
                    split(0, s)
                with pool.Fori(1, E // 2) as i:
                    for s in range(2):
                        split(i, s)

            @block.tensor
            def _(pe):
                pe.sem_inc(s_y, FREE_HALVES)
                pe.wait_ge(s_gw, 16)
                r.matmuls(gate_w)
                pe.wait_ge(s_xl, 1)

                def start(pe, e, s):
                    pe.wait_ge(s_split, e * 2 + 1)

                def hidden(pe, e, s, u):
                    h, n = u // NI, u % NI
                    pe.wait_ge(s_hf, e * U + u - 1 + FREE_UNITS)
                    for w, bank in ((w1, 0), (w3, 1)):
                        for kc in range(KC):
                            for at, (a, b) in enumerate(PASSES):
                                mm = nc.tensor.matmul(ps[2 * (u % 2) + bank][:, :], w[s][a][:, kc, n * P:(n + 1) * P],
                                                      (xh, xl)[b][:, kc, h * HALF:(h + 1) * HALF],
                                                      start=(kc + at == 0), stop=(kc + at == KC + 1))
                    mm.then_inc(s_h, 1)

                def output(pe, e, s, h):
                    pe.wait_ge(s_hT, e * U + (h + 1) * NI)
                    pe.wait_ge(s_split, e * 2 + 2)
                    for pair in range(2):
                        pe.wait_ge(s_acc, e * 4 + h * 2 + pair - 1 + FREE_SUMS)
                        for j in range(2):
                            t = pair * 2 + j
                            for n in range(NI):
                                for at, (a, b) in enumerate(PASSES):
                                    mm = nc.tensor.matmul(ps[4 + pair][:, j * C:(j + 1) * C],
                                                          (hh, hl)[a][:, h, n, t * P:(t + 1) * P], w2[s][b][:, n, :],
                                                          start=(n + at == 0), stop=(n + at == NI + 1))
                        mm.then_inc(s_y, 1)

                experts(pe, start, hidden, output)

            @block.scalar
            def _(act):
                nc.scalar.activation(xh[:, :, :], xnT[:, :, :], ACT.Copy).then_inc(s_xh, 1)
                act.wait_ge(r.s_logits, 1)
                nc.scalar.activation(r.z[:, :, :], r.logits, ACT.Tanh, scale=1.0 / 30.0).then_inc(s_tanh, 1)
                r.exponent(act, scale=30.0)

                def hidden(act, e, s, u):
                    act.wait_ge(s_h, e * U + u + 1)
                    act.wait_ge(s_hf, e * U + u - 1 + FREE_UNITS)
                    nc.scalar.activation(silu[:, u % 2, :], ps[2 * (u % 2)][:, :], ACT.Silu).then_inc(s_silu, 1)
                    act.wait_ge(s_hf, e * U + u + 1 + FREE_UNITS)
                    act.wait_ge(s_y, e * 4 + (u // NI) * 2 - 2 + FREE_HALVES)
                    nc.scalar.activation(hh[:, u // NI, u % NI, :], hf[:, u % 2, :], ACT.Copy).then_inc(s_hh, 1)

                experts(act, lambda *a: None, hidden, lambda *a: None)

            @block.vector
            def _(dve):
                step = Chain(dve, s_dve)
                dve.sem_inc(s_hf, FREE_UNITS)
                dve.sem_inc(s_acc, FREE_SUMS)
                dve.wait_ge(s_xh, 1)
                nc.vector.tensor_tensor(xl[:, :, :], xnT[:, :, :], xh[:, :, :].bitcast(F32),
                                        ALU.subtract).then_inc(s_xl, 1)
                dve.wait_ge(s_tanh, 1)
                r.softmax(dve, step)
                r.top_two(step)
                r.masked(step, weights[:, :, :])

                def start(dve, e, s):
                    nc.vector.tensor_copy(mine[:, s, :], weights[:, :, bass.ds(e, 1)].rearrange(
                        "p b e -> p (b e)")).then_inc(s_mine, 1)

                def hidden(dve, e, s, u):
                    h, n = u // NI, u % NI
                    dve.wait_ge(s_silu, e * U + u + 1)
                    nc.vector.tensor_tensor(hf[:, u % 2, :], silu[:, u % 2, :], ps[2 * (u % 2) + 1][:, :],
                                            ALU.mult).then_inc(s_hf, 1)
                    dve.wait_ge(s_hh, e * U + u + 1)
                    nc.vector.tensor_tensor(hl[:, h, n, :], hf[:, u % 2, :], hh[:, h, n, :].bitcast(F32),
                                            ALU.subtract).then_inc(s_hT, 1)

                def output(dve, e, s, h):
                    if h == 0:
                        dve.wait_ge(s_mine, e + 1)
                    for pair in range(2):
                        dve.wait_ge(s_y, e * 4 + h * 2 + pair + 1 + FREE_HALVES)
                        for j in range(2):
                            b = 4 * h + 2 * pair + j
                            ins = nc.vector.scalar_tensor_tensor(
                                x[:, b, :], ps[4 + pair][:, j * C:(j + 1) * C], mine[:, s, b:b + 1],
                                x[:, b, :], ALU.mult, ALU.add)
                        ins.then_inc(s_acc, 1)

                experts(dve, start, hidden, output)


def l2_attn(k):
    nc, x, xnT, ps = k.nc, k.x, k.xnT, k.ps
    with Stage(k, "L2a", k.now) as st:
        img = k.now.img
        w = sbuf_views(img, *k.parts["L2a"])
        w_qkv = w["w_qkv"].rearrange("p (k n) -> p k n", k=KC)
        w_out = w["w_out"].rearrange("p (k n) -> p k n", k=KC)
        decay = w["decay"]
        head_ones = k.c["head_ones16"]
        ed = st.sb("ed", [P, KC])
        dsum = st.sb("dsum", [P, KC])
        dec = st.sb("dec", [P, KC])
        decays = st.sb("decays", [P, KC, TOK])
        neg = st.sb("neg", [P, 2, 2 * HALF])
        expd = st.sb("expd", [P, 2, 2 * HALF])
        q = st.sb("q", [P, KC, TOK])
        kk = st.sb("kk", [P, KC, TOK])
        kv = st.sb("kv", [P, KC, TOK])
        ksum = st.sb("ksum", [P, KC, TOK])
        kvsum = st.sb("kvsum", [P, KC, TOK])
        s_w = k.now.s_img
        s_qkv, s_neg, s_exp = st.sem("qkv_ready"), st.sem("neg_ready"), st.sem("exp_ready")
        s_free, s_ed, s_qks, s_den = st.sem("qkv_used"), st.sem("exp_decay"), st.sem("qks_ready"), st.sem("den_ready")
        s_o, s_y, s_dve = st.sem("o_ready"), st.sem("y_ready"), st.sem("dve_step")
        with nc.Block() as block:

            @block.tensor
            def _(pe):
                pe.wait_ge(s_w, 16)
                for u in range(4):
                    c, h = u // 2, u % 2
                    if u >= 2:
                        pe.wait_ge(s_free, u - 1)
                    for n, part in enumerate((1, 2, 0)):
                        col = part * C + c * P
                        for kc in range(KC):
                            mm = nc.tensor.matmul(ps[3 * (u % 2) + n][:, :], w_qkv[:, kc, col:col + P],
                                                  xnT[:, kc, h * HALF:(h + 1) * HALF],
                                                  start=(kc == 0), stop=(kc == KC - 1))
                    mm.then_inc(s_qkv, 1)
                for u in range(4):
                    c, h = u // 2, u % 2
                    pe.wait_ge(s_qks, u + 1)
                    if u == 2:
                        pe.wait_ge(s_o, 2)
                    nc.tensor.matmul(ps[6 + h][:, :], head_ones, kk[:, c, h * HALF:(h + 1) * HALF],
                                     start=True, stop=True).then_inc(s_den, 1)
                pe.wait_ge(s_o, 4)
                for b in range(NB):
                    for kc in range(KC):
                        mm = nc.tensor.matmul(ps[b // 2][:, (b % 2) * C:(b % 2 + 1) * C],
                                              q[:, kc, b * P:(b + 1) * P], w_out[:, kc, :],
                                              start=(kc == 0), stop=(kc == KC - 1))
                    if b % 2:
                        mm.then_inc(s_y, 1)

            @block.scalar
            def _(act):
                act.wait_ge(s_w, 16)
                nc.scalar.activation(ed[:, :], decay, ACT.Exp, scale=-1.0).then_inc(s_ed, 1)
                for u in range(4):
                    act.wait_ge(s_neg, 2 * (u + 1))
                    nc.scalar.activation(expd[:, u % 2, :], neg[:, u % 2, :], ACT.Exp).then_inc(s_exp, 1)

            @block.vector
            def _(dve):
                step = Chain(dve, s_dve)
                dve.wait_ge(s_ed, 1)
                step(nc.vector.tensor_scalar(dsum[:, :], ed[:, :], 1.0, None, ALU.add))
                step(nc.vector.reciprocal(dec[:, :], dsum[:, :]))
                step(nc.vector.memset(decays[:, :, :], 1.0))
                for c in range(KC):
                    step(nc.vector.tensor_scalar(decays[:, c, :], decays[:, c, :], dec[:, c:c + 1], None, ALU.mult))
                    step(nc.vector.memset(decays[:, c, 0:TOK:P], 0.0))

                def minus(u):
                    dve.wait_ge(s_qkv, u + 1)
                    if u >= 2:
                        dve.wait_ge(s_exp, u - 1)
                    nc.vector.tensor_scalar(neg[:, u % 2, 0:HALF], ps[3 * (u % 2)][:, :], 0.0, None,
                                            ALU.min).then_inc(s_neg, 1)
                    nc.vector.tensor_scalar(neg[:, u % 2, HALF:], ps[3 * (u % 2) + 2][:, :], 0.0, None,
                                            ALU.min).then_inc(s_neg, 1)

                minus(0)
                for u in range(4):
                    c, h = u // 2, u % 2
                    t = slice(h * HALF, (h + 1) * HALF)
                    if u < 3:
                        minus(u + 1)
                    dve.wait_ge(s_exp, u + 1)
                    step(nc.vector.scalar_tensor_tensor(kk[:, c, t], ps[3 * (u % 2)][:, :], 0.0,
                                                        expd[:, u % 2, 0:HALF], ALU.max, ALU.add))
                    step(nc.vector.tensor_tensor(kv[:, c, t], kk[:, c, t], ps[3 * (u % 2) + 1][:, :], ALU.mult))
                    nc.vector.scalar_tensor_tensor(q[:, c, t], ps[3 * (u % 2) + 2][:, :], 0.0,
                                                   expd[:, u % 2, HALF:], ALU.max, ALU.add).then_inc(s_free, 1)
                    if h == 1:
                        dve.wait_ge(s_free, u + 1)
                        step(nc.vector.tensor_tensor_scan(ksum[:, c, :], decays[:, c, :], kk[:, c, :], 0.0,
                                                          ALU.mult, ALU.add))
                        step(nc.vector.tensor_tensor_scan(kvsum[:, c, :], decays[:, c, :], kv[:, c, :], 0.0,
                                                          ALU.mult, ALU.add))
                        for hh in range(2):
                            tt = slice(hh * HALF, (hh + 1) * HALF)
                            nc.vector.tensor_tensor(kk[:, c, tt], q[:, c, tt], ksum[:, c, tt],
                                                    ALU.mult).then_inc(s_qks, 1)
                for u in range(4):
                    c, h = u // 2, u % 2
                    t = slice(h * HALF, (h + 1) * HALF)
                    dve.wait_ge(s_den, u + 1)
                    step(nc.vector.tensor_scalar(ksum[:, c, t], ps[6 + h][:, :], 1e-6, None, ALU.max))
                    step(nc.vector.reciprocal(ksum[:, c, t], ksum[:, c, t]))
                    step(nc.vector.tensor_tensor(kvsum[:, c, t], kvsum[:, c, t], ksum[:, c, t], ALU.mult))
                    nc.vector.tensor_tensor(q[:, c, t], q[:, c, t], kvsum[:, c, t], ALU.mult).then_inc(s_o, 1)
                for n in range(NB // 2):
                    dve.wait_ge(s_y, n + 1)
                    nc.vector.tensor_tensor(x[:, 2 * n:2 * n + 2, :], x[:, 2 * n:2 * n + 2, :],
                                            ps[n][:, :].rearrange("p (b n) -> p b n", b=2),
                                            ALU.add)


def l2_xattn(k):
    nc, x, xnT, ctxT, ps = k.nc, k.x, k.xnT, k.ctxT, k.ps
    H, hd, MAIN = 16, 16, P - 16
    with Stage(k, "L2x", k.now) as st:
        img = k.now.img
        w = sbuf_views(img, *k.parts["L2x"])
        wq, wo = (w[n].rearrange("p (k n) -> p k n", k=KC) for n in ("wq", "wo"))
        a = SmallHeads(k, st, H, hd, [(0, MAIN), (MAIN, P)], 1.0 / hd ** 0.5)
        a.w_out, a.in_head = wo, k.c["in_head16"]
        ctxm, ctxd = st.sb("ctx_main", [P, NB, P]), st.sb("ctx_dca", [P, NB, P])
        qk = st.sb("qk", [P, NB, 2 * C])
        sq = st.sb("squares", [P, 2, 2 * C])
        mean, var = st.sb("mean", [P, NB, 2 * H]), st.sb("var", [P, NB, 2 * H])
        rstd = st.sb("rstd", [P, NB, 2 * H])
        s_w = k.now.s_img
        s_qk, s_v, s_ctx = st.sem("qk_psum"), st.sem("v_psum"), st.sem("ctx_split")
        s_read, s_cent, s_sq, s_var = st.sem("qk_read"), st.sem("centred"), st.sem("squares_ready"), st.sem("var_ready")
        s_rstd, s_ln, s_t, s_in = st.sem("rstd_ready"), st.sem("normed"), st.sem("qkT_psum"), st.sem("qkT_ready")
        s_vin, s_bias, s_sqread = st.sem("v_ready"), st.sem("bias_added"), st.sem("squares_read")
        with nc.Block() as block:

            @block.tensor
            def _(pe):
                pe.wait_ge(s_w, 16)
                pe.wait_ge(s_ctx, 4)
                for b in range(NB):
                    if b >= 2:
                        pe.wait_ge(s_read, b - 1)
                        pe.wait_ge(s_vin, b - 1)
                    bank, vb = ps[b % 2], ps[2 + b % 2]
                    for kc in range(KC):
                        nc.tensor.matmul(bank[:, 0:C], xnT[:, kc, b * P:(b + 1) * P], wq[:, kc, :],
                                         start=(kc == 0), stop=(kc == KC - 1))
                    nc.tensor.matmul(bank[:, C:2 * C], ctxm[:, b, :], w["wk"], start=True, stop=False)
                    nc.tensor.matmul(bank[:, C:2 * C], ctxd[:, b, :], w["wkd"], start=False,
                                     stop=True).then_inc(s_qk, 1)
                    nc.tensor.matmul(vb[:, 0:C], ctxm[:, b, :], w["wv"], start=True, stop=True)
                    nc.tensor.matmul(vb[:, C:2 * C], ctxd[:, b, :], w["wvd"], start=True, stop=True).then_inc(s_v, 1)
                for half in range(2):
                    for m in range(2):
                        for c in range(KC):
                            for j in range(4):
                                b = 4 * half + j
                                pe.wait_ge(s_ln, b + 1)
                                mm = nc.tensor.transpose(ps[4 + 2 * (m % 2) + c][:, j * P:(j + 1) * P],
                                                         qk[:, b, m * C + c * P:m * C + (c + 1) * P], k.ident)
                            mm.then_inc(s_t, 1)
                    if half == 0:
                        pe.wait_ge(s_in, 4)
                pe.wait_ge(s_in, 8)
                pe.wait_ge(s_vin, NB)
                a.run(pe, a.pe, a.pe_tail)

            @block.scalar
            def _(act):
                for b in range(NB):
                    act.wait_ge(s_cent, b + 1)
                    if b >= 2:
                        act.wait_ge(s_sqread, b - 1)
                    nc.scalar.activation(sq[:, b % 2, :], qk[:, b, :], ACT.Square).then_inc(s_sq, 1)
                act.wait_ge(s_var, 1)
                nc.scalar.activation(rstd[:, :, :], var[:, :, :], ACT.Sqrt).then_inc(s_rstd, 1)
                for half in range(2):
                    for m in range(2):
                        for c in range(KC):
                            act.wait_ge(s_t, 4 * half + 2 * m + c + 1)
                            bank = ps[4 + 2 * m + c][:, :].rearrange("p (b t) -> p b t", b=4)
                            dst = (a.kT if m else a.qT)[:, c, half * HALF:(half + 1) * HALF].rearrange(
                                "p (b t) -> p b t", b=4)
                            ranges = [(0, MAIN, 1), (MAIN, P, 2)] if m else [(0, P, 0)]
                            for t0, t1, n in ranges:
                                ins = nc.scalar.activation(dst[:, :, t0:t1], bank[:, :, t0:t1], ACT.Identity,
                                                           bias=w["nb"][:, n:n + 1], scale=w["nw"][:, n:n + 1])
                            ins.then_inc(s_in, 1)
                a.run(act, a.act, a.act_tail)

            @block.vector
            def _(dve):
                a.step = step = Chain(dve, a.s_step)
                dve.wait_ge(s_w, 16)
                for b in range(NB):
                    dve.wait_ge(s_qk, b + 1)
                    nc.vector.tensor_tensor(qk[:, b, :], ps[b % 2][:, :], w["bqk"], ALU.add).then_inc(s_read, 1)
                    dve.wait_ge(s_v, b + 1)
                    for m in range(2):
                        ins = nc.vector.tensor_tensor(
                            a.v[:, b, :, m * (hd + 1):m * (hd + 1) + hd],
                            ps[2 + b % 2][:, m * C:(m + 1) * C].rearrange("p (h d) -> p h d", h=H),
                            w["bvs"][:, m * C:(m + 1) * C].rearrange("p (h d) -> p h d", h=H), ALU.add)
                    ins.then_inc(s_vin, 1)
                    h3 = qk[:, b, :].rearrange("p (h d) -> p h d", d=hd)
                    dve.wait_ge(s_read, b + 1)
                    step(nc.vector.tensor_reduce(mean[:, b, :], h3, AX.X, ALU.add))
                    step(nc.vector.tensor_scalar(mean[:, b, :], mean[:, b, :], 1.0 / hd, None, ALU.mult))
                    nc.vector.tensor_tensor(h3, h3, along(mean[:, b, :], hd), ALU.subtract).then_inc(s_cent, 1)
                    if b:
                        dve.wait_ge(s_sq, b)
                        nc.vector.tensor_reduce(var[:, b - 1, :], sq[:, (b - 1) % 2, :].rearrange(
                            "p (h d) -> p h d", d=hd), AX.X, ALU.add).then_inc(s_sqread, 1)
                dve.wait_ge(s_sq, NB)
                step(nc.vector.tensor_reduce(var[:, NB - 1, :], sq[:, (NB - 1) % 2, :].rearrange(
                    "p (h d) -> p h d", d=hd), AX.X, ALU.add))
                dve.wait_ge(s_sqread, NB - 1)
                step(nc.vector.tensor_scalar(var[:, :, :], var[:, :, :], 1.0 / hd, 1e-6, ALU.mult, ALU.add))
                nc.vector.reciprocal(var[:, :, :], var[:, :, :]).then_inc(s_var, 1)
                dve.wait_ge(s_rstd, 1)
                for b in range(NB):
                    h3 = qk[:, b, :].rearrange("p (h d) -> p h d", d=hd)
                    nc.vector.tensor_tensor(h3, h3, along(rstd[:, b, :], hd), ALU.mult).then_inc(s_ln, 1)
                dve.wait_ge(s_bias, 3)
                a.run(dve, a.dve, a.dve_tail)

            @block.gpsimd
            def _(pool):
                ctx3 = ctxT[:, :].rearrange("p (b t) -> p b t", b=NB)
                nc.gpsimd.memset(ctxm[:, :, MAIN:P], 0.0).then_inc(s_ctx, 1)
                nc.gpsimd.memset(ctxd[:, :, 0:MAIN], 0.0).then_inc(s_ctx, 1)
                nc.gpsimd.tensor_copy(ctxm[:, :, 0:MAIN], ctx3[:, :, 0:MAIN]).then_inc(s_ctx, 1)
                nc.gpsimd.tensor_copy(ctxd[:, :, MAIN:P], ctx3[:, :, MAIN:P]).then_inc(s_ctx, 1)
                for m in range(2):
                    for b in range(NB):
                        ins = nc.gpsimd.tensor_copy(a.v[:, b, :, m * (hd + 1) + hd:(m + 1) * (hd + 1)],
                                                    over(k.c["key_parts"][:, m:m + 1], H))
                    ins.then_inc(s_bias, 1)
                pool.wait_ge(s_w, 16)
                nc.gpsimd.tensor_tensor(x[:, :, :], x[:, :, :], over(w["bo"], NB), ALU.add).then_inc(s_bias, 1)
                pool.wait_ge(s_in, 8)
                a.run(pool, a.pool, lambda eng: None)


def l2_ffn(k):
    nc, x, xnT, ps = k.nc, k.x, k.xnT, k.ps
    E, R = 6, 16
    A = R + E * R
    with Stage(k, "L2f", k.now) as st:
        img = k.now.img
        w = sbuf_views(img, *k.parts["L2f"])
        base, down, rout = (w[n].rearrange("p (k n) -> p k n", k=KC) for n in ("base", "down", "router"))
        up = w["up"][0:A, :]
        weights = st.sb("weights_e", [P, NB, E])
        h = st.sb("h", [P, NB, A])
        hT = st.sb("hT", [P, TOK])
        r = Router(k, st, E, ps[7])
        s_w = k.now.s_img
        s_h, s_hw, s_hT, s_hTc = (st.sem(n) for n in ("h_psum", "h_ready", "hT_psum", "hT_ready"))
        s_y, s_bias, s_dve = st.sem("y_psum"), st.sem("bias_added"), st.sem("dve_step")
        with nc.Block() as block:

            @block.gpsimd
            def _(pool):
                pool.wait_ge(s_w, 16)
                nc.gpsimd.tensor_tensor(x[:, :, :], x[:, :, :], over(w["b"], NB), ALU.add).then_inc(s_bias, 1)

            @block.tensor
            def _(pe):
                pe.wait_ge(s_w, 16)
                r.matmuls(rout)
                for b in range(NB):
                    for kc in range(KC):
                        mm = nc.tensor.matmul(ps[4 + b // 4][:, (b % 4) * A:(b % 4 + 1) * A],
                                              xnT[:, kc, b * P:(b + 1) * P], down[:, kc, :],
                                              start=(kc == 0), stop=(kc == KC - 1))
                    if b % 4 == 3:
                        mm.then_inc(s_h, 1)
                for half in range(2):
                    pe.wait_ge(s_hw, half + 1)
                    for b in range(4 * half, 4 * half + 4):
                        mm = nc.tensor.transpose(ps[4 + half][0:A, (b % 4) * P:(b % 4 + 1) * P], h[:, b, :], k.ident)
                    mm.then_inc(s_hT, 1)
                for b in range(NB):
                    pe.wait_ge(s_hTc, b // 4 + 1)
                    y = ps[b // 2][:, (b % 2) * C:(b % 2 + 1) * C]
                    for kc in range(KC):
                        nc.tensor.matmul(y, xnT[:, kc, b * P:(b + 1) * P], base[:, kc, :], start=(kc == 0), stop=False)
                    mm = nc.tensor.matmul(y, hT[0:A, b * P:(b + 1) * P], up, start=False, stop=True)
                    if b % 2:
                        mm.then_inc(s_y, 1)

            @block.scalar
            def _(act):
                r.exponent(act)
                for half in range(2):
                    act.wait_ge(s_hT, half + 1)
                    nc.scalar.activation(hT[0:A, half * HALF:(half + 1) * HALF], ps[4 + half][0:A, :],
                                         ACT.Copy).then_inc(s_hTc, 1)

            @block.vector
            def _(dve):
                step = Chain(dve, s_dve)
                dve.wait_ge(s_w, 16)
                dve.wait_ge(r.s_logits, 1)
                step(nc.vector.tensor_tensor(r.z[:, :, :], r.logits, over(w["b_router"], NB), ALU.add))
                r.softmax(dve, step)
                r.top_two(step)
                r.masked(step, weights[:, :, :])
                for half in range(2):
                    dve.wait_ge(s_h, half + 1)
                    hp = ps[4 + half][:, 0:4 * A].rearrange("p (b n) -> p b n", b=4)
                    bs = slice(4 * half, 4 * half + 4)
                    nc.vector.tensor_copy(h[:, bs, 0:R], hp[:, :, 0:R])
                    for b in range(4):
                        ins = nc.vector.tensor_tensor(
                            h[:, 4 * half + b, R:A].rearrange("p (e r) -> p e r", e=E),
                            hp[:, b, R:A].rearrange("p (e r) -> p e r", e=E),
                            along(weights[:, 4 * half + b, :], R), ALU.mult)
                    ins.then_inc(s_hw, 1)
                dve.wait_ge(s_bias, 1)
                for n in range(4):
                    dve.wait_ge(s_y, n + 1)
                    nc.vector.tensor_tensor(x[:, 2 * n:2 * n + 2, :], x[:, 2 * n:2 * n + 2, :],
                                            ps[n][:, :].rearrange("p (b n) -> p b n", b=2), ALU.add)


def l3_attn(k):
    nc, x, xnT, ps = k.nc, k.x, k.xnT, k.ps
    N, HD, NH, TAPS = 32, 64, 64, 4
    triu, ones = k.c["triu"], k.c["ones"]
    with Stage(k, "L3a", k.now) as st:
        img = k.now.img
        w = sbuf_views(img, *k.parts["L3a"])
        wb, wc, wdt = (w[n].rearrange("p (k n) -> p k n", k=KC) for n in ("wb", "wc", "wdt"))
        slot = k.now.slot
        xh, xl = (st.sb(f"xnT_{n}", [P, KC, TOK], F32R) for n in ("high", "low"))
        wh, wl = (st.sb(f"w_{n}", [P, 2, 2 * KC * P], F32R) for n in ("high", "low"))
        wz, wx = ([[t[:, s, m * KC * P:(m + 1) * KC * P].rearrange("p (k n) -> p k n", k=KC) for t in (wh, wl)]
                   for s in range(2)] for m in range(2))
        at = 2 * KC * P + C
        wo_raw = [t[:, 2 * KC * P:at] for t in slot]
        taps = [t[:, at:at + TAPS] for t in slot]
        cb = [t[:, at + TAPS:at + TAPS + 1] for t in slot]
        dcol = [t[:, at + TAPS + 1:at + TAPS + 2] for t in slot]
        nw = [t[:, at + TAPS + 2:at + TAPS + 3] for t in slot]
        zdt, az, dt, da = (st.sb(n, [P, NB, NH]) for n in ("z_dt", "abs_dt", "dt", "dA"))
        bT, cT = st.sb("bT", [P, TOK]), st.sb("cT", [P, TOK])
        cbm = st.sb("cb_masked", [P, NB, P])
        conv = k.now.spare(2, NB, P)
        xT = st.sb("xT", [P, 2, TOK])
        sz = k.after.spare(2, TOK)
        dac = st.sb("dA_pair", [P, 2, NB, 2])
        dtc = st.sb("dt_pair", [P, 2, NB, 2])
        wo = st.sb("wo", [P, 2, C])
        dcols = st.sb("d_pair", [P, 2, 1])
        dal = st.sb("dA_low", [P, 2 * NB])
        dar = st.sb("dA_high", [P, 2 * NB], F32R)
        rhs = st.sb("dA_steps", [P, 2, 2 * NB, P], F32R)
        below = st.sb("below", [P, P], F32R)
        dec = st.sb("decays", [P, 2, NB, 2, P])
        dtx = st.sb("dtx", [P, 2, NB, 2, HD])
        yg = st.sb("y_gated", [P, 2, TOK])
        ysq, sqsum = k.now.spare(TOK), k.now.spare(TOK)
        zero = st.sb("zero", [P, P])
        ms, rms, tmp = (st.sb(n, [P, NB]) for n in ("mean_square", "rms", "newton"))
        S = {n: st.sem(n) for n in (
            "dt_psum", "zdt", "abs_dt", "exp_dt", "exp1_dt", "log_dt", "bc_psum", "bc_first", "bc_conv",
            "bc_ready", "cb_psum", "cb_ready", "da_ready", "z_psum", "x_psum", "z_read", "x_scaled", "x_read",
            "x_conv", "x_ready", "xt_psum", "xt_read", "steps_ready", "diff_psum", "diff_read", "dec_ready",
            "y_psum", "y_read", "y_ready", "pair_small", "wo_ready", "out_done", "sq_ready", "sq_added",
            "ms_psum", "zero_set", "dve_step", "slot_read", "d_ready", "x_high", "x_low", "w_high",
            "w_split", "below_set", "dA_halved")}
        s_w, s_load = k.now.s_img, k.now.s_slot

        SLOT_FREE = 1

        USES = [("x", 0), ("x", 1), ("z", 0), ("z", 1), ("y", 0), ("y", 1), ("t", 0), ("t", 1),
                ("d", 0), ("d", 1), ("d", 2), ("d", 3)]
        READ = {"x": "x_read", "z": "z_read", "y": "y_read", "d": "diff_read", "t": "xt_read"}
        COUNT = {"x": 2, "z": 2, "y": 2, "d": 4, "t": 2}

        def bank(name, n):
            return ps[4 + USES.index((name, n)) % 4]

        def free(pe, j, name, n):
            i = USES.index((name, n)) - 4
            passes = j
            if i < 0:
                i, passes = i + len(USES), j - 1
            name, n = USES[i]
            if name == "y":
                passes = passes - 1
                if isinstance(passes, int) and passes < 0:
                    name, n = USES[i - 4]
                    passes = passes + 1
            if isinstance(passes, int) and passes < 0:
                return
            pe.wait_ge(S[READ[name]], passes * COUNT[name] + n + 1)

        def conv_first(act, psum, dst, w3, bias):
            return nc.scalar.activation(dst, psum, ACT.Identity, bias=bias, scale=w3)

        def conv_tap(psum, dst, d, wcol):
            return nc.vector.scalar_tensor_tensor(dst[:, :, d:], psum[:, :, 0:P - d], wcol, dst[:, :, d:],
                                                  ALU.mult, ALU.add)

        def passes(eng, body, tail):
            body(eng, 0, 0, 0, False)
            body(eng, 1, 1, 0, True)
            with eng.Fori(1, N // 2) as i:
                for s in range(2):
                    body(eng, i * 2 + s, s, i, True)
            tail(eng)

        with nc.Block() as block:

            @block.sync
            def _(sp):
                def pair(sp, j, s, i, later):
                    if not isinstance(j, int):
                        sp.wait_ge(S["slot_read"], j * 2 - 2)
                        src = k.dram["L3p"][bass.ds(j, 1), :, :].rearrange("a p n -> (a p) n")
                        sp.dma_start(slot[s], src).then_inc(s_load[s], 16)

                passes(sp, pair, lambda eng: None)

            @block.tensor
            def _(pe):
                pe.wait_ge(s_w, 16)
                for b in range(NB):
                    for kc in range(KC):
                        mm = nc.tensor.matmul(ps[0][:, b * NH:(b + 1) * NH], xnT[:, kc, b * P:(b + 1) * P],
                                              wdt[:, kc, :], start=(kc == 0), stop=(kc == KC - 1))
                mm.then_inc(S["dt_psum"], 1)
                for m, wm in enumerate((wb, wc)):
                    for half in range(2):
                        for kc in range(KC):
                            mm = nc.tensor.matmul(ps[4 + 2 * m + half][:, :], wm[:, kc, :],
                                                  xnT[:, kc, half * HALF:(half + 1) * HALF],
                                                  start=(kc == 0), stop=(kc == KC - 1))
                        mm.then_inc(S["bc_psum"], 1)
                pe.wait_ge(S["bc_ready"], 2)
                pe.wait_ge(S["zdt"], 1)
                for b in range(NB):
                    mm = nc.tensor.matmul(ps[b // 4][:, (b % 4) * P:(b % 4 + 1) * P], bT[:, b * P:(b + 1) * P],
                                          cT[:, b * P:(b + 1) * P], start=True, stop=True)
                    if b % 4 == 3:
                        mm.then_inc(S["cb_psum"], 1)
                pe.wait_ge(S["cb_ready"], 2)
                pe.wait_ge(S["zero_set"], 2)
                for n in range(4):
                    nc.tensor.matmul(ps[n][:, :], zero[:, :], xnT[:, 0, 0:HALF], start=True, stop=False,
                                     skip_group_check=True)

                def make_y(pe, j, o):
                    pe.wait_ge(S["dec_ready"], j)
                    pe.wait_ge(S["xt_read"], j * 2)
                    for half in range(2):
                        if isinstance(j, int) and j == N:
                            pe.wait_ge(S["diff_read"], 4 * N)
                        else:
                            free(pe, j, "y", half)
                        for b in range(4):
                            g = 4 * half + b
                            for h in range(2):
                                mm = nc.tensor.matmul(
                                    bank("y", half)[h * HD:(h + 1) * HD, b * P:(b + 1) * P], dtx[:, o, g, h, :],
                                    dec[:, o, g, h, :], start=True, stop=True)
                        mm.then_inc(S["y_psum"], 1)

                def output(pe, j, o):
                    pe.wait_ge(S["wo_ready"], j + 1)
                    for half in range(2):
                        pe.wait_ge(S["y_ready"], j * 2 + half + 1)
                        for b in range(4):
                            g = 4 * half + b
                            mm = nc.tensor.matmul(ps[g // 2][:, (g % 2) * C:(g % 2 + 1) * C],
                                                  yg[:, o, g * P:(g + 1) * P], wo[:, o, :], start=False, stop=False,
                                                  skip_group_check=True)
                    mm.then_inc(S["out_done"], 1)

                def pair(pe, j, s, i, later):
                    pe.wait_ge(S["w_split"], j + 1)
                    for name, wm, sem in (("x", wx[s], "x_psum"), ("z", wz[s], "z_psum")):
                        for half in range(2):
                            free(pe, j, name, half)
                            for kc in range(KC):
                                for at, (a, b) in enumerate(((0, 0), (0, 1), (1, 0))):
                                    mm = nc.tensor.matmul(bank(name, half)[:, :], wm[a][:, kc, :],
                                                          (xh, xl)[b][:, kc, half * HALF:(half + 1) * HALF],
                                                          start=(kc + at == 0), stop=(kc + at == KC + 1))
                            mm.then_inc(S[sem], 1)
                    if not (isinstance(j, int) and j < 2):
                        output(pe, j - 2, s)
                    if later:
                        make_y(pe, j, 1 - s)
                    for half in range(2):
                        free(pe, j, "t", half)
                        pe.wait_ge(S["x_ready"], j * 2 + half + 1)
                        for b in range(4):
                            g = 4 * half + b
                            mm = nc.tensor.transpose(bank("t", half)[:, b * P:(b + 1) * P],
                                                     xT[:, s, g * P:(g + 1) * P], k.ident)
                        mm.then_inc(S["xt_psum"], 1)
                    for n in range(4):
                        if n % 2 == 0:
                            pe.wait_ge(S["steps_ready"], j * 2 + n // 2 + 1)
                        free(pe, j, "d", n)
                        for m in range(2):
                            mm = nc.tensor.matmul(bank("d", n)[:, :], below[:, :],
                                                  rhs[:, m, 4 * n:4 * n + 4, :].rearrange("p m t -> p (m t)"),
                                                  start=(m == 0), stop=(m == 1))
                        mm.then_inc(S["diff_psum"], 1)

                def tail(pe):
                    output(pe, N - 2, 0)
                    make_y(pe, N, 1)
                    output(pe, N - 1, 1)
                    pe.wait_ge(S["sq_added"], N)
                    pe.wait_ge(S["diff_read"], 4 * N)
                    for b in range(NB):
                        mm = nc.tensor.matmul(ps[6][:, b:b + 1], sqsum[:, b * P:(b + 1) * P], ones[:, 0:1],
                                              start=True, stop=True)
                    mm.then_inc(S["ms_psum"], 1)

                pe.sem_inc(S["out_done"], SLOT_FREE)
                pe.wait_ge(S["x_low"], 1)
                pe.wait_ge(S["below_set"], 1)
                passes(pe, pair, tail)

            @block.scalar
            def _(act):
                nc.scalar.activation(xh[:, :, :], xnT[:, :, :], ACT.Copy).then_inc(S["x_high"], 1)
                act.wait_ge(s_w, 16)
                act.wait_ge(S["abs_dt"], 1)
                nc.scalar.activation(az[:, :, :], az[:, :, :], ACT.Exp, scale=-1.0).then_inc(S["exp_dt"], 1)
                for m, dst in enumerate((bT, cT)):
                    cw = w["conv_bc"][:, m * (TAPS + 1):(m + 1) * (TAPS + 1)]
                    for half in range(2):
                        act.wait_ge(S["bc_psum"], 2 * m + half + 1)
                        conv_first(act, ps[4 + 2 * m + half][:, :],
                                   conv[:, m, 4 * half:4 * half + 4, :].rearrange("p b t -> p (b t)"),
                                   cw[:, 3:4], cw[:, 4:5]).then_inc(S["bc_first"], 1)
                act.wait_ge(S["exp1_dt"], 1)
                nc.scalar.activation(az[:, :, :], az[:, :, :], ACT.Ln).then_inc(S["log_dt"], 1)
                for m, dst in enumerate((bT, cT)):
                    act.wait_ge(S["bc_conv"], m + 1)
                    nc.scalar.activation(dst[:, :], conv[:, m, :, :].rearrange("p b t -> p (b t)"),
                                         ACT.Silu).then_inc(S["bc_ready"], 1)

                def squares(act, j, o):
                    act.wait_ge(S["y_ready"], (j - 1) * 2 + 2)
                    if not (isinstance(j, int) and j < 2):
                        act.wait_ge(S["sq_added"], j - 1)
                    nc.scalar.activation(ysq, yg[:, o, :], ACT.Square).then_inc(S["sq_ready"], 1)

                def pair(act, j, s, i, later):
                    act.wait_ge(s_load[s], i * 16 + 16)
                    for half in range(2):
                        act.wait_ge(S["x_psum"], j * 2 + half + 1)
                        conv_first(act, bank("x", half)[:, :],
                                   conv[:, s, 4 * half:4 * half + 4, :].rearrange("p b t -> p (b t)"),
                                   taps[s][:, 3:4], cb[s]).then_inc(S["x_scaled"], 1)
                    for half in range(2):
                        act.wait_ge(S["z_psum"], j * 2 + half + 1)
                        if not isinstance(j, int):
                            act.wait_ge(S["y_ready"], j * 2 - 2)
                        nc.scalar.activation(sz[:, s, half * HALF:(half + 1) * HALF], bank("z", half)[:, :],
                                             ACT.Silu).then_inc(S["z_read"], 1)
                    for half in range(2):
                        act.wait_ge(S["x_conv"], j * 2 + half + 1)
                        if not isinstance(j, int):
                            act.wait_ge(S["y_ready"], j * 2 - 2)
                        nc.scalar.activation(xT[:, s, half * HALF:(half + 1) * HALF],
                                             conv[:, s, 4 * half:4 * half + 4, :].rearrange("p b t -> p (b t)"),
                                             ACT.Silu).then_inc(S["x_ready"], 1)
                    d4 = dec[:, s, :, :, :].rearrange("p b h t -> p (b h t)")
                    for n in range(4):
                        act.wait_ge(S["diff_psum"], j * 4 + n + 1)
                        if not isinstance(j, int):
                            act.wait_ge(S["y_psum"], j * 2 - 2)
                        nc.scalar.activation(d4[:, n * HALF:(n + 1) * HALF], bank("d", n)[:, :],
                                             ACT.Exp).then_inc(S["diff_read"], 1)
                    if later:
                        squares(act, j, 1 - s)

                passes(act, pair, lambda act: squares(act, N, 1))

            @block.vector
            def _(dve):
                step = Chain(dve, S["dve_step"])
                nc.vector.memset(zero[:, :], 0.0).then_inc(S["zero_set"], 1)
                nc.vector.tensor_copy(below[:, :], k.c["below"]).then_inc(S["below_set"], 1)
                dve.wait_ge(S["x_high"], 1)
                nc.vector.tensor_tensor(xl[:, :, :], xnT[:, :, :], xh[:, :, :].bitcast(F32),
                                        ALU.subtract).then_inc(S["x_low"], 1)
                dve.wait_ge(s_w, 16)
                dve.wait_ge(S["dt_psum"], 1)
                nc.vector.tensor_tensor(zdt[:, :, :], ps[0][:, :].rearrange("p (b h) -> p b h", b=NB),
                                        over(w["dt_bias"], NB), ALU.add).then_inc(S["zdt"], 1)
                dve.wait_ge(S["zdt"], 1)
                nc.vector.scalar_tensor_tensor(az[:, :, :], zdt[:, :, :], -1.0, zdt[:, :, :], ALU.mult,
                                               ALU.max).then_inc(S["abs_dt"], 1)
                for m in range(2):
                    cw = w["conv_bc"][:, m * (TAPS + 1):(m + 1) * (TAPS + 1)]
                    for half in range(2):
                        dve.wait_ge(S["bc_first"], 2 * m + half + 1)
                        p3 = ps[4 + 2 * m + half][:, :].rearrange("p (b t) -> p b t", b=4)
                        for d in (1, 2, 3):
                            ins = conv_tap(p3, conv[:, m, 4 * half:4 * half + 4, :], d, cw[:, 3 - d:4 - d])
                            if (half, d) == (1, 3):
                                ins.then_inc(S["bc_conv"], 1)
                            else:
                                step(ins)
                dve.wait_ge(S["exp_dt"], 1)
                nc.vector.tensor_scalar(az[:, :, :], az[:, :, :], 1.0, None, ALU.add).then_inc(S["exp1_dt"], 1)
                dve.wait_ge(S["log_dt"], 1)
                step(nc.vector.scalar_tensor_tensor(dt[:, :, :], zdt[:, :, :], 0.0, az[:, :, :], ALU.max, ALU.add))
                nc.vector.tensor_tensor(da[:, :, :], dt[:, :, :], over(w["A"], NB), ALU.mult).then_inc(S["da_ready"], 1)
                for half in range(2):
                    dve.wait_ge(S["cb_psum"], half + 1)
                    nc.vector.tensor_tensor(cbm[:, 4 * half:4 * half + 4, :],
                                            ps[half][:, :].rearrange("p (b t) -> p b t", b=4), over(triu, 4),
                                            ALU.mult).then_inc(S["cb_ready"], 1)
                dve.wait_ge(S["cb_ready"], 2)

                def gate(dve, j, o):
                    dve.wait_ge(S["d_ready"], j)
                    for half in range(2):
                        t = slice(half * HALF, (half + 1) * HALF)
                        dve.wait_ge(S["y_psum"], (j - 1) * 2 + half + 1)
                        if not (isinstance(j, int) and j < 2):
                            dve.wait_ge(S["out_done"], j - 2 + SLOT_FREE)
                            dve.wait_ge(S["sq_ready"], j - 1)
                        nc.vector.scalar_tensor_tensor(yg[:, o, t], xT[:, o, t], dcols[:, o, :],
                                                       bank("y", half)[:, :], ALU.mult,
                                                       ALU.add).then_inc(S["y_read"], 1)
                        dve.wait_ge(S["y_read"], (j - 1) * 2 + half + 1)
                        nc.vector.tensor_tensor(yg[:, o, t], yg[:, o, t], sz[:, o, t],
                                                ALU.mult).then_inc(S["y_ready"], 1)

                def add_squares(dve, j):
                    dve.wait_ge(S["sq_ready"], j)
                    if not (isinstance(j, int) and j < 2):
                        dve.wait_ge(S["sq_added"], j - 1)
                    nc.vector.tensor_tensor(sqsum, sqsum, ysq, ALU.add).then_inc(S["sq_added"], 1)

                def pair(dve, j, s, i, later):
                    step.restart()
                    for half in range(2):
                        dve.wait_ge(S["x_scaled"], j * 2 + half + 1)
                        p3 = bank("x", half)[:, :].rearrange("p (b t) -> p b t", b=4)
                        c4 = conv[:, s, 4 * half:4 * half + 4, :]
                        for d in (1, 2):
                            step(conv_tap(p3, c4, d, taps[s][:, 3 - d:4 - d]))
                        conv_tap(p3, c4, 3, taps[s][:, 0:1]).then_inc(S["x_read"], 1)
                        dve.wait_ge(S["x_read"], j * 2 + half + 1)
                        dve.sem_inc(S["x_conv"], 1)
                    if later:
                        gate(dve, j, 1 - s)
                    dve.wait_ge(S["pair_small"], j * 2 + 2)
                    for half in range(2):
                        dve.wait_ge(S["xt_psum"], j * 2 + half + 1)
                        bs = slice(4 * half, 4 * half + 4)
                        nc.vector.tensor_tensor(dtx[:, s, bs, :, :],
                                                bank("t", half)[:, :].rearrange("p (b h d) -> p b h d", b=4, h=2),
                                                along(dtc[:, s, bs, :], HD), ALU.mult).then_inc(S["xt_read"], 1)
                    dve.wait_ge(S["diff_read"], j * 4 + 4)
                    for h in range(2):
                        ins = nc.vector.tensor_tensor(dec[:, s, :, h, :], dec[:, s, :, h, :], cbm[:, :, :], ALU.mult)
                    ins.then_inc(S["dec_ready"], 1)
                    if later:
                        add_squares(dve, j)

                def tail(dve):
                    step.restart()
                    gate(dve, N, 1)
                    add_squares(dve, N)
                    dve.wait_ge(S["ms_psum"], 1)
                    step(nc.vector.tensor_scalar(ms[:, :], ps[6][:, 0:NB], 1.0 / (N * P), 1e-5, ALU.mult, ALU.add))
                    rsqrt(nc, step, ms[:, :], rms[:, :], tmp[:, :])
                    dve.wait_ge(S["out_done"], N + SLOT_FREE)
                    for b in range(NB):
                        nc.vector.scalar_tensor_tensor(x[:, b, :], ps[b // 2][:, (b % 2) * C:(b % 2 + 1) * C],
                                                       rms[:, b:b + 1], x[:, b, :], ALU.mult, ALU.add)

                dve.wait_ge(S["zero_set"], 2)
                passes(dve, pair, tail)

            @block.gpsimd
            def _(pool):
                nc.gpsimd.memset(sqsum, 0.0).then_inc(S["zero_set"], 1)
                pool.wait_ge(S["zero_set"], 1)
                pool.wait_ge(S["da_ready"], 1)

                def pair(pool, j, s, i, later):
                    pool.wait_ge(s_load[s], i * 16 + 16)
                    if not isinstance(j, int):
                        pool.wait_ge(S["z_psum"], j * 2 - 2)
                    w2 = slot[s][:, 0:2 * KC * P]
                    nc.gpsimd.tensor_tensor(wh[:, s, :], w2, k.c["zero"].to_broadcast([P, 2 * KC * P]),
                                            ALU.add).then_inc(S["w_high"], 1)
                    pool.wait_ge(S["w_high"], j + 1)
                    nc.gpsimd.tensor_tensor(wl[:, s, :], w2, wh[:, s, :].bitcast(F32),
                                            ALU.subtract).then_inc(S["w_split"], 1)
                    if not isinstance(j, int):
                        pool.wait_ge(S["xt_read"], j * 2 - 2)
                    hs = slice(j * 2, j * 2 + 2) if isinstance(j, int) else bass.ds(j * 2, 2)
                    nc.gpsimd.tensor_tensor(dac[:, s, :, :], da[:, :, hs],
                                            k.c["zero"].unsqueeze(2).to_broadcast([P, NB, 2]),
                                            ALU.add).then_inc(S["pair_small"], 1)
                    nc.gpsimd.tensor_copy(dtc[:, s, :, :], dt[:, :, hs]).then_inc(S["pair_small"], 1)
                    pool.wait_ge(S["pair_small"], j * 2 + 2)
                    dsel = dac[:, s, :, :].rearrange("p b h -> p (b h)")
                    nc.gpsimd.tensor_tensor(dar[:, :], dsel, k.c["zero"].to_broadcast([P, 2 * NB]),
                                            ALU.add).then_inc(S["dA_halved"], 1)
                    pool.wait_ge(S["dA_halved"], j * 2 + 1)
                    nc.gpsimd.tensor_tensor(dal[:, :], dsel, dar[:, :].bitcast(F32),
                                            ALU.subtract).then_inc(S["dA_halved"], 1)
                    pool.wait_ge(S["dA_halved"], j * 2 + 2)
                    for half in range(2):
                        if later:
                            pool.wait_ge(S["diff_psum"], j * 4 - 2 + 2 * half)
                        bs = slice(half * NB, (half + 1) * NB)
                        nc.gpsimd.tensor_tensor(rhs[:, 0, bs, :], along(dar[:, bs].bitcast(F32), P), over(triu, NB),
                                                ALU.mult)
                        nc.gpsimd.tensor_tensor(rhs[:, 1, bs, :], along(dal[:, bs], P), over(triu, NB),
                                                ALU.mult).then_inc(S["steps_ready"], 1)
                    if not isinstance(j, int):
                        pool.wait_ge(S["out_done"], j - 1 + SLOT_FREE)
                        pool.wait_ge(S["y_read"], j * 2 - 2)
                    nc.gpsimd.tensor_tensor(wo[:, s, :], wo_raw[s], nw[s].to_broadcast([P, C]),
                                            ALU.mult).then_inc(S["wo_ready"], 1)
                    nc.gpsimd.tensor_copy(dcols[:, s, :], dcol[s]).then_inc(S["d_ready"], 1)
                    pool.wait_ge(S["x_ready"], j * 2 + 2)
                    pool.wait_ge(S["wo_ready"], j + 1)
                    pool.wait_ge(S["d_ready"], j + 1)
                    pool.sem_inc(S["slot_read"], 2)

                passes(pool, pair, lambda pool: None)


def l3_xattn(k):
    nc, x, xnT, ctxT, ps = k.nc, k.x, k.xnT, k.ctxT, k.ps
    H = 8
    SCALE = P ** -0.5
    uses = [(n, h) for n in ("sb", "qa", "tb", "k", "ob", "v", "sa", "qb", "ta", "oa") for h in range(2)]
    with Stage(k, "L3x", k.now) as st:
        s_kread, s_vread, s_qread, s_sread = (st.sem(n) for n in ("k_read", "v_read", "q_read", "s_read"))
        a = WideHeads(k, st, None)
        readers = {"k": (s_kread, 2, 0), "v": (s_vread, 2, 0)}
        for name, sem in (("q", s_qread), ("s", s_sread), ("t", a.s_pT), ("o", a.s_oT)):
            readers.update({name + "a": (sem, 4, 0), name + "b": (sem, 4, 2)})
        tr = a.turns = Turns(k, uses, readers, ("sb", "tb", "ob"), H)
        a.sm = st.sb("masked_scores", [P, 2, HALF])
        a.scored = lambda tr, tag, h: a.sm[:, h, :]
        slot = k.now.slot
        mask8 = st.sb("mask8", [P, TOK], U8)
        maskc8 = st.sb("maskc8", [P, NB], U8)
        neg = st.sb("neg", [P, TOK])
        keep = st.sb("keep", [P, NB])
        s_m, s_load, s_mask = st.sem("mask_loaded"), k.now.s_slot, st.sem("mask_ready")
        s_wo = [st.sem(f"wo_loaded{s}") for s in range(2)]
        s_q, s_kp, s_v, s_dve = (st.sem(n) for n in ("q_psum", "k_psum", "v_psum", "dve_step"))

        with nc.Block() as block:

            @block.sync
            def _(sp):
                sp.dma_start(mask8[:, :], k.dram["mask"]).then_inc(s_m, 16)
                sp.dma_start(maskc8[:, :], k.dram["maskT"]).then_inc(s_m, 16)

                for s in range(2):
                    sp.sem_inc(s_wo[s], 16)
                with sp.Fori(1, H // 2) as i:
                    for s in range(2):
                        src = k.dram["L3x"][bass.ds(i * 2 + s, 1), :, :].rearrange("a p n -> (a p) n")
                        sp.wait_ge(s_q, (i * 2 + s) * 4 - 4)
                        sp.dma_start(slot[s][:, 0:6 * P], src[:, 0:6 * P]).then_inc(s_load[s], 16)
                        sp.wait_ge(a.s_y, (i * 2 + s) * 4 - 4)
                        sp.dma_start(slot[s][:, 6 * P:], src[:, 6 * P:]).then_inc(s_wo[s], 16)

            @block.gpsimd
            def _(pool):
                pool.wait_ge(s_m, 32)
                nc.gpsimd.tensor_copy(neg[:, :], mask8[:, :]).then_inc(s_mask, 1)
                nc.gpsimd.tensor_copy(keep[:, :], maskc8[:, :]).then_inc(s_mask, 1)
                pool.wait_ge(s_mask, 2)
                nc.gpsimd.tensor_scalar(neg[:, :], neg[:, :], 1.0, BIG, ALU.subtract, ALU.mult).then_inc(s_mask, 1)

            @block.tensor
            def _(pe):
                a.clear_sums(pe)

                def head(pe, j, s, i):
                    w = slot[s]
                    wq = w[:, 0:4 * P].rearrange("p (k n) -> p k n", k=KC)
                    wk, wv = w[:, 4 * P:5 * P], w[:, 5 * P:6 * P]
                    wo = [t[:, 6 * P:].rearrange("p (q n) -> p q n", q=2) for t in slot]
                    first, last = isinstance(j, int) and j == 0, isinstance(j, int) and j == H

                    def queries(n, tag):
                        for h in range(2):
                            tr.free(pe, j, ("q" + tag, h))
                            for kc in range(KC):
                                mm = nc.tensor.matmul(tr.bank(("q" + tag, h))[:, :], wq[:, kc, n * P:(n + 1) * P],
                                                      xnT[:, kc, h * HALF:(h + 1) * HALF],
                                                      start=(kc == 0), stop=(kc == KC - 1))
                            mm.then_inc(s_q, 1)

                    if not first:
                        pe.wait_ge(s_qread, j * 4)
                        a.scores(pe, j, "b")
                    if not last:
                        pe.wait_ge(s_load[s], i * 16 + 16)
                        queries(0, "a")
                    if not first:
                        a.turn_probs(pe, j, j * 2 - 1, "b")
                    if not last:
                        for h in range(2):
                            tr.free(pe, j, ("k", h))
                            nc.tensor.matmul(tr.bank(("k", h))[:, :], wk, ctxT[:, h * HALF:(h + 1) * HALF],
                                             start=True, stop=True).then_inc(s_kp, 1)
                    if not first:
                        a.values(pe, j, j * 2 - 1, "b", a.v[:, 0, :])
                    if not last:
                        for h in range(2):
                            tr.free(pe, j, ("v", h))
                            for b in range(4):
                                g = 4 * h + b
                                mm = nc.tensor.matmul(tr.bank(("v", h))[:, b * P:(b + 1) * P],
                                                      ctxT[:, g * P:(g + 1) * P], wv, start=True, stop=True)
                            mm.then_inc(s_v, 1)
                        pe.wait_ge(s_kread, j * 2 + 2)
                        pe.wait_ge(s_qread, j * 4 + 2)
                        a.scores(pe, j, "a")
                        queries(1, "b")
                        a.turn_probs(pe, j, j * 2, "a")
                    if not first:
                        pe.wait_ge(s_wo[1 - s], (i + s) * 16)
                        a.project(pe, j * 2 - 1, wo[1 - s][:, 1, :])
                    if not last:
                        pe.wait_ge(s_vread, j * 2 + 2)
                        a.values(pe, j, j * 2, "a", a.v[:, 0, :])
                        pe.wait_ge(s_wo[s], i * 16 + 16)
                        a.project(pe, j * 2, wo[s][:, 0, :])

                passes(pe, H, head)

            @block.scalar
            def _(act):
                def head(act, j, s, i):
                    first, last = isinstance(j, int) and j == 0, isinstance(j, int) and j == H

                    def queries(n, tag):
                        for h in range(2):
                            act.wait_ge(s_q, j * 4 + 2 * n + h + 1)
                            if n or not first:
                                act.wait_ge(a.s_s, j * 4 + 2 * n)
                            nc.scalar.activation(a.qT[:, h * HALF:(h + 1) * HALF], tr.bank(("q" + tag, h))[:, :],
                                                 ACT.Copy).then_inc(s_qread, 1)

                    if not first:
                        a.exponent(act, j * 2 - 1, "b", lambda b: SCALE)
                    if not last:
                        queries(0, "a")
                        for h in range(2):
                            act.wait_ge(s_kp, j * 2 + h + 1)
                            if not first:
                                act.wait_ge(a.s_s, j * 4)
                            nc.scalar.activation(a.kT[:, h * HALF:(h + 1) * HALF], tr.bank(("k", h))[:, :],
                                                 ACT.Copy).then_inc(s_kread, 1)
                    if not first:
                        a.copy_out(act, j * 2 - 1, "b")
                    if not last:
                        a.exponent(act, j * 2, "a", lambda b: SCALE)
                        queries(1, "b")
                        a.copy_out(act, j * 2, "a")

                passes(act, H, head)

            @block.vector
            def _(dve):
                step = Chain(dve, s_dve)
                nc.vector.memset(a.zero[:, :], 0.0).then_inc(a.s_zero, 1)
                dve.wait_ge(s_mask, 3)

                def head(dve, j, s, i):
                    first, last = isinstance(j, int) and j == 0, isinstance(j, int) and j == H
                    step.restart()

                    def softmax(u, tag):
                        for h in range(2):
                            dve.wait_ge(a.s_s, u * 2 + h + 1)
                            sm = a.sm[:, h, :]
                            nc.vector.tensor_tensor(sm, tr.bank(("s" + tag, h))[:, :],
                                                    neg[:, h * HALF:(h + 1) * HALF], ALU.add).then_inc(s_sread, 1)
                            dve.wait_ge(s_sread, u * 2 + h + 1)
                            step(nc.vector.tensor_reduce(a.mx[:, h, :], sm.rearrange("p (b t) -> p b t", b=4),
                                                         AX.X, ALU.max))
                            nc.vector.tensor_scalar(a.nb[:, h, :], a.mx[:, h, :], -SCALE, None,
                                                    ALU.mult).then_inc(a.s_nb, 1)
                        for h in range(2):
                            a.dve_probs(dve, step, u, h)
                        for h in range(2):
                            a.dve_turned(dve, u, tag, h)

                    if not first:
                        softmax(j * 2 - 1, "b")
                    if not last:
                        for h in range(2):
                            dve.wait_ge(s_v, j * 2 + h + 1)
                            if not first:
                                dve.wait_ge(a.s_oTp, j * 4)
                            nc.vector.tensor_tensor(a.v[:, 0, h * HALF:(h + 1) * HALF].rearrange("p (b t) -> p b t", b=4),
                                                    tr.bank(("v", h))[:, :].rearrange("p (b t) -> p b t", b=4),
                                                    along(keep[:, 4 * h:4 * h + 4], P), ALU.mult).then_inc(s_vread, 1)
                        softmax(j * 2, "a")

                passes(dve, H, head)
                dve.wait_ge(a.s_y, 4 * H)
                a.add(dve)


def l3_ffn(k):
    nc, x, xnT, ps = k.nc, k.x, k.xnT, k.ps
    HID = [1, 2, 3, 4, 1, 2, 3, 4]
    E, NCH = len(HID), sum(HID)
    first = [sum(HID[:e]) for e in range(E)] + [NCH]
    sizes = HID + [1]
    with Stage(k, "L3f", k.now) as st:
        img = k.now.img
        w = sbuf_views(img, *k.parts["L3f"])
        down, rout, core = (w[n].rearrange("p (k n) -> p k n", k=KC) for n in ("down", "router", "core"))
        w1 = w["w1"].rearrange("p (c n) -> p c n", c=NCH + 1)
        w2 = w["w2"].rearrange("p (c n) -> p c n", c=NCH + 1)
        b1 = w["b1"]
        gh = st.sb("gelu_hT", [P, TOK])
        hb = st.sb("hT", [P, 2, HALF])
        gx = st.sb("gelu_xT", [P, KC, TOK])
        u = st.sb("u", [P, 2, 4, TOK])
        u0 = st.sb("u0", [P, NCH])
        u0e = st.sb("u0_by_expert", [P, NCH, E])
        d = st.sb("idle_out", [E, P])
        gates = st.sb("gates", [P, NB, E + 1])
        idle = st.sb("idle_weights", [P, NB, E])
        idleT = st.sb("idle_weightsT", [E, TOK])
        b2sum = st.sb("b2_sum", [P, P])
        gdiff, gexp, g1, g2 = (st.sb(n, [P, NB]) for n in ("gdiff", "gexp", "g1", "g2"))
        acc = st.sb("acc", [P, NB, P])
        accT = st.sb("accT", [P, TOK])
        r = Router(k, st, E, ps[7])
        s_w = k.now.s_img
        s_h, s_hc, s_gh, s_gx = (st.sem(n) for n in ("h_psum", "h_read", "gelu_h", "gelu_x"))
        s_u0, s_u0e, s_dp, s_d = (st.sem(n) for n in ("u0", "u0_placed", "idle_psum", "idle_ready"))
        s_it, s_itc, s_c, s_acc0 = (st.sem(n) for n in ("idleT_psum", "idleT_ready", "corr_psum", "acc_started"))
        s_gd, s_ge, s_idle, s_up, s_u = (st.sem(n) for n in ("gate_diff", "gate_exp", "idle_w", "u_psum", "u_ready"))
        s_y, s_yr, s_at, s_atc, s_o = (st.sem(n) for n in ("y_psum", "y_read", "accT_psum", "accT_ready", "out_psum"))
        s_bias, s_dve = st.sem("bias_added"), st.sem("dve_step")
        done = [2 * sum(sizes[:e]) for e in range(E + 2)]

        def hidden_units():
            n = 0
            for e in range(E + 1):
                for c in range(sizes[e]):
                    for half in range(2):
                        yield e, c, half, n
                        n += 1

        with nc.Block() as block:

            @block.gpsimd
            def _(pool):
                nc.gpsimd.memset(u0e[:, :, :], 0.0).then_inc(s_bias, 1)
                pool.wait_ge(s_w, 16)
                nc.gpsimd.tensor_tensor(x[:, :, :], x[:, :, :], over(w["up_b"], NB), ALU.add).then_inc(s_bias, 1)
                pool.wait_ge(s_bias, 2)
                nc.gpsimd.tensor_tensor(x[:, :, :], x[:, :, :], over(w["core_b"], NB), ALU.add).then_inc(s_bias, 1)
                pool.wait_ge(s_u0, 1)
                for e in range(E):
                    ins = nc.gpsimd.tensor_copy(u0e[:, first[e]:first[e] + HID[e], e], u0[:, first[e]:first[e] + HID[e]])
                ins.then_inc(s_u0e, 1)

            @block.tensor
            def _(pe):
                pe.wait_ge(s_w, 16)
                r.matmuls(rout)
                for half in range(2):
                    for kc in range(KC):
                        mm = nc.tensor.matmul(ps[half][:, :], down[:, kc, :], xnT[:, kc, half * HALF:(half + 1) * HALF],
                                              start=(kc == 0), stop=(kc == KC - 1))
                    mm.then_inc(s_h, 1)
                pe.wait_ge(s_u0e, 1)
                for c in range(NCH):
                    mm = nc.tensor.matmul(ps[6][0:E, 0:P], u0e[:, c, :], w2[:, c, :], start=(c == 0),
                                          stop=(c == NCH - 1))
                mm.then_inc(s_dp, 1)
                pe.wait_ge(s_idle, 1)
                for b in range(NB):
                    if b % 4 == 0:
                        pe.wait_ge(s_gh, 2)
                    mm = nc.tensor.transpose(ps[4 + b // 4][0:E, (b % 4) * P:(b % 4 + 1) * P], idle[:, b, :], k.ident)
                    if b % 4 == 3:
                        mm.then_inc(s_it, 1)
                pe.wait_ge(s_itc, 2)
                pe.wait_ge(s_d, 1)
                for b in range(NB):
                    mm = nc.tensor.matmul(ps[4 + b // 4][:, (b % 4) * P:(b % 4 + 1) * P], idleT[:, b * P:(b + 1) * P],
                                          d[:, :], start=True, stop=True)
                    if b % 4 == 3:
                        mm.then_inc(s_c, 1)
                pe.wait_ge(s_acc0, 2)

                def out(e):
                    pe.wait_ge(s_u, done[e + 1])
                    for half in range(2):
                        if e >= 2:
                            pe.wait_ge(s_yr, 2 * (e - 2) + half + 1)
                        bank = ps[4 + 2 * (e % 2) + half]
                        for j in range(4):
                            b = 4 * half + j
                            for c in range(sizes[e]):
                                mm = nc.tensor.matmul(bank[:, j * P:(j + 1) * P], u[:, e % 2, c, b * P:(b + 1) * P],
                                                      w2[:, first[e] + c, :], start=(c == 0), stop=(c == sizes[e] - 1))
                        mm.then_inc(s_y, 1)

                for e, c, half, n in hidden_units():
                    if n >= 4:
                        pe.wait_ge(s_u, n - 3)
                    nc.tensor.matmul(ps[n % 4][:, :], w1[:, first[e] + c, :], gh[:, half * HALF:(half + 1) * HALF],
                                     start=True, stop=True).then_inc(s_up, 1)
                    if e and c == 0 and half == 1:
                        out(e - 1)
                out(E)
                for b in range(NB):
                    if b % 4 == 0:
                        pe.wait_ge(s_yr, 2 * E + b // 4 + 1)
                        pe.wait_ge(s_u, done[E + 1])
                    mm = nc.tensor.transpose(ps[b // 4][:, (b % 4) * P:(b % 4 + 1) * P], acc[:, b, :], k.ident)
                    if b % 4 == 3:
                        mm.then_inc(s_at, 1)
                pe.wait_ge(s_gx, 1)
                for b in range(NB):
                    pe.wait_ge(s_atc, b // 4 + 1)
                    y = ps[4 + b // 2][:, (b % 2) * C:(b % 2 + 1) * C]
                    nc.tensor.matmul(y, accT[:, b * P:(b + 1) * P], w["up"], start=True, stop=False)
                    for kc in range(KC):
                        mm = nc.tensor.matmul(y, gx[:, kc, b * P:(b + 1) * P], core[:, kc, :], start=False,
                                              stop=(kc == KC - 1))
                    if b % 2:
                        mm.then_inc(s_o, 1)

            @block.scalar
            def _(act):
                act.wait_ge(s_w, 16)
                r.exponent(act)
                act.wait_ge(s_gd, 1)
                nc.scalar.activation(gexp[:, :], gdiff[:, :], ACT.Exp).then_inc(s_ge, 1)
                nc.scalar.activation(u0[:, :], b1[:, 0:NCH], ACT.Gelu).then_inc(s_u0, 1)
                for half in range(2):
                    act.wait_ge(s_h, half + 1)
                    nc.scalar.activation(hb[:, half, :], ps[half][:, :], ACT.Identity,
                                         bias=w["down_b"]).then_inc(s_hc, 1)
                for half in range(2):
                    act.wait_ge(s_hc, half + 1)
                    nc.scalar.activation(gh[:, half * HALF:(half + 1) * HALF], hb[:, half, :],
                                         ACT.Gelu).then_inc(s_gh, 1)
                nc.scalar.activation(gx[:, :, :], xnT[:, :, :], ACT.Gelu).then_inc(s_gx, 1)
                for e, c, half, n in hidden_units():
                    act.wait_ge(s_up, n + 1)
                    if e >= 2:
                        act.wait_ge(s_y, 2 * (e - 2) + 2)
                    nc.scalar.activation(u[:, e % 2, c, half * HALF:(half + 1) * HALF], ps[n % 4][:, :], ACT.Gelu,
                                         bias=b1[:, first[e] + c:first[e] + c + 1]).then_inc(s_u, 1)
                for half in range(2):
                    act.wait_ge(s_at, half + 1)
                    nc.scalar.activation(accT[:, half * HALF:(half + 1) * HALF], ps[half][:, :],
                                         ACT.Copy).then_inc(s_atc, 1)

            @block.vector
            def _(dve):
                step = Chain(dve, s_dve)
                dve.wait_ge(s_w, 16)
                dve.wait_ge(r.s_logits, 1)
                step(nc.vector.tensor_tensor(r.z[:, :, :], r.logits, over(w["b_router"], NB), ALU.add))
                step(nc.vector.tensor_tensor(r.z[:, :, :], r.z[:, :, :], over(k.c["cost"], NB), ALU.subtract))
                r.softmax(dve, step)
                r.top_two(step)
                nc.vector.tensor_tensor(gdiff[:, :], r.top2[:, :], r.top1[:, :], ALU.subtract).then_inc(s_gd, 1)
                dve.wait_ge(s_ge, 1)
                step(nc.vector.tensor_scalar(g2[:, :], gexp[:, :], 1.0, None, ALU.add))
                step(nc.vector.reciprocal(g1[:, :], g2[:, :]))
                step(nc.vector.tensor_tensor(g2[:, :], gexp[:, :], g1[:, :], ALU.mult))
                step(nc.vector.memset(gates[:, :, E:E + 1], 0.1))
                step(nc.vector.tensor_tensor(r.first[:, :, :], r.first[:, :, :], along(g1[:, :], E), ALU.mult))
                step(nc.vector.tensor_tensor(r.second[:, :, :], r.second[:, :, :], along(g2[:, :], E), ALU.mult))
                step(nc.vector.tensor_tensor(gates[:, :, 0:E], r.first[:, :, :], r.second[:, :, :], ALU.add))
                nc.vector.tensor_scalar(idle[:, :, :], gates[:, :, 0:E], -1.0, 1.0, ALU.mult,
                                        ALU.add).then_inc(s_idle, 1)
                b2 = w["b2"].rearrange("p (e l) -> p e l", e=E + 1)
                step(nc.vector.tensor_reduce(b2sum[:, :], b2[:, 0:E, :].rearrange("p e l -> p l e"), AX.X, ALU.add))
                step(nc.vector.scalar_tensor_tensor(b2sum[:, :], b2[:, E, :], 0.1, b2sum[:, :], ALU.mult, ALU.add))
                dve.wait_ge(s_dp, 1)
                nc.vector.tensor_copy(d[:, :], ps[6][0:E, 0:P]).then_inc(s_d, 1)
                for half in range(2):
                    dve.wait_ge(s_it, half + 1)
                    nc.vector.tensor_copy(idleT[:, half * HALF:(half + 1) * HALF], ps[4 + half][0:E, :]).then_inc(s_itc, 1)
                for half in range(2):
                    dve.wait_ge(s_c, half + 1)
                    nc.vector.tensor_tensor(acc[:, 4 * half:4 * half + 4, :],
                                            ps[4 + half][:, :].rearrange("p (b l) -> p b l", b=4),
                                            over(b2sum[:, :], 4), ALU.add).then_inc(s_acc0, 1)
                dve.wait_ge(s_acc0, 2)
                for e in range(E + 1):
                    for half in range(2):
                        dve.wait_ge(s_y, 2 * e + half + 1)
                        if e:
                            dve.wait_ge(s_yr, 2 * (e - 1) + half + 1)
                        for j in range(4):
                            b = 4 * half + j
                            ins = nc.vector.scalar_tensor_tensor(
                                acc[:, b, :], ps[4 + 2 * (e % 2) + half][:, j * P:(j + 1) * P], gates[:, b, e:e + 1],
                                acc[:, b, :], ALU.mult, ALU.add)
                        ins.then_inc(s_yr, 1)
                dve.wait_ge(s_bias, 3)
                for n in range(4):
                    dve.wait_ge(s_o, n + 1)
                    nc.vector.tensor_tensor(x[:, 2 * n:2 * n + 2, :], x[:, 2 * n:2 * n + 2, :],
                                            ps[4 + n][:, :].rearrange("p (b n) -> p b n", b=2), ALU.add)


STAGES = [l0_attn, l0_xattn, l0_ffn, l1_attn, l1_xattn, l1_ffn, l2_attn, l2_xattn, l2_ffn, l3_attn, l3_xattn, l3_ffn]
WEIGHTS = [("L0a", None), ("L0x", None), ("L0f", None), ("L1a", None), ("L1n", "L1x"), ("L1g", "L1f"),
           ("L2a", None), ("L2x", None), ("L2f", None), ("L3a", "L3p"), (None, "L3x"), ("L3f", None)]


def program(nc, dram, parts, width, out):
    k = K()
    k.nc, k.dram, k.parts, k.width = nc, dram, parts, width
    with ExitStack() as ctx:
        k.ps = [ctx.enter_context(nc.psum_tensor(f"bank{i}", [P, HALF], F32)) for i in range(8)]
        k.x = ctx.enter_context(nc.sbuf_tensor("x", [P, NB, C], F32))
        k.xn = ctx.enter_context(nc.sbuf_tensor("xn", [P, NB, C], F32))
        k.xnT = ctx.enter_context(nc.sbuf_tensor("xnT", [P, KC, TOK], F32))
        k.ctxT = ctx.enter_context(nc.sbuf_tensor("ctxT", [P, TOK], F32))
        const = ctx.enter_context(nc.sbuf_tensor("const", [P, width["const"]], F32))
        k.c = sbuf_views(const, *parts["const"])
        k.ident = k.c["ident"]
        widest = max((width[i] if i else 0) + (2 * dram[s].shape[-1] if s else 0) for i, s in WEIGHTS)
        k.arena = [ctx.enter_context(nc.sbuf_tensor(f"arena{n}", [P, widest], F32)) for n in range(2)]
        k.now = Weights(k, FIRST)
        with Stage(k, "begin") as st:
            s_in = st.sem("inputs_loaded")
            with nc.Block() as block:

                @block.sync
                def _(sp):
                    sp.dma_start(k.x[:, :, :], dram["x"]).then_inc(s_in, 16)
                    sp.dma_start(k.ctxT[:, :], dram["ctxT"]).then_inc(s_in, 16)
                    sp.dma_start(const[:, :], dram["const"]).then_inc(s_in, 16)
                    k.now.load(sp)
                    sp.wait_ge(s_in, 48)
        for n, stage in enumerate(STAGES):
            if FIRST <= n <= LAST:
                after = k.after = Weights(k, n + 1) if n + 1 < len(STAGES) else None
                layernorm(k, n, after if n < LAST else None)
                stage(k)
                k.now = after
        with Stage(k, "end") as st:
            s_out = st.sem("output_stored")
            with nc.Block() as block:

                @block.sync
                def _(sp):
                    sp.dma_start(out, k.x[:, :, :]).then_inc(s_out, 16)
                    sp.wait_ge(s_out, 16)



def rows(a):
    a = np.asarray(a)
    return a.reshape(-1, P, a.shape[1]).transpose(1, 0, 2).reshape(P, -1)


def cols(v):
    return np.asarray(v).reshape(-1, P).T


def each(v):
    return np.broadcast_to(np.asarray(v).reshape(1, -1), (P, np.asarray(v).size))


def constants():
    i = np.arange(P)
    c = {"ident": np.eye(P), "ones": np.ones((P, P)), "zero": np.zeros((P, 1)), "triu": (i[:, None] <= i[None, :]) * 1.0,
         "causal": np.where(i[None, :] <= i[:, None], 0.0, -BIG),
         "causalT": np.where(i[:, None] <= i[None, :], 0.0, -BIG),
         "head_ones16": (i[:, None] // 16 == i[None, :] // 16) * 1.0,
         "in_head16": (i[:, None] // 16 == np.arange(8)[None, :]) * 1.0,
         "in_head8": (i[:, None] // 8 == np.arange(16)[None, :]) * 1.0,
         "iota": each(np.arange(8.0)), "iota_far": each(np.arange(8.0) + 100.0)}
    return {n: np.asarray(a, np.float32) for n, a in c.items()}


def images(i):
    im = {"const": constants()}
    im["L2a"] = {"w_qkv": rows(i["L2_attn_w_qkv"]), "w_out": rows(i["L2_attn_w_out"]),
                 "decay": cols(np.repeat(np.asarray(i["L2_attn_decay_param"]), 16))}
    im["L0a"] = {"wq": rows(i["L0_attn_Wq"].T), "wk": rows(i["L0_attn_Wk"].T), "wv": rows(i["L0_attn_Wv"].T),
                 "wp": rows(i["L0_attn_Wp"].T), "bq": cols(i["L0_attn_bq"]), "bk": cols(i["L0_attn_bk"]),
                 "bv": each(i["L0_attn_bv"]), "bp": each(i["L0_attn_bp"])}
    im["const"]["freq"] = np.tile(np.array([1.0, 10000.0 ** -0.5], np.float32), (P, 2))
    im["L0x"] = {"wq": rows(i["L0_xattn_Wq"]), "wkv": np.asarray(i["L0_xattn_Wkv"]),
                 "wout": rows(i["L0_xattn_Wout"]), "bout": each(i["L0_xattn_bout"]),
                 "pos": np.repeat(np.asarray(i["fside_BxSx2_0"]).transpose(1, 0, 2), 2, axis=2).reshape(P, -1)}
    im["L0f"] = {"gate_w": rows(i["L0_ffn_gate_w"].T), "val_w": rows(i["L0_ffn_val_w"].T),
                 "out_w": rows(i["L0_ffn_out_w"].T), "gate_b": each(i["L0_ffn_gate_b"]),
                 "val_b": each(i["L0_ffn_val_b"]), "out_b": each(i["L0_ffn_out_b"])}
    n, f = np.arange(16), np.arange(9)
    turn = 2 * np.pi * n[:, None] * f[None, :] / 16
    both = np.where((f == 0) | (f == 8), 1.0, 2.0 ** 0.5)
    wave = np.stack([np.cos(turn) * both, -np.sin(turn) * both], 1)
    fwd = np.zeros((16, 16, 2, 16, 9), np.float32)
    for h in range(16):
        fwd[h, :, :, h, :] = wave
    fwd = fwd.reshape(C, 288)
    im["L1a"] = {"wq": rows(i["L1_attn_W_q"]), "wkv": rows(i["L1_attn_W_kv"]),
                 "woT": rows(np.asarray(i["L1_attn_W_o"]).T), "fwd": rows(fwd),
                 "inv": rows(np.asarray(wave_inverse(), np.float32))}
    im["L1n"] = {"gq": cols(i["L1_xattn_gq"]), "gk": cols(i["L1_xattn_gk"])}
    im["L1g"] = {"w_gate": rows(i["L1_ffn_w_gate"])}
    main_rows = (np.arange(P) < P - 16)[:, None]
    im["const"]["key_parts"] = np.concatenate([main_rows, ~main_rows], 1).astype(np.float32)
    heads = np.arange(512).reshape(16, 2, 16)
    kcols, vcols = heads[:, 0].ravel(), heads[:, 1].ravel()
    wkv = np.concatenate([np.asarray(i["L2_xattn_Wk"]), np.asarray(i["L2_xattn_Wv"])], 1)
    bkv = np.concatenate([np.asarray(i["L2_xattn_bk"]), np.asarray(i["L2_xattn_bv"])])
    wd, bd = np.asarray(i["L2_xattn_Wkv_dca"]), np.asarray(i["L2_xattn_bkv_dca"])
    zero = np.zeros((), np.float32)
    im["L2x"] = {"wq": rows(i["L2_xattn_Wq"]), "wo": rows(i["L2_xattn_Wo"]),
                 "wk": wkv[:, kcols], "wv": wkv[:, vcols], "wkd": wd[:, :C], "wvd": wd[:, C:],
                 "bqk": np.concatenate([each(i["L2_xattn_bq"]), np.where(main_rows, bkv[kcols], bd[:C])], 1),
                 "bvs": np.concatenate([np.where(main_rows, bkv[vcols], zero), np.where(main_rows, zero, bd[C:])], 1),
                 "nw": np.stack([np.tile(np.asarray(i[f"L2_xattn_{n}_w"]), 8) for n in ("qn", "kn", "kn_dca")], 1),
                 "nb": np.stack([np.tile(np.asarray(i[f"L2_xattn_{n}_b"]), 8) for n in ("qn", "kn", "kn_dca")], 1),
                 "bo": each(i["L2_xattn_bo"])}
    ar, br = np.asarray(i["L2_ffn_A_r"]), np.asarray(i["L2_ffn_B_r"])
    down = np.concatenate([np.asarray(i["L2_ffn_A_s"]), ar.transpose(1, 0, 2).reshape(C, -1)], 1)
    up = np.concatenate([np.asarray(i["L2_ffn_B_s"]), br.reshape(-1, C), np.zeros((16, C), np.float32)])
    im["L2f"] = {"base": rows(i["L2_ffn_W_base"]), "down": rows(down), "up": up,
                 "router": rows(i["L2_ffn_W_router"]), "b": each(i["L2_ffn_b_base"]),
                 "b_router": each(i["L2_ffn_b_router"])}
    n = np.arange(P)
    im["const"]["below"] = (n[:, None] > n[None, :]).astype(np.float32)
    w_in, cw = np.asarray(i["L3_attn_W_in"]), np.asarray(i["L3_attn_conv_w"])
    cwb = np.concatenate([cw, np.asarray(i["L3_attn_conv_b"])[:, None]], 1)
    im["L3a"] = {"wb": rows(w_in[:, 8192:8320]), "wc": rows(w_in[:, 8320:8448]), "wdt": rows(w_in[:, 8448:]),
                 "dt_bias": each(i["L3_attn_dt_bias"]), "A": each(i["L3_attn_A"]),
                 "conv_bc": np.concatenate([cwb[4096:4224], cwb[4224:4352]], 1)}
    experts = [f"e{e}" for e in range(8)] + ["shared"]
    p3 = {n: [np.asarray(i[f"L3_ffn_{e}_{n}"]) for e in experts] for n in ("w1", "b1", "w2", "b2")}
    w1 = np.concatenate(p3["w1"], 1)
    im["const"]["cost"] = each(np.float32(1e-7) * np.array([2 * 128 * h for h in (128, 256, 384, 512) * 2], np.float32))
    im["L3f"] = {"down": rows(i["L3_ffn_down_w"]), "router": rows(i["L3_ffn_router_w"]),
                 "core": rows(i["L3_ffn_core_w"]), "up": np.asarray(i["L3_ffn_up_w"]), "w1": w1,
                 "w2": rows(np.concatenate(p3["w2"])), "b1": cols(np.concatenate(p3["b1"])),
                 "b2": each(np.concatenate(p3["b2"])), "down_b": cols(i["L3_ffn_down_b"]),
                 "up_b": each(i["L3_ffn_up_b"]), "core_b": each(i["L3_ffn_core_b"]),
                 "b_router": each(i["L3_ffn_router_b"])}
    return im


def kernel(**inputs):
    import concourse.bacc as bacc
    from concourse.bass_utils import run_bass_kernel_spmd

    im = images(inputs)
    arrays = {n: np.concatenate(list(parts.values()), axis=-1) for n, parts in im.items()}
    arrays["x"] = np.asarray(inputs["x"]).transpose(1, 0, 2)
    arrays["ctxT"] = np.asarray(inputs["ctx_1024"]).reshape(TOK, P).T
    arrays["L1x"] = np.stack([np.concatenate(
        [rows(np.asarray(inputs["L1_xattn_Wq"])[:, h * P:(h + 1) * P]),
         np.asarray(inputs["L1_xattn_Wk"])[:, h * P:(h + 1) * P], np.asarray(inputs["L1_xattn_Wv"])[:, h * P:(h + 1) * P],
         np.asarray(inputs["L1_xattn_Wo"])[h * P:(h + 1) * P]], 1) for h in range(16)])
    arrays["L1f"] = np.stack([np.concatenate([rows(inputs[f"L1_ffn_{n}"][e]) for n in ("w1", "w3", "w2")], 1)
                              for e in range(8)])
    w_in, w_out = np.asarray(inputs["L3_attn_W_in"]), np.asarray(inputs["L3_attn_W_out"])
    small = np.concatenate([np.asarray(inputs["L3_attn_conv_w"])[:4096], np.asarray(inputs["L3_attn_conv_b"])[:4096, None],
                            np.repeat(np.asarray(inputs["L3_attn_D"]), 64)[:, None],
                            np.asarray(inputs["L3_attn_norm_w"])[:, None], np.zeros((4096, 1), np.float32)], 1)
    arrays["L3p"] = np.stack([np.concatenate([rows(w_in[:, c * P:(c + 1) * P]),
                                              rows(w_in[:, 4096 + c * P:4096 + (c + 1) * P]),
                                              w_out[c * P:(c + 1) * P], small[c * P:(c + 1) * P]], 1)
                              for c in range(32)])
    arrays["L3x"] = np.stack([np.concatenate(
        [rows(np.asarray(inputs["L3_xattn_Wq"])[:, h * C:(h + 1) * C]),
         np.asarray(inputs["L3_xattn_Wk"])[:, h * P:(h + 1) * P], np.asarray(inputs["L3_xattn_Wv"])[:, h * P:(h + 1) * P],
         rows(np.asarray(inputs["L3_xattn_Wo"])[h * C:(h + 1) * C])], 1) for h in range(8)])
    mask = np.asarray(inputs["mask_BxS2_bf1"]).view(np.uint8)
    arrays["mask"] = np.broadcast_to(mask.reshape(1, TOK), (P, TOK))
    arrays["maskT"] = mask.T
    arrays = {n: np.ascontiguousarray(a) for n, a in arrays.items()}
    parts = {n: (list(p), {m: a.shape[-1] for m, a in p.items()}) for n, p in im.items()}
    width = {n: arrays[n].shape[-1] for n in im}
    nc = bacc.Bacc("TRN2", target_bir_lowering=False, num_devices=1)
    dram = {n: nc.dram_tensor(f"in_{n}", a.shape, mybir.dt.from_np(a.dtype), kind="ExternalInput").ap()
            for n, a in arrays.items()}
    out = nc.dram_tensor("out_x", (P, NB, C), F32, kind="ExternalOutput").ap()
    program(nc, dram, parts, width, out)
    r = run_bass_kernel_spmd(nc, [{f"in_{n}": a for n, a in arrays.items()}], core_ids=[0])
    return np.ascontiguousarray(r.results[0]["out_x"].reshape(P, NB, C).transpose(1, 0, 2))


def wave_inverse():
    n, f = np.arange(16), np.arange(9)
    turn = 2 * np.pi * n[:, None] * f[None, :] / 16
    part = np.stack([np.cos(turn), -np.sin(turn)], 1) / 16
    inv = np.zeros((16, 16, 2, 16, 9))
    for h in range(16):
        inv[h, :, :, h, :] = part
    return inv.reshape(C, 288)
```
